# Optimizing a Trainium2 kernel written in Bass

```python
import numpy as np
import jax
import jax.numpy as jnp

def _softmax(x, axis=-1):
    return jax.nn.softmax(x, axis=axis)

def _gelu(x):
    return jax.nn.gelu(x, approximate=True)

def _silu(x):
    return jax.nn.silu(x)

def _sigmoid(x):
    return jax.nn.sigmoid(x)

def _layernorm(x, axis=-1, eps=1e-05):
    m = jnp.mean(x, axis=axis, keepdims=True)
    v = jnp.var(x, axis=axis, keepdims=True)
    return (x - m) / jnp.sqrt(v + eps)

def _scatter_add(tgt, idx, src, axis=0):
    return tgt.at[idx].add(src)

def _segment_sum(src, seg, n):
    return jax.ops.segment_sum(src, seg, n)
kernel_name = 'mk_early_fusion_embed_d2_tok_img1024_r4_a07539'

def setup_inputs(seed: int=0):
    np.random.seed(seed)
    _w = jnp.asarray

    def _rec_inputs():
        import jax
        import jax.numpy as jnp
        _rk = jax.random.key(seed)
        x = jax.random.uniform(jax.random.fold_in(_rk, 1), (8, 3, 256, 256), jnp.float32, 0.0, 1)
        x_txt = jax.random.randint(jax.random.fold_in(_rk, 51), (8, 128), 0, 12564, jnp.int32)
        return (x, x_txt)
    x, x_txt = _rec_inputs()

    def _L0_tok_setup():
        import jax, jax.numpy as jnp
        import numpy as np
        _GRAY_W = (0.2989, 0.587, 0.114)
        key = jax.random.key(seed)
        x = jax.random.uniform(key, (32, 3, 256, 256), dtype=jnp.float32)
        sx = jnp.array([[-3.0, 0.0, 3.0], [-10.0, 0.0, 10.0], [-3.0, 0.0, 3.0]], dtype=jnp.float32)
        scharr = jnp.stack([sx, sx.T])[:, None, :, :]
        return {'x': x, 'scharr': scharr}
    _L0_tok_all = _L0_tok_setup()
    _L0_tok_in = {k: v for k, v in _L0_tok_all.items() if k in ('scharr',)}
    del _L0_tok_all

    def _L0_txt_setup():
        import jax, jax.numpy as jnp
        import numpy as np
        BIGRAM_VOCAB = 262144
        BIGRAM_DIM = 64
        MODEL_DIM = 256
        BATCH, SEQ = (4, 2048)

        def bigram_hash(tokens, vocab_size):
            t = tokens.astype(jnp.int32)
            mod = np.int32(vocab_size - 1)
            a = jnp.int32(36313) * t[..., 1:] ^ jnp.int32(27191) * t[..., :-1]
            h = a % mod
            first = jnp.full(t.shape[:-1] + (1,), mod, dtype=jnp.int32)
            return jnp.concatenate([first, h], axis=-1)
        key = jax.random.key(seed)
        k1, k2, k3 = jax.random.split(key, 3)
        token_ids = jax.random.randint(k1, (BATCH, SEQ), 0, 50257, dtype=jnp.int64)
        embed_weight = jax.random.normal(k2, (BIGRAM_VOCAB, BIGRAM_DIM), dtype=jnp.float32) * 0.02
        proj_weight = jax.random.normal(k3, (MODEL_DIM, BIGRAM_DIM), dtype=jnp.float32) * 0.02
        scale = jnp.float32(0.05)
        return {'token_ids': token_ids, 'embed_weight': embed_weight, 'proj_weight': proj_weight, 'scale': scale}
    _L0_txt_all = _L0_txt_setup()
    _L0_txt_in = {k: v for k, v in _L0_txt_all.items() if k in ('embed_weight', 'proj_weight', 'scale')}
    del _L0_txt_all

    def _L0_attn_setup():
        import jax, jax.numpy as jnp
        import numpy as np
        import math
        D_MODEL = 256
        NUM_HEADS = 16
        HEAD_DIM = D_MODEL // NUM_HEADS
        LN_EPS = 1e-05

        def _layer_norm(x, g, b):
            mu = jnp.mean(x, axis=-1, keepdims=True)
            var = jnp.mean(jnp.square(x - mu), axis=-1, keepdims=True)
            return (x - mu) * jax.lax.rsqrt(var + LN_EPS) * g + b

        def _rope_tables(seq_len, dim, dtype):
            inv_freq = 1.0 / 10000.0 ** (jnp.arange(0, dim, 2, dtype=jnp.float32) / dim)
            t = jnp.arange(seq_len, dtype=jnp.float32)
            freqs = t[:, None] * inv_freq[None, :]
            emb = jnp.concatenate([freqs, freqs], axis=-1)
            return (jnp.cos(emb).astype(dtype), jnp.sin(emb).astype(dtype))

        def _rotate_half(x):
            x1, x2 = jnp.split(x, 2, axis=-1)
            return jnp.concatenate([-x2, x1], axis=-1)
        key = jax.random.key(seed)
        ks = jax.random.split(key, 8)
        B, S, D = (2, 512, D_MODEL)
        s_in = 1.0 / math.sqrt(D)
        return {'x': jax.random.normal(ks[0], (B, S, D), jnp.float32), 'ln1_g': jnp.ones((D,), jnp.float32), 'ln1_b': jnp.zeros((D,), jnp.float32), 'Wqkv': jax.random.normal(ks[1], (D, 3 * D), jnp.float32) * s_in, 'bqkv': jnp.zeros((3 * D,), jnp.float32), 'Wo': jax.random.normal(ks[2], (D, D), jnp.float32) * s_in, 'bo': jnp.zeros((D,), jnp.float32), 'ln2_g': jnp.ones((D,), jnp.float32), 'ln2_b': jnp.zeros((D,), jnp.float32), 'W1': jax.random.normal(ks[3], (D, 4 * D), jnp.float32) * s_in, 'b1': jnp.zeros((4 * D,), jnp.float32), 'W2': jax.random.normal(ks[4], (4 * D, D), jnp.float32) / math.sqrt(4 * D), 'b2': jnp.zeros((D,), jnp.float32)}
    _L0_attn_all = _L0_attn_setup()
    _L0_attn_in = {k: v for k, v in _L0_attn_all.items() if k in ('ln1_g', 'ln1_b', 'Wqkv', 'bqkv', 'Wo', 'bo', 'ln2_g', 'ln2_b', 'W1', 'b1', 'W2', 'b2')}
    del _L0_attn_all

    def _L0_ffn_setup():
        import jax, jax.numpy as jnp
        import numpy as np
        EPS = 1e-05

        def _quantize(W):
            gamma = jnp.mean(jnp.abs(W))
            return jnp.clip(jnp.round(W / (gamma + EPS)), -1.0, 1.0)
        key = jax.random.key(seed)
        k_x, k_w1, k_b1, k_w2, k_b2 = jax.random.split(key, 5)
        n_embd = 256
        d_ff = 4 * n_embd
        B, S = (4, 1024)
        bound1 = 1.0 / np.sqrt(n_embd)
        bound2 = 1.0 / np.sqrt(d_ff)
        x = jax.random.normal(k_x, (B, S, n_embd), dtype=jnp.float32)
        W1 = jax.random.uniform(k_w1, (d_ff, n_embd), jnp.float32, -bound1, bound1)
        b1 = jax.random.uniform(k_b1, (d_ff,), jnp.float32, -bound1, bound1)
        W2 = jax.random.uniform(k_w2, (n_embd, d_ff), jnp.float32, -bound2, bound2)
        b2 = jax.random.uniform(k_b2, (n_embd,), jnp.float32, -bound2, bound2)
        return {'x': x, 'W1': W1, 'b1': b1, 'W2': W2, 'b2': b2}
    _L0_ffn_all = _L0_ffn_setup()
    _L0_ffn_in = {k: v for k, v in _L0_ffn_all.items() if k in ('W1', 'b1', 'W2', 'b2')}
    del _L0_ffn_all

    def _L1_attn_setup():
        import jax, jax.numpy as jnp
        import numpy as np
        B, T = (2, 512)
        TOK, POS = (128, 128)
        H, D, KVH = (16, 64, 4)
        key = jax.random.key(seed)
        ks = jax.random.split(key, 7)

        def w(k, shape, fan_in):
            return jax.random.normal(k, shape, jnp.float32) / np.float32(np.sqrt(fan_in))
        x = jax.random.normal(ks[0], (B, T, TOK + POS), jnp.float32)
        Wq = w(ks[1], (POS, H * D), POS)
        Wk = w(ks[2], (POS, KVH * D), POS)
        Wv = w(ks[3], (TOK, KVH * D), TOK)
        Wo = w(ks[4], (H * D, TOK + POS), H * D)
        q_phase_angle = 0.1 * jax.random.normal(ks[5], (H,), jnp.float32)
        alibi_log_slopes = jnp.full((H,), np.float32(np.log(np.log(10.0))))
        return dict(x=x, Wq=Wq, Wk=Wk, Wv=Wv, Wo=Wo, q_phase_angle=q_phase_angle, alibi_log_slopes=alibi_log_slopes)
    _L1_attn_all = _L1_attn_setup()
    _L1_attn_in = {k: v for k, v in _L1_attn_all.items() if k in ('Wq', 'Wk', 'Wv', 'Wo', 'q_phase_angle', 'alibi_log_slopes')}
    del _L1_attn_all

    def _L1_ffn_setup():
        import jax, jax.numpy as jnp
        import numpy as np
        NUM_EXPERTS = 8
        TOP_K = 2
        CAPACITY_FACTOR = 1.25
        key = jax.random.key(seed)
        k1, k2, k3, k4, k5 = jax.random.split(key, 5)
        B, S, H, I, E = (4, 512, 256, 1024, NUM_EXPERTS)
        return {'hidden_states': jax.random.normal(k1, (B, S, H), dtype=jnp.float32), 'router_gate': jax.random.normal(k2, (H, E), dtype=jnp.float32) * 0.02, 'gate_w': jax.random.normal(k3, (E, H, I), dtype=jnp.float32) * 0.02, 'up_w': jax.random.normal(k4, (E, H, I), dtype=jnp.float32) * 0.02, 'down_w': jax.random.normal(k5, (E, I, H), dtype=jnp.float32) * 0.02}
    _L1_ffn_all = _L1_ffn_setup()
    _L1_ffn_in = {k: v for k, v in _L1_ffn_all.items() if k in ('router_gate', 'gate_w', 'up_w', 'down_w')}
    del _L1_ffn_all
    return {'x': x, 'x_txt': x_txt, 'L0_tok_scharr': _L0_tok_in['scharr'], 'L0_txt_embed_weight': _L0_txt_in['embed_weight'], 'L0_txt_proj_weight': _L0_txt_in['proj_weight'], 'L0_txt_scale': _L0_txt_in['scale'], 'L0_attn_ln1_g': _L0_attn_in['ln1_g'], 'L0_attn_ln1_b': _L0_attn_in['ln1_b'], 'L0_attn_Wqkv': _L0_attn_in['Wqkv'], 'L0_attn_bqkv': _L0_attn_in['bqkv'], 'L0_attn_Wo': _L0_attn_in['Wo'], 'L0_attn_bo': _L0_attn_in['bo'], 'L0_attn_ln2_g': _L0_attn_in['ln2_g'], 'L0_attn_ln2_b': _L0_attn_in['ln2_b'], 'L0_attn_W1': _L0_attn_in['W1'], 'L0_attn_b1': _L0_attn_in['b1'], 'L0_attn_W2': _L0_attn_in['W2'], 'L0_attn_b2': _L0_attn_in['b2'], 'L0_ffn_W1': _L0_ffn_in['W1'], 'L0_ffn_b1': _L0_ffn_in['b1'], 'L0_ffn_W2': _L0_ffn_in['W2'], 'L0_ffn_b2': _L0_ffn_in['b2'], 'L1_attn_Wq': _L1_attn_in['Wq'], 'L1_attn_Wk': _L1_attn_in['Wk'], 'L1_attn_Wv': _L1_attn_in['Wv'], 'L1_attn_Wo': _L1_attn_in['Wo'], 'L1_attn_q_phase_angle': _L1_attn_in['q_phase_angle'], 'L1_attn_alibi_log_slopes': _L1_attn_in['alibi_log_slopes'], 'L1_ffn_router_gate': _L1_ffn_in['router_gate'], 'L1_ffn_gate_w': _L1_ffn_in['gate_w'], 'L1_ffn_up_w': _L1_ffn_in['up_w'], 'L1_ffn_down_w': _L1_ffn_in['down_w']}

def reference(x, x_txt, L0_tok_scharr, L0_txt_embed_weight, L0_txt_proj_weight, L0_txt_scale, L0_attn_ln1_g, L0_attn_ln1_b, L0_attn_Wqkv, L0_attn_bqkv, L0_attn_Wo, L0_attn_bo, L0_attn_ln2_g, L0_attn_ln2_b, L0_attn_W1, L0_attn_b1, L0_attn_W2, L0_attn_b2, L0_ffn_W1, L0_ffn_b1, L0_ffn_W2, L0_ffn_b2, L1_attn_Wq, L1_attn_Wk, L1_attn_Wv, L1_attn_Wo, L1_attn_q_phase_angle, L1_attn_alibi_log_slopes, L1_ffn_router_gate, L1_ffn_gate_w, L1_ffn_up_w, L1_ffn_down_w):
    import jax
    import jax.numpy as jnp

    def _L0_tok_ref(x, scharr):
        import jax, jax.numpy as jnp
        import numpy as np
        _GRAY_W = (0.2989, 0.587, 0.114)
        w = jnp.asarray(_GRAY_W, dtype=x.dtype)
        gray = jnp.einsum('bchw,c->bhw', x, w)[:, None]
        edges = jax.lax.conv_general_dilated(gray, scharr, window_strides=(1, 1), padding='SAME', dimension_numbers=('NCHW', 'OIHW', 'NCHW'))
        abs_edges = jnp.sqrt(jnp.square(edges))
        edge = abs_edges.sum(axis=1) / 2
        return edge

    def _L0_txt_ref(token_ids, embed_weight, proj_weight, scale):
        import jax, jax.numpy as jnp
        import numpy as np
        BIGRAM_VOCAB = 262144
        BIGRAM_DIM = 64
        MODEL_DIM = 256
        BATCH, SEQ = (4, 2048)

        def bigram_hash(tokens, vocab_size):
            t = tokens.astype(jnp.int32)
            mod = np.int32(vocab_size - 1)
            a = jnp.int32(36313) * t[..., 1:] ^ jnp.int32(27191) * t[..., :-1]
            h = a % mod
            first = jnp.full(t.shape[:-1] + (1,), mod, dtype=jnp.int32)
            return jnp.concatenate([first, h], axis=-1)
        idx = bigram_hash(token_ids, BIGRAM_VOCAB)
        h = embed_weight[idx]
        h = jnp.einsum('bsd,md->bsm', h, proj_weight)
        return h * scale.astype(h.dtype)

    def _L0_attn_ref(x, ln1_g, ln1_b, Wqkv, bqkv, Wo, bo, ln2_g, ln2_b, W1, b1, W2, b2):
        import jax, jax.numpy as jnp
        import numpy as np
        import math
        D_MODEL = 256
        NUM_HEADS = 16
        HEAD_DIM = D_MODEL // NUM_HEADS
        LN_EPS = 1e-05

        def _layer_norm(x, g, b):
            mu = jnp.mean(x, axis=-1, keepdims=True)
            var = jnp.mean(jnp.square(x - mu), axis=-1, keepdims=True)
            return (x - mu) * jax.lax.rsqrt(var + LN_EPS) * g + b

        def _rope_tables(seq_len, dim, dtype):
            inv_freq = 1.0 / 10000.0 ** (jnp.arange(0, dim, 2, dtype=jnp.float32) / dim)
            t = jnp.arange(seq_len, dtype=jnp.float32)
            freqs = t[:, None] * inv_freq[None, :]
            emb = jnp.concatenate([freqs, freqs], axis=-1)
            return (jnp.cos(emb).astype(dtype), jnp.sin(emb).astype(dtype))

        def _rotate_half(x):
            x1, x2 = jnp.split(x, 2, axis=-1)
            return jnp.concatenate([-x2, x1], axis=-1)
        B, S, D = x.shape
        H, hd = (NUM_HEADS, HEAD_DIM)
        normed = _layer_norm(x, ln1_g, ln1_b)
        qkv = (normed @ Wqkv + bqkv).reshape(B, S, 3, H, hd)
        qkv = jnp.transpose(qkv, (2, 0, 3, 1, 4))
        q, k, v = (qkv[0], qkv[1], qkv[2])
        cos, sin = _rope_tables(S, hd, q.dtype)
        cos = cos[None, None, :, :]
        sin = sin[None, None, :, :]
        q = q * cos + _rotate_half(q) * sin
        k = k * cos + _rotate_half(k) * sin
        scores = jnp.einsum('bhqd,bhkd->bhqk', q, k) / math.sqrt(hd)
        causal = jnp.triu(jnp.ones((S, S), dtype=bool), k=1)
        scores = jnp.where(causal[None, None], -jnp.inf, scores)
        attn = jax.nn.softmax(scores, axis=-1)
        attn_out = jnp.einsum('bhqk,bhkd->bhqd', attn, v)
        attn_out = jnp.transpose(attn_out, (0, 2, 1, 3)).reshape(B, S, D)
        attn_out = attn_out @ Wo + bo
        x = x + attn_out
        h = _layer_norm(x, ln2_g, ln2_b)
        h = jax.nn.gelu(h @ W1 + b1, approximate=False) @ W2 + b2
        return x + h

    def _L0_ffn_ref(x, W1, b1, W2, b2):
        import jax, jax.numpy as jnp
        import numpy as np
        EPS = 1e-05

        def _quantize(W):
            gamma = jnp.mean(jnp.abs(W))
            return jnp.clip(jnp.round(W / (gamma + EPS)), -1.0, 1.0)
        Wq1 = _quantize(W1)
        Wq2 = _quantize(W2)
        h = jax.nn.relu(jnp.einsum('bsd,fd->bsf', x, Wq1) + b1)
        out = jnp.einsum('bsf,df->bsd', h, Wq2) + b2
        return out

    def _L1_attn_ref(x, Wq, Wk, Wv, Wo, q_phase_angle, alibi_log_slopes):
        import jax, jax.numpy as jnp
        import numpy as np
        B, T = (2, 512)
        TOK, POS = (128, 128)
        H, D, KVH = (16, 64, 4)
        b, t, _ = x.shape
        x_tok = x[:, :, :TOK]
        x_pos = x[:, :, TOK:]
        q = (x_pos @ Wq).reshape(b, t, H, D).transpose(0, 2, 1, 3)
        k = (x_pos @ Wk).reshape(b, t, KVH, D).transpose(0, 2, 1, 3)
        v = (x_tok @ Wv).reshape(b, t, KVH, D).transpose(0, 2, 1, 3)
        c = jnp.cos(q_phase_angle)[None, :, None, None]
        s = jnp.sin(q_phase_angle)[None, :, None, None]
        q2 = q.reshape(b, H, t, D // 2, 2)
        q0, q1 = (q2[..., 0], q2[..., 1])
        q = jnp.stack([q0 * c - q1 * s, q0 * s + q1 * c], axis=-1).reshape(b, H, t, D)
        rep = H // KVH
        k = jnp.repeat(k, rep, axis=1)
        v = jnp.repeat(v, rep, axis=1)
        att = jnp.einsum('bhqd,bhkd->bhqk', q, k) / np.float32(np.sqrt(D))
        pos = jnp.arange(t)
        rel = (pos[:, None] - pos[None, :]).astype(jnp.float32)
        att = att + jnp.exp(alibi_log_slopes)[None, :, None, None] * rel[None, None]
        mask = pos[:, None] >= pos[None, :]
        att = jnp.where(mask[None, None], att, -jnp.inf)
        m = jnp.max(att, axis=-1, keepdims=True)
        e = jnp.exp(att - m)
        att = e / (1.0 + jnp.sum(e, axis=-1, keepdims=True))
        out = jnp.einsum('bhqk,bhkd->bhqd', att, v)
        out = out.transpose(0, 2, 1, 3).reshape(b, t, H * D)
        return out @ Wo

    def _L1_ffn_ref(hidden_states, router_gate, gate_w, up_w, down_w):
        import jax, jax.numpy as jnp
        import numpy as np
        NUM_EXPERTS = 8
        TOP_K = 2
        CAPACITY_FACTOR = 1.25
        B, S, H = hidden_states.shape
        E = router_gate.shape[1]
        K = TOP_K
        x = hidden_states.reshape(-1, H)
        T = x.shape[0]
        cap = int(CAPACITY_FACTOR * ((T * K + E - 1) // E))
        probs = jax.nn.softmax(x @ router_gate, axis=-1)
        topw, topi = jax.lax.top_k(probs, K)
        topw = topw / (topw.sum(-1, keepdims=True) + 1e-09)
        gates = jnp.zeros((T, E), x.dtype).at[jnp.arange(T)[:, None], topi].set(topw)
        top_g, tok_idx = jax.lax.top_k(gates.T, cap)
        xe = x[tok_idx]
        h = jax.nn.silu(jnp.einsum('ech,ehi->eci', xe, gate_w)) * jnp.einsum('ech,ehi->eci', xe, up_w)
        ye = jnp.einsum('eci,eih->ech', h, down_w) * top_g[..., None]
        out = jnp.zeros_like(x).at[tok_idx.reshape(-1)].add(ye.reshape(-1, H))
        return out.reshape(B, S, H)
    h = _L0_tok_ref(x, L0_tok_scharr)
    h = jnp.concatenate([h, _L0_txt_ref(x_txt, L0_txt_embed_weight, L0_txt_proj_weight, L0_txt_scale)], axis=1)
    h = h + _L0_attn_ref(_layernorm(h, axis=-1), L0_attn_ln1_g, L0_attn_ln1_b, L0_attn_Wqkv, L0_attn_bqkv, L0_attn_Wo, L0_attn_bo, L0_attn_ln2_g, L0_attn_ln2_b, L0_attn_W1, L0_attn_b1, L0_attn_W2, L0_attn_b2)
    h = h + _L0_ffn_ref(_layernorm(h, axis=-1), L0_ffn_W1, L0_ffn_b1, L0_ffn_W2, L0_ffn_b2)
    h = h + _L1_attn_ref(_layernorm(h, axis=-1), L1_attn_Wq, L1_attn_Wk, L1_attn_Wv, L1_attn_Wo, L1_attn_q_phase_angle, L1_attn_alibi_log_slopes)
    h = h + _L1_ffn_ref(_layernorm(h, axis=-1), L1_ffn_router_gate, L1_ffn_gate_w, L1_ffn_up_w, L1_ffn_down_w)
    return h

_drawn_inputs = setup_inputs


def setup_inputs(seed=0):
    import zlib

    import numpy as np

    out = dict(_drawn_inputs(seed))
    spreads = {'L0_attn_ln1_g': (1.0, 0.2),
     'L0_attn_ln1_b': (0.0, 0.1),
     'L0_attn_bqkv': (0.0, 0.1),
     'L0_attn_bo': (0.0, 0.1),
     'L0_attn_ln2_g': (1.0, 0.2),
     'L0_attn_ln2_b': (0.0, 0.1),
     'L0_attn_b1': (0.0, 0.1),
     'L0_attn_b2': (0.0, 0.1),
     'L1_attn_alibi_log_slopes': (0.834032416343689, 0.6)}
    factors = {'L0_ffn_b1': 8.0,
     'L0_ffn_b2': 8.0,
     'L1_attn_Wq': 8.0,
     'L1_attn_Wk': 8.0,
     'L1_attn_Wv': 8.0,
     'L1_attn_Wo': 8.0,
     'L1_attn_q_phase_angle': 8.0,
     'L1_ffn_router_gate': 8.0,
     'L1_ffn_gate_w': 8.0,
     'L1_ffn_up_w': 8.0,
     'L1_ffn_down_w': 8.0}
    for name, (base, spread) in spreads.items():
        noise = np.random.default_rng([zlib.crc32(name.encode()), seed]).standard_normal(out[name].shape)
        drawn = base * np.exp(spread * noise) if base else spread * noise
        out[name] = jnp.asarray(drawn.astype(out[name].dtype))
    for name, factor in factors.items():
        out[name] = (out[name] * factor).astype(out[name].dtype)
    return out
```

```python
import math
from contextlib import ExitStack

import numpy as np

import concourse.bass as bass
from concourse import mybir

F32 = mybir.dt.float32
F32R = mybir.dt.float32r
I32 = mybir.dt.int32
ALU = mybir.AluOpType
ACT = mybir.ActivationFunctionType
AX = mybir.AxisListType

P = 128
B = 8
IMG = 256
TXT = 128
D = 256
DC = D // P
S = IMG + TXT
NT = S // P
T = B * S
TILES = T // P
VOCAB_MOD = 262143
HASH_CUR, HASH_PREV = 36313, 27191
EMB = 64
EPS = 1e-5
H0, HD0 = 16, 16
H1, HD1, KV1 = 16, 64, 4
FF = 4 * D
FM = FF // P
E = 8
CAP = 960
CP = 120
CT = CAP // CP
HALF = CAP // 2
NEG = -3.0e38
GRAY = (0.2989, 0.587, 0.114)
HEADS = 16
SEG = [0, P, 3 * P]
TWO_PI_HI, TWO_PI_LO = 6.28125, 2 * math.pi - 6.28125
ROUND = 12582912.0

COLS = {}
NC_COLS = 0
for _name, _n in (("ident", P), ("rel", S), ("mask", S), ("cos", NT * 2 * HD0), ("sin", NT * 2 * HD0),
                  ("shift", 3 * P), ("before", P), ("ones", P), ("tiebreak", E * TILES),
                  ("expert_row", E * TILES), ("scan_keep", E * TILES)):
    COLS[_name] = (NC_COLS, NC_COLS + _n)
    NC_COLS += _n


def shape_constants():
    c = np.zeros((P, NC_COLS), np.float32)

    def put(name, value):
        a, b = COLS[name]
        c[:, a:b] = np.asarray(value, np.float32).reshape(P, b - a)

    p = np.arange(P)
    put("ident", np.eye(P))
    rel = (S - P) + p[:, None] - np.arange(S)[None, :]
    put("rel", rel)
    put("mask", np.where(rel < 0, NEG, 0.0))
    inv_freq = (1.0 / np.float32(10000.0) ** (np.arange(0, HD0, 2, dtype=np.float32) / np.float32(HD0))).astype(np.float32)
    pos = (p[:, None] + P * np.arange(NT)[None, :]).astype(np.float32)
    freqs = pos[..., None] * inv_freq
    cos, sin = np.cos(freqs).astype(np.float32), np.sin(freqs).astype(np.float32)
    cos2 = np.concatenate([cos, cos], -1)
    sin2 = np.concatenate([-sin, sin], -1)
    scale = np.float32(HD0 ** -0.5)
    put("cos", np.stack([cos2 * scale, cos2], 2))
    put("sin", np.stack([sin2 * scale, sin2], 2))
    put("shift", np.stack([np.eye(P, k=1 - dy) for dy in range(3)], 1))
    put("before", np.triu(np.ones((P, P)), 1))
    put("ones", np.ones((P, P)))
    e = np.repeat(np.arange(E), TILES)
    put("tiebreak", np.broadcast_to(E - e, (P, E * TILES)))
    put("expert_row", np.broadcast_to(e * CAP, (P, E * TILES)))
    put("scan_keep", np.broadcast_to(np.tile(np.arange(TILES) > 0, E), (P, E * TILES)))
    return c


def psum_plan():
    setup = [("txt_index", 0, 1), ("projT", 1, 1)]
    setup += [(f"embT{b}", 2 + b % 2, 1) for b in range(B)]
    setup += [(f"txt{b}", 4 + b % 2, 1) for b in range(B)]
    setup += [("gamma", 6, 1)]
    setup += [(f"f1T{g}", (7, 0, 1, 2)[g], 1) for g in range(4)]
    setup += [(f"f2T{g}", (3, 4, 5, 6)[g], 1) for g in range(4)]

    body = [("conv0", 0, 1), ("conv1", 1, 1)]
    body += [(f"ln_attn0_T{c}", 6 + c, 1) for c in range(DC)]
    for t in range(NT):
        body += [(f"qk0_{t}", 2 * t, 1), (f"v0_{t}", 2 * t + 1, 1)]
    for t in range(NT):
        body += [(f"stack{t}_{g}", (6 + 4 * t + g) % 8, 1) for g in range(4)]
    for layer in range(2):
        if layer == 1:
            body += [(f"ln_attn1_T{c}", 6 + c, 1) for c in range(DC)]
            body += [(f"k1_{m}", m, 1) for m in range(2)]
            body += [(f"v1_{t}", 2 + t, 1) for t in range(NT)]
            body += [(f"q1_{m}", (5 + m) % 8, 1) for m in range(8)]
        for n in range(HEADS):
            body += [(f"scores{layer}_{n}", 2 * (n % 2), 1), (f"scores_b{layer}_{n}", 2 * (n % 2) + 1, 1)]
            body += [(f"probsT{layer}_{n}", 4, 1), (f"probsT_b{layer}_{n}", 5, 1)]
        body += [(f"out{layer}_{c}", 6 + c % 2, 1) for c in range(2 if layer == 0 else 8)]
        if layer == 0:
            body += [("proj0_a", 0, 1), ("proj0_b", 1, 1)]
            body += [(f"ln_mlp_T{c}", 6 + c, 1) for c in range(DC)]
            body += [(f"up0_{m}", m % 6, 1) for m in range(FM)]
            body += [("down0_a", 6, 1), ("down0_b", 7, 1)]
            body += [(f"ln_ffn_T{c}", c, 1) for c in range(DC)]
            body += [(f"up1_{m}", 2 + m % 4, 1) for m in range(FM)]
            body += [("down1_a", 6, 1), ("down1_b", 7, 1)]
    body += [("proj1_a", 0, 1), ("proj1_b", 1, 1)]
    body += [(f"ln_moe_T{c}", 2 + c, 1) for c in range(DC)]
    body += [("logits", 4, 1)]

    route = [("prefix", 0, 1), ("slots", 1, 1)]

    expert = [(f"xT{c}_{h}", 2 * h + c, 1) for h in range(2) for c in range(DC)]
    for h in range(2):
        for m in range(FM):
            k = (4 + 2 * (FM * h + m)) % 8
            expert += [(f"gate{h}_{m}", k, 1), (f"up{h}_{m}", k + 1, 1)]
    expert += [(f"down{j}", (4 + j) % 8, 1) for j in range(CT // 2)]
    return setup, body, route, expert


class Banks:

    def __init__(self, filled, freed):
        self.filled, self.freed = filled, freed
        self.at = {}
        fills, takes = [0] * 8, [1] * 8
        for k, (section, times) in enumerate(zip(psum_plan(), (1, B, 1, E))):
            f0, t0 = list(fills), list(takes)
            here = {}
            for name, bank, n in section:
                here[name] = (bank, fills[bank] + 1 - f0[bank], takes[bank] - t0[bank])
                fills[bank] += 1
                takes[bank] += n
            per_f = [a - b for a, b in zip(fills, f0)]
            per_t = [a - b for a, b in zip(takes, t0)]
            for name, (bank, f, t) in here.items():
                self.at[(k, name)] = (bank, f0[bank], per_f[bank], f, t0[bank], per_t[bank], t)
            fills = [a + (times - 1) * n for a, n in zip(fills, per_f)]
            takes = [a + (times - 1) * n for a, n in zip(takes, per_t)]

    def bank(self, section, name):
        return self.at[(section, name)][0]

    def wait_free(self, pe, section, name, i=0):
        bank, _, _, _, base, per, n = self.at[(section, name)]
        pe.wait_ge(self.freed[bank], i * per + (base + n))

    def wait_taken(self, eng, section, name, i=0):
        bank, _, _, _, base, per, n = self.at[(section, name)]
        eng.wait_ge(self.freed[bank], i * per + (base + n + 1))

    def wait_filled(self, eng, section, name, i=0):
        bank, base, per, n, _, _, _ = self.at[(section, name)]
        eng.wait_ge(self.filled[bank], i * per + (base + n))


SETUP, BODY, ROUTE, EXPERT = range(4)
LOADS = 32
SEARCH = 30


def early_fusion_kernel(nc, a, const, out):
    ctx = ExitStack()
    offsets = {"top": nc.sbuf_base + (-nc.sbuf_base) % 64}

    def width(shape):
        return 4 * int(np.prod(shape[1:]))

    def place(name, shape, dt, at):
        assert at + width(shape) <= nc.sbuf_usable_end, (name, at + width(shape))
        return nc.alloc_sbuf_tensor_at(name, shape, dt, offset=at)

    def sb(name, shape, dt=F32):
        at = offsets["top"]
        offsets["top"] = at + (width(shape) + 31) // 32 * 32
        return place(name, shape, dt, at)

    def region(at, *tensors):
        made = []
        for name, shape, dt in tensors:
            made.append(place(name, shape, dt, at))
            at += (width(shape) + 31) // 32 * 32
        return made, at

    with ctx:
        def sem(name):
            return ctx.enter_context(nc.semaphore(name))

        h_dram = nc.dram_tensor("h_rows", [T, D], F32).ap()
        xn_dram = nc.dram_tensor("xn_rows", [T, D], F32).ap()
        xg_dram = nc.dram_tensor("expert_in", [E * CAP, D], F32).ap()
        yg_dram = nc.dram_tensor("expert_out", [E * CAP, D], F32).ap()

        cst = sb("cst", [P, NC_COLS])

        def const_cols(name):
            x, y = COLS[name]
            return cst[:, x:y]

        ident = const_cols("ident")
        logits_all = sb("logits_all", [P, TILES, E])
        small = sb("small", [P, 96])
        loop_start = offsets["top"]
        wqkv = sb("wqkv", [P, DC, 3 * D])
        wo0 = sb("wo0", [P, DC, D])
        w1 = sb("w1", [P, DC, FF])
        w2 = sb("w2", [P, FM, D])
        f1T = sb("f1T", [P, DC, FF])
        f2T = sb("f2T", [P, FM, D])
        wq1 = sb("wq1", [P, 8, 2, HD1])
        wk1 = sb("wk1", [P, KV1 * HD1])
        wv1 = sb("wv1", [P, KV1 * HD1])
        wo1 = sb("wo1", [P, 8, D])
        wr = sb("wr", [P, DC, E])
        rows = sb("rows", [P, 3 * D + 3 * D])
        bqkv, bo_r, b2_r, bf2_r = rows[:, 0:768], rows[:, 768:1024], rows[:, 1024:1280], rows[:, 1280:1536]
        cols = sb("cols", [P, 4 * DC + 2 * FM])
        band = sb("band", [P, 2, 3, P])
        edge_w = sb("edge_w", [3, 2, 2, P])
        alibi = sb("alibi", [P, H1, S])
        img = sb("img", [P, 3, 2, IMG])
        halo = sb("halo", [3, 3, 2, IMG])
        gray = sb("gray", [P, 2, IMG + 2])
        halo_gray = sb("halo_gray", [3, 2, IMG])
        h = sb("h", [P, NT, D])
        x1 = sb("x1", [P, NT, D])
        xh = sb("xh", [P, NT, D])
        y = sb("y", [P, NT, D])
        xT = sb("xT", [P, DC, S])
        stats = sb("stats", [P, NT, 6])
        mean_var = sb("mean_var", [P, NT, 2])
        rstd = sb("rstd", [P, NT])
        eps = sb("eps", [P, NT])
        carrier = sb("carrier", [P, 5])
        power = sb("power", [P, NT])
        vpad = sb("vpad", [P, NT, 8, 64])
        nmax = sb("nmax", [P, 2, NT])
        rowsum = sb("rowsum", [P, 2, NT])
        rinv = sb("rinv", [P, 2, NT])
        attention_start = offsets["top"]
        masked = sb("masked", [P, 2, 2 * S])
        probs = sb("probs", [P, 2, 2 * S])
        probsT = sb("probsT", [P, 2, 2 * S])
        o0T = sb("o0T", [P, DC, S])
        shared = offsets["top"]
        (stack_q, stack_k, q0T, k0T, qk, rot1, rot2), end_shared = region(
            shared, ("stack_q", [P, 2, H0 * 64], F32R), ("stack_k", [P, 2, H0 * 64], F32R),
            ("q0T", [P, 8, S], F32R), ("k0T", [P, 8, S], F32R),
            ("qk", [P, 512], F32), ("rot1", [P, 512], F32), ("rot2", [P, 512], F32))
        (q1T, k1T, v1, o1T), _ = region(
            shared, ("q1T", [P, 8, S], F32), ("k1T", [P, 2, S], F32),
            ("v1", [P, NT, KV1 * HD1], F32), ("o1T", [P, 8, S], F32))
        (hidT,), _ = region(shared, ("hidT", [P, FM, S], F32))
        (edge,), _ = region(shared, ("edge", [P, 2, 512], F32))

        (emb, embT, proj_raw, projT, txt_rows, hashf, hash_i, wq1_raw, rot_tmp, ang, scharr_b, scharr_h, zeros,
         tok, by0, by1, by2, by3, t_hi, t_lo, f1_raw, f2_raw, tern, tern_b), _ = region(
            attention_start,
            ("emb", [P, B, EMB], F32), ("embT", [EMB, 2, P], F32), ("proj_raw", [P, 2, EMB], F32),
            ("projT", [EMB, D], F32), ("txt_rows", [P, B, D], F32), ("hashf", [B, 4, TXT], F32),
            ("hash_i", [P, B], I32), ("wq1_raw", [P, H1, HD1 // 2, 2], F32), ("rot_tmp", [P, 2, P], F32),
            ("ang", [P, 8, H1], F32), ("scharr_b", [P, 2, 3, 3], F32), ("scharr_h", [3, 2, 3], F32),
            ("zeros", [P, 1024], F32),
            *[(n, [B, 2, TXT + 1], I32) for n in ("tok", "by0", "by1", "by2", "by3", "t_hi", "t_lo")],
            ("f1_raw", [P, FM, D], F32), ("f2_raw", [P, DC, FF], F32),
            ("tern", [P, 2048], F32), ("tern_b", [P, 2048], F32))
        txt_scale = small[:, 8:9]
        absum, above, below, gsum = small[:, 0:2], small[:, 2:4], small[:, 4:6], small[:, 6:8]

        (gate_w, up_w, down_w, xe, xeT, sil, hT, ye), end_e = region(
            loop_start, ("gate_w", [P, DC, FF], F32), ("up_w", [P, DC, FF], F32), ("down_w", [P, FM, D], F32),
            ("xe", [P, CT, D], F32), ("xeT", [P, DC, CAP], F32), ("sil", [P, 2, HALF], F32),
            ("hT", [P, FM, CAP], F32), ("ye", [P, CT, D], F32))
        (xall,), end_x = region(end_e, ("xall", [P, TILES, D], F32))
        (pr, oh1, oh2, gts, selm, eqm, r_a, r_b, r_c, r_tot), end_r = region(
            end_x, *[(n, [P, E, TILES], F32) for n in (
                "pr", "oh1", "oh2", "gts", "selm", "eqm", "r_a", "r_b", "r_c", "r_tot")])
        (sel_eq, kv, cand, thr, bit, cnt, want, pos_f, scat_i, gath_i, wk), _ = region(
            end_r, ("sel_eq", [P, 2, E * TILES], F32), ("kv", [P, 8, TILES], F32), ("cand", [P, E], I32),
            ("thr", [P, E], I32), ("bit", [P, 1], I32), ("cnt", [P, E], F32), ("want", [P, E], F32),
            ("pos_f", [P, 4, TILES], F32), ("scat_i", [P, 2, TILES], I32), ("gath_i", [P, 2, TILES], I32),
            ("wk", [P, 2, TILES], F32))
        (y1, y2), _ = region(loop_start, ("y1", [P, TILES, D], F32), ("y2", [P, TILES, D], F32))

        ps = [ctx.enter_context(nc.psum_tensor(f"bank{k}", [P, 512], F32)) for k in range(8)]

        filled = [sem(f"bank{k}_filled") for k in range(8)]
        freed = [sem(f"bank{k}_freed") for k in range(8)]
        banks = Banks(filled, freed)
        loaded = sem("loaded")
        tokens_loaded = sem("tokens_loaded")
        zeros_ready = sem("zeros_ready")
        cleared = sem("cleared")
        expert_in_cleared = sem("expert_in_cleared")
        hash_ready = sem("hash_ready")
        emb_loaded = sem("emb_loaded")
        abs_ready = sem("abs_ready")
        ternary_ready = sem("ternary_ready")
        reduced = sem("reduced")
        angles_ready = sem("angles_ready")
        setup_dve = sem("setup_dve")
        img_loaded = sem("img_loaded")
        gray_ready = sem("gray_ready")
        txt_row_loaded = sem("txt_row_loaded")
        h_stored = sem("h_stored")
        var_ready = sem("var_ready")
        rstd_ready = sem("rstd_ready")
        norm_ready = sem("norm_ready")
        qk_ready = sem("qk_ready")
        rot2_ready = sem("rot2_ready")
        roped = sem("roped")
        stack_hi = sem("stack_hi")
        stack_ready = sem("stack_ready")
        masked_ready = sem("masked_ready")
        exp_done = sem("exp_done")
        rinv_ready = sem("rinv_ready")
        probs_ready = sem("probs_ready")
        resid_ready = sem("resid_ready")
        logits_ready = sem("logits_ready")
        xall_loaded = sem("xall_loaded")
        lse_shift = sem("lse_shift")
        lse_exp = sem("lse_exp")
        counts_ready = sem("counts_ready")
        counts_taken = sem("counts_taken")
        sel_ready = sem("sel_ready")
        index_ready = sem("index_ready")
        scattered = sem("scattered")
        expert_gate_loaded = sem("expert_gate_loaded")
        expert_down_loaded = sem("expert_down_loaded")
        xe_loaded = sem("xe_loaded")
        ye_free = sem("ye_free")
        gathered = [sem(f"gathered{k}") for k in range(4)]
        h_reloaded = sem("h_reloaded")
        out_ready = sem("out_ready")
        out_stored = sem("out_stored")

        block = ctx.enter_context(nc.Block())

        def scores_place(layer, n, t):
            if t == 1:
                return ps[banks.bank(BODY, f"scores_b{layer}_{n}")][:, 0:2 * P]
            return ps[banks.bank(BODY, f"scores{layer}_{n}")][:, (0, 0, P)[t]:(P, 0, 4 * P)[t]]

        def pair_head(n):
            m, s = divmod(n, 2)
            return 8 * (m // 4) + 4 * s + m % 4

        def seg(t):
            return slice(SEG[t], SEG[t] + P * (t + 1))

        @block.sync
        def _(sp):
            sp.dma_start(cst[:], const).then_inc(loaded, 16)
            for s in range(2):
                sp.dma_start(tok[:, s, 1:], a["x_txt"]).then_inc(tokens_loaded, 16)
            n = 1
            for dst, src in (
                (f1_raw[:], a["L0_ffn_W1"].rearrange("(m p) d -> p m d", p=P)),
                (f2_raw[:], a["L0_ffn_W2"].rearrange("(c p) f -> p c f", p=P)),
                (proj_raw[:], a["L0_txt_proj_weight"].rearrange("(c p) e -> p c e", p=P)),
                (wq1_raw[:].rearrange("p h i r -> p (h i r)"), a["L1_attn_Wq"]),
                (wqkv[:], a["L0_attn_Wqkv"].rearrange("(c p) n -> p c n", p=P)),
                (wo0[:], a["L0_attn_Wo"].rearrange("(c p) n -> p c n", p=P)),
                (w1[:], a["L0_attn_W1"].rearrange("(c p) n -> p c n", p=P)),
                (w2[:], a["L0_attn_W2"].rearrange("(m p) n -> p m n", p=P)),
                (wk1[:], a["L1_attn_Wk"]),
                (wv1[:], a["L1_attn_Wv"]),
                (bqkv, a["L0_attn_bqkv"].partition_broadcast(P)),
                (bo_r, a["L0_attn_bo"].partition_broadcast(P)),
                (b2_r, a["L0_attn_b2"].partition_broadcast(P)),
                (bf2_r, a["L0_ffn_b2"].partition_broadcast(P)),
                (ang[:, 0, :], a["L1_attn_q_phase_angle"].partition_broadcast(P)),
                (ang[:, 1, :], a["L1_attn_alibi_log_slopes"].partition_broadcast(P)),
                (scharr_b[:].rearrange("p k a b -> p (k a b)"),
                 a["L0_tok_scharr"].rearrange("k o a b -> (k o a b)").partition_broadcast(P)),
                (txt_scale, a["L0_txt_scale"].partition_broadcast(P)),
                (wr[:], a["L1_ffn_router_gate"].rearrange("(c p) e -> p c e", p=P)),
            ):
                sp.dma_start(dst, src).then_inc(loaded, 16)
                n += 1
            wo1_src = a["L1_attn_Wo"].rearrange("(g s r d) n -> g s d r n", g=2, s=2, r=4, d=HD1)
            for g in range(2):
                for s in range(2):
                    sp.dma_start(wo1[64 * s:64 * s + 64, 4 * g:4 * g + 4, :], wo1_src[g, s]).then_inc(loaded, 16)
                    n += 1
            for k, name in enumerate(("L0_attn_ln1_g", "L0_attn_ln1_b", "L0_attn_ln2_g", "L0_attn_ln2_b")):
                sp.dma_start(cols[:, DC * k:DC * k + DC], a[name].rearrange("(c p) -> p c", p=P),
                             allow_slow_non_contiguous=True).then_inc(loaded, 16)
                n += 1
            for k, name in enumerate(("L0_attn_b1", "L0_ffn_b1")):
                sp.dma_start(cols[:, 4 * DC + FM * k:4 * DC + FM * k + FM], a[name].rearrange("(m p) -> p m", p=P),
                             allow_slow_non_contiguous=True).then_inc(loaded, 16)
                n += 1
            for k in range(2):
                sp.dma_start(scharr_h[:, k, :], a["L0_tok_scharr"][k, 0].rearrange("a b -> b a"),
                             allow_slow_non_contiguous=True).then_inc(loaded, 16)
                n += 1
            assert n == LOADS
            sp.wait_ge(zeros_ready, 1)
            for r in range(E * CAP // (4 * P)):
                sp.dma_start(xg_dram[4 * P * r:4 * P * (r + 1)].rearrange("(p q) d -> p (q d)", q=4), zeros[:]) \
                    .then_inc(expert_in_cleared, 16)
            banks.wait_taken(sp, SETUP, f"txt{B - 1}")
            sp.dma_start(h_dram.rearrange("(b t p) d -> p b t d", b=B, t=NT)[:, :, NT - 1, :],
                         txt_rows[:]).then_inc(h_stored, 16)
            sp.wait_ge(h_stored, 16)

            def load_image(i):
                x = a["x"]
                sp.dma_start(img[:].rearrange("p c h w -> p (c h) w"),
                             x[i].rearrange("c (h p) w -> p (c h) w", p=P)).then_inc(img_loaded, 16)
                for dx in range(3):
                    lo, hi = max(0, 1 - dx), min(IMG, IMG + 1 - dx)
                    sp.dma_start(halo[dx:dx + 1, :, :, lo:hi],
                                 x[i, :, P - 1:P + 1, lo + dx - 1:hi + dx - 1].unsqueeze(0)).then_inc(img_loaded, 16)

            def load_text(i):
                sp.dma_start(h[:, NT - 1, :], h_dram.rearrange("(b t p) d -> b t p d", b=B, t=NT)[i, NT - 1]) \
                    .then_inc(txt_row_loaded, 16)

            def store_tokens(i):
                sp.wait_ge(norm_ready, 5 * i + 5)
                sp.dma_start(xn_dram.rearrange("(b t p) d -> b p t d", b=B, t=NT)[i], xh[:]).then_inc(h_stored, 16)
                sp.dma_start(h_dram.rearrange("(b t p) d -> b p t d", b=B, t=NT)[i], h[:]).then_inc(h_stored, 16)
                sp.wait_ge(h_stored, 32 * i + 48)

            sp.wait_ge(cleared, 1)
            load_image(0)
            load_text(0)
            with sp.Fori(0, B - 1) as i:
                sp.wait_ge(gray_ready, i + 1)
                load_image(i + 1)
                store_tokens(i)
                load_text(i + 1)
            store_tokens(B - 1)

            sp.dma_start(xall[:], xn_dram.rearrange("(n p) d -> p n d", p=P)).then_inc(xall_loaded, 16)

            def load_gate_up(e):
                sp.dma_start(gate_w[:], a["L1_ffn_gate_w"][e].rearrange("(c p) n -> p c n", p=P)) \
                    .then_inc(expert_gate_loaded, 16)
                sp.dma_start(up_w[:], a["L1_ffn_up_w"][e].rearrange("(c p) n -> p c n", p=P)) \
                    .then_inc(expert_gate_loaded, 16)

            def load_down(e):
                sp.dma_start(down_w[:], a["L1_ffn_down_w"][e].rearrange("(m p) n -> p m n", p=P)) \
                    .then_inc(expert_down_loaded, 16)

            def load_rows(e):
                sp.dma_start(xe[0:CP], xg_dram.rearrange("(e j p) d -> e p j d", e=E, j=CT)[e]).then_inc(xe_loaded, 16)

            yg_view = yg_dram.rearrange("(e s j p) d -> e s p j d", e=E, s=2, p=CP)

            def store_rows(e):
                for s in range(2):
                    banks.wait_taken(sp, EXPERT, f"down{2 * s + 1}", e)
                    sp.dma_start(yg_view[e, s], ye[0:CP, CT // 2 * s:CT // 2 * (s + 1)]).then_inc(ye_free, 16)

            sp.wait_ge(logits_ready, B)
            load_gate_up(0)
            load_down(0)
            sp.wait_ge(scattered, 16 * 2 * TILES)
            load_rows(0)
            with sp.Fori(0, E - 1) as e:
                banks.wait_filled(sp, EXPERT, f"xT{DC - 1}_1", e)
                load_rows(e + 1)
                banks.wait_filled(sp, EXPERT, f"up1_{FM - 1}", e)
                load_gate_up(e + 1)
                store_rows(e)
                load_down(e + 1)
            store_rows(E - 1)

            sp.wait_ge(ye_free, 32 * E + 16)
            sp.dma_start(xall[:], h_dram.rearrange("(n p) d -> p n d", p=P)).then_inc(h_reloaded, 16)
            for k in range(4):
                sp.wait_ge(out_ready, k + 1)
                n0, n1 = TILES // 4 * k, TILES // 4 * (k + 1)
                sp.dma_start(out.rearrange("b (t p) d -> p (b t) d", p=P)[:, n0:n1], xall[:, n0:n1]) \
                    .then_inc(out_stored, 16)
            sp.wait_ge(out_stored, 64)

        @block.tensor
        def _(pe):
            mm, tr = nc.tensor.matmul, nc.tensor.transpose

            def transposed(section, prefix, src, i, what, count):
                pe.wait_ge(what, count)
                for c in range(DC):
                    name = f"{prefix}{c}"
                    banks.wait_free(pe, section, name, i)
                    bank = banks.bank(section, name)
                    for t in range(NT):
                        last = tr(ps[bank][:, P * t:P * (t + 1)], src[:, t, P * c:P * (c + 1)], ident)
                    last.then_inc(filled[bank], 1)

            pe.wait_ge(loaded, 16 * LOADS)
            banks.wait_free(pe, SETUP, "projT")
            for c in range(DC):
                last = tr(ps[1][0:EMB, P * c:P * (c + 1)], proj_raw[:, c, :], ident)
            last.then_inc(filled[1], 1)
            pe.wait_ge(hash_ready, 1)
            banks.wait_free(pe, SETUP, "txt_index")
            tr(ps[0][:, 0:B], hashf[:, 0, :], ident[0:B, 0:B]).then_inc(filled[0], 1)
            pe.wait_ge(abs_ready, 1)
            banks.wait_free(pe, SETUP, "gamma")
            mm(ps[6][:, 0:2], const_cols("ones"), absum, start=True, stop=True).then_inc(filled[6], 1)
            pe.wait_ge(emb_loaded, 16 * B)
            banks.wait_taken(pe, SETUP, "projT")
            for b in range(B + 1):
                if b < B:
                    k = banks.bank(SETUP, f"embT{b}")
                    banks.wait_free(pe, SETUP, f"embT{b}")
                    tr(ps[k][0:EMB, 0:P], emb[:, b, :], ident).then_inc(filled[k], 1)
                if b > 0:
                    k = banks.bank(SETUP, f"txt{b - 1}")
                    banks.wait_free(pe, SETUP, f"txt{b - 1}")
                    banks.wait_taken(pe, SETUP, f"embT{b - 1}")
                    mm(ps[k][:, 0:D], embT[:, (b - 1) % 2, :], projT[:], start=True, stop=True) \
                        .then_inc(filled[k], 1)
            for g in range(4):
                k = banks.bank(SETUP, f"f1T{g}")
                banks.wait_free(pe, SETUP, f"f1T{g}")
                pe.wait_ge(ternary_ready, 1)
                c, m0 = divmod(g, 2)
                for q in range(4):
                    m = 4 * m0 + q
                    last = tr(ps[k][:, P * q:P * (q + 1)], tern[:, D * m + P * c:D * m + P * (c + 1)], ident)
                last.then_inc(filled[k], 1)
            for g in range(4):
                k = banks.bank(SETUP, f"f2T{g}")
                banks.wait_free(pe, SETUP, f"f2T{g}")
                pe.wait_ge(ternary_ready, 2)
                for q in range(4):
                    m, c = 2 * g + q // 2, q % 2
                    last = tr(ps[k][:, P * q:P * (q + 1)], tern_b[:, FF * c + P * m:FF * c + P * (m + 1)], ident)
                last.then_inc(filled[k], 1)
            pe.wait_ge(setup_dve, 1)
            banks.wait_taken(pe, SETUP, "f2T3")

            def head_scores(layer, n, i):
                ba, bb = banks.bank(BODY, f"scores{layer}_{n}"), banks.bank(BODY, f"scores_b{layer}_{n}")
                banks.wait_free(pe, BODY, f"scores{layer}_{n}", i)
                banks.wait_free(pe, BODY, f"scores_b{layer}_{n}", i)
                for t in (0, 2, 1):
                    if layer == 0:
                        half = slice(64 * (n % 2), 64 * (n % 2) + 64)
                        q, k = q0T[half, n // 2, :], k0T[half, n // 2, :]
                    else:
                        half = slice(64 * (n % 2), 64 * (n % 2) + 64)
                        q, k = q1T[half, n // 2, :], k1T[half, n // 8, :]
                    last = mm(scores_place(layer, n, t), q[:, P * t:P * (t + 1)], k[:, 0:P * (t + 1)],
                              start=True, stop=True)
                    if t == 2:
                        last.then_inc(filled[ba], 1)
                last.then_inc(filled[bb], 1)

            def probs_transposed(layer, n, i):
                ba, bb = banks.bank(BODY, f"probsT{layer}_{n}"), banks.bank(BODY, f"probsT_b{layer}_{n}")
                pe.wait_ge(probs_ready, 2 * HEADS * i + (HEADS * layer + n + 1))
                p = probs[:, n % 2, :]
                banks.wait_free(pe, BODY, f"probsT{layer}_{n}", i)
                for t in range(NT):
                    last = tr(ps[ba][:, P * t:P * (t + 1)], p[:, SEG[t]:SEG[t] + P], ident)
                last = tr(ps[ba][:, 3 * P:4 * P], p[:, SEG[2] + 2 * P:SEG[2] + 3 * P], ident)
                last.then_inc(filled[ba], 1)
                banks.wait_free(pe, BODY, f"probsT_b{layer}_{n}", i)
                for t in (1, 2):
                    last = tr(ps[bb][:, P * (t - 1):P * t], p[:, SEG[t] + P:SEG[t] + 2 * P], ident)
                last.then_inc(filled[bb], 1)

            def head_out(layer, n, i):
                c = n // 8 if layer == 0 else n // 2
                bank = banks.bank(BODY, f"out{layer}_{c}")
                if n == c * (8 if layer == 0 else 2):
                    banks.wait_free(pe, BODY, f"out{layer}_{c}", i)
                banks.wait_taken(pe, BODY, f"probsT{layer}_{n}", i)
                banks.wait_taken(pe, BODY, f"probsT_b{layer}_{n}", i)
                pT = probsT[:, n % 2, :]
                for j, cols_j in enumerate((slice(0, 3 * P), slice(4 * P, 6 * P), slice(3 * P, 4 * P))):
                    if layer == 0:
                        rows_o = slice(32 * (n % 8 // 2), 32 * (n % 8 // 2) + 32)
                        v = vpad[:, j, n // 2, 32 * (n % 2):32 * (n % 2) + 32]
                        first, final = n % 2 == 0 and j == 0, n % 2 == 1 and j == 2
                    else:
                        rows_o = slice(64 * (n % 2), 64 * (n % 2) + 64)
                        kv = pair_head(n) // 4
                        v = v1[:, j, HD1 * kv:HD1 * (kv + 1)]
                        first, final = j == 0, j == 2
                    last = mm(ps[bank][rows_o, P * j:S], v, pT[:, cols_j], start=first, stop=final)
                if n % (8 if layer == 0 else 2) == (7 if layer == 0 else 1):
                    last.then_inc(filled[bank], 1)

            def attention(layer, i):
                head_scores(layer, 0, i)
                head_scores(layer, 1, i)
                for n in range(HEADS):
                    if n + 2 < HEADS:
                        head_scores(layer, n + 2, i)
                    probs_transposed(layer, n, i)
                    if n >= 1:
                        head_out(layer, n - 1, i)
                head_out(layer, HEADS - 1, i)

            def token_major(names, i, lhs, weights, chunks, n_cols=D):
                for t in range(NT):
                    name = names[t // 2]
                    bank = banks.bank(BODY, name)
                    if t != 1:
                        banks.wait_free(pe, BODY, name, i)
                    o = ps[bank][:, n_cols * (t % 2):n_cols * (t % 2) + n_cols]
                    for m in range(chunks):
                        last = mm(o, lhs[:, m, P * t:P * (t + 1)], weights[:, m, :],
                                  start=(m == 0), stop=(m == chunks - 1))
                    if t != 0:
                        last.then_inc(filled[bank], 1)

            def xT_wait(i, name):
                for c in range(DC):
                    banks.wait_taken(pe, BODY, f"{name}{c}", i)

            def up(names, i, w):
                for m in range(FM):
                    bank = banks.bank(BODY, names + str(m))
                    banks.wait_free(pe, BODY, names + str(m), i)
                    for c in range(DC):
                        last = mm(ps[bank][:, 0:S], w[:, c, P * m:P * (m + 1)], xT[:, c, :],
                                  start=(c == 0), stop=(c == DC - 1))
                    last.then_inc(filled[bank], 1)

            with pe.Fori(0, B) as i:
                pe.wait_ge(gray_ready, i + 1)
                for hf in range(2):
                    name = f"conv{hf}"
                    bank = banks.bank(BODY, name)
                    banks.wait_free(pe, BODY, name, i)
                    for k in range(2):
                        o = ps[bank][:, IMG * k:IMG * (k + 1)]
                        for dx in range(3):
                            mm(o, band[:, k, dx, :], gray[:, hf, dx:dx + IMG], start=(dx == 0), stop=False)
                        last = mm(o, edge_w[:, hf, k, :], halo_gray[:, 1 - hf, :], start=False, stop=True)
                    last.then_inc(filled[bank], 1)

                transposed(BODY, "ln_attn0_T", xh, i, norm_ready, 5 * i + 1)
                xT_wait(i, "ln_attn0_T")
                for t in range(NT):
                    bq, bv = banks.bank(BODY, f"qk0_{t}"), banks.bank(BODY, f"v0_{t}")
                    banks.wait_free(pe, BODY, f"qk0_{t}", i)
                    for c in range(DC):
                        last = mm(ps[bq][:], xT[:, c, P * t:P * (t + 1)], wqkv[:, c, 0:2 * D],
                                  start=(c == 0), stop=(c == DC - 1))
                    last.then_inc(filled[bq], 1)
                    banks.wait_free(pe, BODY, f"v0_{t}", i)
                    for c in range(DC):
                        last = mm(ps[bv][:, 0:D], xT[:, c, P * t:P * (t + 1)], wqkv[:, c, 2 * D:3 * D],
                                  start=(c == 0), stop=(c == DC - 1))
                    last.then_inc(filled[bv], 1)
                for t in range(NT):
                    pe.wait_ge(stack_ready, NT * i + (t + 1))
                    for g in range(4):
                        bank = banks.bank(BODY, f"stack{t}_{g}")
                        banks.wait_free(pe, BODY, f"stack{t}_{g}", i)
                        src = (stack_q, stack_k)[g // 2][:, t % 2, :].bitcast(F32)
                        for q in range(4):
                            hp = 4 * (g % 2) + q
                            last = tr(ps[bank][:, P * q:P * (q + 1)], src[:, P * hp:P * (hp + 1)], ident)
                        last.then_inc(filled[bank], 1)
                for g in (2, 3):
                    banks.wait_taken(pe, BODY, f"stack{NT - 1}_{g}", i)
                attention(0, i)
                banks.wait_taken(pe, BODY, "out0_1", i)
                token_major(("proj0_a", "proj0_b"), i, o0T, wo0, DC)

                transposed(BODY, "ln_mlp_T", xh, i, norm_ready, 5 * i + 2)
                xT_wait(i, "ln_mlp_T")
                up("up0_", i, w1)
                banks.wait_taken(pe, BODY, f"up0_{FM - 1}", i)
                token_major(("down0_a", "down0_b"), i, hidT, w2, FM)

                transposed(BODY, "ln_ffn_T", xh, i, norm_ready, 5 * i + 3)
                xT_wait(i, "ln_ffn_T")
                up("up1_", i, f1T)
                for m in (FM - 2, FM - 1):
                    banks.wait_taken(pe, BODY, f"up1_{m}", i)
                token_major(("down1_a", "down1_b"), i, hidT, f2T, FM)

                transposed(BODY, "ln_attn1_T", xh, i, norm_ready, 5 * i + 4)
                xT_wait(i, "ln_attn1_T")
                for m in range(2):
                    bank = banks.bank(BODY, f"k1_{m}")
                    banks.wait_free(pe, BODY, f"k1_{m}", i)
                    mm(ps[bank][:, 0:S], wk1[:, P * m:P * (m + 1)], xT[:, 1, :], start=True, stop=True) \
                        .then_inc(filled[bank], 1)
                for t in range(NT):
                    bank = banks.bank(BODY, f"v1_{t}")
                    banks.wait_free(pe, BODY, f"v1_{t}", i)
                    mm(ps[bank][:, 0:KV1 * HD1], xT[:, 0, P * t:P * (t + 1)], wv1[:], start=True, stop=True) \
                        .then_inc(filled[bank], 1)
                for m in range(8):
                    bank = banks.bank(BODY, f"q1_{m}")
                    banks.wait_free(pe, BODY, f"q1_{m}", i)
                    mm(ps[bank][:, 0:S], wq1[:, m].rearrange("p s d -> p (s d)"), xT[:, 1, :],
                       start=True, stop=True).then_inc(filled[bank], 1)
                for m in (6, 7):
                    banks.wait_taken(pe, BODY, f"q1_{m}", i)
                attention(1, i)
                banks.wait_taken(pe, BODY, "out1_7", i)
                token_major(("proj1_a", "proj1_b"), i, o1T, wo1, 8)

                transposed(BODY, "ln_moe_T", xh, i, norm_ready, 5 * i + 5)
                xT_wait(i, "ln_moe_T")
                bank = banks.bank(BODY, "logits")
                banks.wait_free(pe, BODY, "logits", i)
                for t in range(NT):
                    for c in range(DC):
                        last = mm(ps[bank][:, E * t:E * (t + 1)], xT[:, c, P * t:P * (t + 1)], wr[:, c, :],
                                  start=(c == 0), stop=(c == DC - 1))
                last.then_inc(filled[bank], 1)

            with pe.Fori(0, SEARCH) as r:
                pe.wait_ge(counts_ready, r + 1)
                mm(ps[7][:, 0:E], const_cols("ones"), cnt[:], start=True, stop=True).then_inc(counts_taken, 1)
            for k, name in enumerate(("prefix", "slots")):
                bank = banks.bank(ROUTE, name)
                pe.wait_ge(sel_ready, k + 1)
                banks.wait_free(pe, ROUTE, name)
                w = E * TILES
                if k == 0:
                    mm(ps[6][:, 0:w], const_cols("ones"), sel_eq[:, 1, :], start=True, stop=True)
                mm(ps[bank][:, 0:w], const_cols("ones"), sel_eq[:, 0, :], start=True, stop=True)
                mm(ps[bank][:, w:2 * w], const_cols("before"), sel_eq[:, 0, :], start=True, stop=True) \
                    .then_inc(filled[bank], 1)

            with pe.Fori(0, E) as e:
                pe.wait_ge(xe_loaded, 16 * e + 16)
                for hf in range(2):
                    for c in range(DC):
                        bank = banks.bank(EXPERT, f"xT{c}_{hf}")
                        banks.wait_free(pe, EXPERT, f"xT{c}_{hf}", e)
                        for q in range(4):
                            last = tr(ps[bank][:, CP * q:CP * (q + 1)], xe[0:CP, 4 * hf + q, P * c:P * (c + 1)],
                                      ident[0:CP, 0:CP])
                        last.then_inc(filled[bank], 1)
                pe.wait_ge(expert_gate_loaded, 32 * e + 32)
                for hf in range(2):
                    for c in range(DC):
                        banks.wait_taken(pe, EXPERT, f"xT{c}_{hf}", e)
                    for m in range(FM):
                        for name, w in ((f"gate{hf}_{m}", gate_w), (f"up{hf}_{m}", up_w)):
                            bank = banks.bank(EXPERT, name)
                            banks.wait_free(pe, EXPERT, name, e)
                            for c in range(DC):
                                last = mm(ps[bank][:, 0:HALF], w[:, c, P * m:P * (m + 1)],
                                          xeT[:, c, HALF * hf:HALF * (hf + 1)],
                                          start=(c == 0), stop=(c == DC - 1))
                            last.then_inc(filled[bank], 1)
                pe.wait_ge(expert_down_loaded, 16 * e + 16)
                for j in range(CT):
                    bank = banks.bank(EXPERT, f"down{j // 2}")
                    if j % 2 == 0:
                        banks.wait_free(pe, EXPERT, f"down{j // 2}", e)
                    if j in (0, 4):
                        banks.wait_taken(pe, EXPERT, f"up{j // 4}_{FM - 1}", e)
                    for m in range(FM):
                        last = mm(ps[bank][0:CP, D * (j % 2):D * (j % 2) + D], hT[:, m, CP * j:CP * (j + 1)],
                                  down_w[:, m, :], start=(m == 0), stop=(m == FM - 1))
                    if j % 2 == 1:
                        last.then_inc(filled[bank], 1)

        @block.scalar
        def _(act):
            f = nc.scalar.activation

            def take(section, name, i, dst, fn, width, rows_p=P, **kw):
                banks.wait_filled(act, section, name, i)
                bank = banks.bank(section, name)
                src = ps[bank][0:rows_p, 0:width]
                if fn is None:
                    ins = nc.scalar.copy(dst, src)
                else:
                    ins = f(dst, src, fn, **kw)
                ins.then_inc(freed[bank], 1)

            act.wait_ge(loaded, 16 * LOADS)
            take(SETUP, "projT", 0, projT[:], None, D, EMB)
            for b in range(B):
                if b >= 2:
                    banks.wait_filled(act, SETUP, f"txt{b - 2}")
                take(SETUP, f"embT{b}", 0, embT[:, b % 2, :], None, P, EMB)
            act.wait_ge(reduced, 1)
            f(ang[:, 4, :], ang[:, 2, :], ACT.Sin)
            f(ang[:, 5, :], ang[:, 3, :], ACT.Sin)
            f(ang[:, 6, :], ang[:, 1, :], ACT.Exp).then_inc(angles_ready, 1)
            for g in range(4):
                c, m0 = divmod(g, 2)
                take(SETUP, f"f1T{g}", 0, f1T[:, c, 4 * P * m0:4 * P * (m0 + 1)], None, 4 * P)
            for g in range(4):
                take(SETUP, f"f2T{g}", 0, f2T[:, 2 * g:2 * g + 2, :].rearrange("p m n -> p (m n)"), None, 4 * P)
            act.wait_ge(setup_dve, 1)
            act.wait_ge(h_stored, 16)
            act.wait_ge(expert_in_cleared, 16 * (E * CAP // (4 * P)))

            def ln_out(name, i, g=None, b=None):
                if g is None:
                    take(BODY, f"{name}0", i, xT[:, 0, :], None, S)
                else:
                    take(BODY, f"{name}0", i, xT[:, 0, :], ACT.Identity, S,
                         bias=cols[:, b:b + 1], scale=cols[:, g:g + 1])

            def take_stack(t, g, i):
                name = f"stack{t}_{g}"
                banks.wait_filled(act, BODY, name, i)
                bank = banks.bank(BODY, name)
                nc.scalar.copy((q0T, k0T)[g // 2][:, 4 * (g % 2):4 * (g % 2) + 4, P * t:P * (t + 1)],
                               ps[bank][:].rearrange("p (q n) -> p q n", q=4)).then_inc(freed[bank], 1)

            def exps(layer, n, i):
                act.wait_ge(masked_ready, 2 * HEADS * i + (HEADS * layer + n + 1))
                s = n % 2
                if n >= 2:
                    banks.wait_filled(act, BODY, f"probsT_b{layer}_{n - 2}", i)
                for t in range(NT):
                    last = f(probs[:, s, seg(t)], masked[:, s, seg(t)], ACT.Exp, bias=nmax[:, s, t:t + 1],
                             accum_out=rowsum[:, s, t:t + 1])
                last.then_inc(exp_done, 1)

            def attention(layer, i):
                per = 8 if layer == 0 else 2
                exps(layer, 0, i)
                for n in range(HEADS):
                    if n + 1 < HEADS:
                        exps(layer, n + 1, i)
                    take(BODY, f"probsT{layer}_{n}", i, probsT[:, n % 2, 0:4 * P], None, 4 * P)
                    if n % per == 0 and n > 0:
                        take(BODY, f"out{layer}_{n // per - 1}", i, (o0T, o1T)[layer][:, n // per - 1, :], None, S)
                c = HEADS // per - 1
                take(BODY, f"out{layer}_{c}", i, (o0T, o1T)[layer][:, c, :], None, S)

            with act.Fori(0, B) as i:
                for hf in range(2):
                    take(BODY, f"conv{hf}", i, edge[:, hf, :], ACT.Abs, 2 * IMG)
                ln_out("ln_attn0_T", i, 0, 2)
                for t in range(NT):
                    act.wait_ge(roped, NT * i + (t + 1))
                    if t >= 2:
                        banks.wait_filled(act, BODY, f"stack{t - 2}_3", i)
                    for x, (dst, slots) in enumerate(((stack_q, (0, 2)), (stack_k, (0, 1)))):
                        o = dst[:, t % 2, :].rearrange("p (h s d) -> p h s d", h=H0, s=4)
                        for s in slots:
                            last = nc.scalar.copy(o[:, :, s, :], rot1[:, D * x:D * (x + 1)].rearrange(
                                "p (h d) -> p h d", h=H0))
                    last.then_inc(stack_hi, 1)
                    if t >= 1:
                        take_stack(t - 1, 0, i)
                        take_stack(t - 1, 2, i)
                take_stack(NT - 1, 0, i)
                take_stack(NT - 1, 2, i)
                attention(0, i)
                ln_out("ln_mlp_T", i, 4, 6)
                for m in range(FM):
                    take(BODY, f"up0_{m}", i, hidT[:, m, :], ACT.Gelu, S,
                         bias=cols[:, 4 * DC + m:4 * DC + m + 1])
                ln_out("ln_ffn_T", i)
                for m in range(0, FM, 2):
                    take(BODY, f"up1_{m}", i, hidT[:, m, :], ACT.Relu, S,
                         bias=cols[:, 4 * DC + FM + m:4 * DC + FM + m + 1])
                ln_out("ln_attn1_T", i)
                for m in range(2):
                    take(BODY, f"k1_{m}", i, k1T[:, m, :], None, S)
                for m in range(0, 8, 2):
                    take(BODY, f"q1_{m}", i, q1T[:, m, :], None, S)
                attention(1, i)
                ln_out("ln_moe_T", i)

            act.wait_ge(lse_shift, 1)
            f(pr[:], pr[:], ACT.Exp).then_inc(lse_exp, 1)

            with act.Fori(0, E) as e:
                for hf in range(2):
                    take(EXPERT, f"xT0_{hf}", e, xeT[:, 0, HALF * hf:HALF * (hf + 1)], None, HALF)
                for hf in range(2):
                    for m in range(FM):
                        k = (FM * hf + m) % 2
                        if FM * hf + m >= 2:
                            banks.wait_taken(act, EXPERT, "up%d_%d" % divmod(FM * hf + m - 2, FM), e)
                        take(EXPERT, f"gate{hf}_{m}", e, sil[:, k, :], ACT.Silu, HALF)
                act.wait_ge(ye_free, 32 * e + 16)
                for j in range(0, 2):
                    take(EXPERT, f"down{j}", e, ye[0:CP, 2 * j:2 * j + 2, :].rearrange("p j d -> p (j d)"),
                         None, 2 * D, CP)

        @block.vector
        def _(dve):
            v = nc.vector
            ts, tt, stt = v.tensor_scalar, v.tensor_tensor, v.scalar_tensor_tensor
            then = v.drain

            def bank_of(section, name, i=0):
                banks.wait_filled(dve, section, name, i)
                k = banks.bank(section, name)
                return ps[k], freed[k]

            v.memset(tok[:, :, 0:1], 0)
            v.memset(zeros[:], 0.0).then_inc(zeros_ready, 1)
            v.memset(halo[:], 0.0)
            v.memset(gray[:], 0.0)
            v.memset(edge_w[:], 0.0)
            v.memset(vpad[:], 0.0)
            v.memset(eps[:], EPS)
            v.memset(power[:], -0.5).then_inc(cleared, 1)
            dve.wait_ge(tokens_loaded, 32)
            then()
            for dst, shift in ((by0, 0), (by1, 8), (by2, 16), (by3, 24)):
                ts(dst[:], tok[:], shift, 255, ALU.logical_shift_right, ALU.bitwise_and)
            then()
            for s, factor in ((0, HASH_CUR), (1, HASH_PREV)):
                for dst in (by0, by1, by2, by3):
                    ts(dst[:, s, :], dst[:, s, :], float(factor), None, ALU.mult)
            then()
            ts(t_lo[:], by1[:], 255, 8, ALU.bitwise_and, ALU.logical_shift_left)
            ts(t_hi[:], by0[:], 0xFFFF, None, ALU.bitwise_and)
            then()
            tt(t_lo[:], t_lo[:], t_hi[:], ALU.add)
            ts(by1[:], by1[:], 8, None, ALU.logical_shift_right)
            ts(by2[:], by2[:], 0xFFFF, None, ALU.bitwise_and)
            ts(by3[:], by3[:], 255, 8, ALU.bitwise_and, ALU.logical_shift_left)
            then()
            ts(t_hi[:], by0[:], 16, None, ALU.logical_shift_right)
            then()
            ts(by0[:], t_lo[:], 16, None, ALU.logical_shift_right)
            for part in (by1, by2, by3, by0):
                then()
                tt(t_hi[:], t_hi[:], part[:], ALU.add)
            then()
            for limb in (t_hi, t_lo):
                ts(limb[:], limb[:], 0xFFFF, None, ALU.bitwise_and)
            then()
            hi, lo = by0[:, 0, 0:TXT], by1[:, 0, 0:TXT]
            tt(hi, t_hi[:, 0, 1:TXT + 1], t_hi[:, 1, 0:TXT], ALU.bitwise_xor)
            tt(lo, t_lo[:, 0, 1:TXT + 1], t_lo[:, 1, 0:TXT], ALU.bitwise_xor)
            then()
            ts(by2[:, 0, 0:TXT], hi, 3, 16, ALU.bitwise_and, ALU.logical_shift_left)
            ts(by3[:, 0, 0:TXT], hi, 2, None, ALU.logical_shift_right)
            ts(by2[:, 1, 0:TXT], hi, 15, None, ALU.logical_shift_right)
            then()
            tt(by2[:, 0, 0:TXT], by2[:, 0, 0:TXT], lo, ALU.bitwise_or)
            then()
            tt(hashf[:, 0, :], by2[:, 0, 0:TXT], by3[:, 0, 0:TXT], ALU.add)
            then()
            stt(hashf[:, 1, :], by2[:, 1, 0:TXT], -16384.0, hashf[:, 0, :], ALU.mult, ALU.add)
            then()
            ts(hashf[:, 2, :], hashf[:, 1, :], 0.0, float(VOCAB_MOD), ALU.is_lt, ALU.mult)
            then()
            tt(hashf[:, 3, :], hashf[:, 1, :], hashf[:, 2, :], ALU.add)
            then()
            ts(hashf[:, 2, :], hashf[:, 3, :], float(VOCAB_MOD), -float(VOCAB_MOD), ALU.is_ge, ALU.mult)
            then()
            tt(hashf[:, 0, :], hashf[:, 3, :], hashf[:, 2, :], ALU.add)
            then()
            v.memset(hashf[:, 0, 0:1], float(VOCAB_MOD)).then_inc(hash_ready, 1)
            k, f_ = bank_of(SETUP, "txt_index")
            v.tensor_copy(hash_i[:], k[:, 0:B]).then_inc(f_, 1)

            dve.wait_ge(loaded, 16 * LOADS)
            v.tensor_reduce(absum[:, 0:1], f1_raw[:].rearrange("p m d -> p (m d)"), AX.X, ALU.add,
                            apply_absolute_value=True)
            v.tensor_reduce(absum[:, 1:2], f2_raw[:].rearrange("p m d -> p (m d)"), AX.X, ALU.add,
                            apply_absolute_value=True).then_inc(abs_ready, 1)
            ts(ang[:, 7, :], ang[:, 0, :], 1.0 / (2 * math.pi), ROUND, ALU.mult, ALU.add)
            then()
            ts(ang[:, 7, :], ang[:, 7, :], ROUND, None, ALU.subtract)
            then()
            stt(ang[:, 2, :], ang[:, 7, :], -TWO_PI_HI, ang[:, 0, :], ALU.mult, ALU.add)
            then()
            stt(ang[:, 2, :], ang[:, 7, :], -TWO_PI_LO, ang[:, 2, :], ALU.mult, ALU.add)
            then()
            ts(ang[:, 2, :], ang[:, 2, :], -math.pi, math.pi, ALU.max, ALU.min)
            then()
            ts(ang[:, 3, :], ang[:, 2, :], -1.0, None, ALU.mult)
            then()
            tt(ang[:, 3, :], ang[:, 3, :], ang[:, 2, :], ALU.max)
            then()
            ts(ang[:, 3, :], ang[:, 3, :], -1.0, math.pi / 2, ALU.mult, ALU.add).then_inc(reduced, 1)
            k, f_ = bank_of(SETUP, "gamma")
            ts(above, k[:, 0:2], 1.0 / (D * FF), EPS, ALU.mult, ALU.add).then_inc(f_, 1)
            then()
            ts(below, above, -0.5, None, ALU.mult)
            then()
            ts(above, below, -1.0, None, ALU.mult)
            then()
            for k, (raw, dst) in enumerate(((f1_raw, tern), (f2_raw, tern_b))):
                flat = raw[:].rearrange("p m d -> p (m d)")
                ts(dst[:], flat, above[:, k:k + 1], None, ALU.is_gt)
                ts(flat, flat, below[:, k:k + 1], None, ALU.is_lt)
                then()
                tt(dst[:], dst[:], flat, ALU.subtract).then_inc(ternary_ready, 1)

            ts(scharr_b[:], scharr_b[:], 0.5, None, ALU.mult)
            then()
            shift = const_cols("shift").rearrange("p (y m) -> p y m", y=3)
            for y_ in range(3):
                for k in range(2):
                    for dx in range(3):
                        w = scharr_b[:, k, y_, dx:dx + 1]
                        if y_ == 0:
                            ts(band[:, k, dx, :], shift[:, 0, :], w, None, ALU.mult)
                        else:
                            stt(band[:, k, dx, :], shift[:, y_, :], w, band[:, k, dx, :], ALU.mult, ALU.add)
                then()
            for k in range(2):
                ts(edge_w[:, 0, k, P - 1:P], scharr_h[:, k, 2:3], 0.5, None, ALU.mult)
                ts(edge_w[:, 1, k, 0:1], scharr_h[:, k, 0:1], 0.5, None, ALU.mult)

            for b in range(B):
                k, f_ = bank_of(SETUP, f"txt{b}")
                ts(txt_rows[:, b, :], k[:, 0:D], txt_scale, None, ALU.mult).then_inc(f_, 1)

            dve.wait_ge(angles_ready, 1)
            ts(ang[:, 4:6, :], ang[:, 4:6, :], HD1 ** -0.5, None, ALU.mult)
            then()
            for g in range(2):
                for s in range(2):
                    h0 = 8 * g + 4 * s
                    q0 = wq1_raw[:, h0:h0 + 4, :, 0]
                    q1 = wq1_raw[:, h0:h0 + 4, :, 1]
                    dst = wq1[:, 4 * g:4 * g + 4, s, :].rearrange("p r (i z) -> p r i z", z=2)
                    sn = ang[:, 4, h0:h0 + 4].unsqueeze(2).to_broadcast([P, 4, HD1 // 2])
                    cs = ang[:, 5, h0:h0 + 4].unsqueeze(2).to_broadcast([P, 4, HD1 // 2])
                    t1 = rot_tmp[:, 0, :].rearrange("p (r i) -> p r i", r=4)
                    t2 = rot_tmp[:, 1, :].rearrange("p (r i) -> p r i", r=4)
                    for z, (m0, m1, op) in enumerate(((cs, sn, ALU.subtract), (sn, cs, ALU.add))):
                        tt(t1, q0, m0, ALU.mult)
                        tt(t2, q1, m1, ALU.mult)
                        then()
                        tt(dst[:, :, :, z], t1, t2, op)
                        then()
            for hh in range(H1):
                stt(alibi[:, hh, :], const_cols("rel"), ang[:, 6, hh:hh + 1], const_cols("mask"), ALU.mult, ALU.add)

            then()
            v.nop().then_inc(setup_dve, 1)
            dve.wait_ge(expert_in_cleared, 16 * (E * CAP // (4 * P)))

            def moments(src):
                for t in range(NT):
                    v.bn_stats(stats[:, t, :], src[:, t, :])
                then()
                for t in range(NT):
                    last = v.bn_aggr(mean_var[:, t, :], stats[:, t, :])
                last.then_inc(var_ready, 1)

            def normalise(dst, src, i, k):
                dve.wait_ge(rstd_ready, 6 * i + k)
                for t in range(NT):
                    last = ts(dst[:, t, :], src[:, t, :], mean_var[:, t, 0:1], rstd[:, t:t + 1],
                              ALU.subtract, ALU.mult)
                return last

            def ln_out(name, i, g=None, b=None):
                k, f_ = bank_of(BODY, f"{name}1", i)
                if g is None:
                    v.tensor_copy(xT[:, 1, :], k[:, 0:S]).then_inc(f_, 1)
                else:
                    ts(xT[:, 1, :], k[:, 0:S], cols[:, g:g + 1], cols[:, b:b + 1], ALU.mult, ALU.add) \
                        .then_inc(f_, 1)

            def add_tokens(dst, names, other, i):
                for name, t0, t1 in ((names[0], 0, 2), (names[1], 2, 3)):
                    k, f_ = bank_of(BODY, name, i)
                    tt(dst[:, t0:t1, :], k[:, 0:D * (t1 - t0)].rearrange("p (t d) -> p t d", d=D),
                       other[:, t0:t1, :], ALU.add).then_inc(f_, 1)
                then()

            def mask_max(layer, n, i):
                s = n % 2
                if n >= 2:
                    dve.wait_ge(exp_done, 2 * HEADS * i + (HEADS * layer + n - 1))
                bias = const_cols("mask") if layer == 0 else alibi[:, pair_head(n), :]
                _, f_a = bank_of(BODY, f"scores{layer}_{n}", i)
                _, f_b = bank_of(BODY, f"scores_b{layer}_{n}", i)
                v.memset(carrier[:, 0:1], 0.0)
                for t in (0, 2, 1):
                    last = v.tensor_tensor_reduce(
                        out=masked[:, s, seg(t)], in0=scores_place(layer, n, t), in1=bias[:, P * (2 - t):S],
                        scale=1.0, scalar=NEG, op0=ALU.add, op1=ALU.max, accum_out=nmax[:, s, t:t + 1])
                    if t != 0:
                        last.then_inc(f_a if t == 2 else f_b, 1)
                then()
                ts(nmax[:, s, :], nmax[:, s, :], -1.0, None, ALU.mult).then_inc(masked_ready, 1)

            def denominators(layer, n, i):
                s = n % 2
                dve.wait_ge(exp_done, 2 * HEADS * i + (HEADS * layer + n + 1))
                if layer == 1:
                    ts(rowsum[:, s, :], rowsum[:, s, :], 1.0, None, ALU.add)
                    then()
                v.reciprocal(rinv[:, s, :], rowsum[:, s, :]).then_inc(rinv_ready, 1)

            def attention(layer, i):
                mask_max(layer, 0, i)
                mask_max(layer, 1, i)
                denominators(layer, 0, i)
                for n in range(HEADS):
                    if n + 2 < HEADS:
                        mask_max(layer, n + 2, i)
                    if n + 1 < HEADS:
                        denominators(layer, n + 1, i)
                    k, f_ = bank_of(BODY, f"probsT_b{layer}_{n}", i)
                    v.tensor_copy(probsT[:, n % 2, 4 * P:6 * P], k[:, 0:2 * P]).then_inc(f_, 1)

            def take_stack(t, g, i):
                k, f_ = bank_of(BODY, f"stack{t}_{g}", i)
                v.tensor_copy((q0T, k0T)[g // 2][:, 4 * (g % 2):4 * (g % 2) + 4, P * t:P * (t + 1)],
                              k[:].rearrange("p (q n) -> p q n", q=4)).then_inc(f_, 1)

            with dve.Fori(0, B) as i:
                dve.wait_ge(img_loaded, 64 * i + 64)
                for c, weight in enumerate(GRAY):
                    pairs = ((gray[:, :, 1:IMG + 1], img[:, c]), (halo_gray[:], halo[:, c]))
                    for g_, x_ in pairs:
                        if c == 0:
                            last = ts(g_, x_, weight, None, ALU.mult)
                        else:
                            last = stt(g_, x_, weight, g_, ALU.mult, ALU.add)
                    if c < 2:
                        then()
                last.then_inc(gray_ready, 1)
                dve.wait_ge(h_stored, 32 * i + 16)
                for hf in range(2):
                    banks.wait_taken(dve, BODY, f"conv{hf}", i)
                    tt(h[:, hf, :], edge[:, hf, 0:IMG], edge[:, hf, IMG:2 * IMG], ALU.add)
                then()
                dve.wait_ge(txt_row_loaded, 16 * i + 16)
                moments(h)
                normalise(x1, h, i, 1)
                then()
                moments(x1)
                normalise(xh, x1, i, 2).then_inc(norm_ready, 1)
                ln_out("ln_attn0_T", i, 1, 3)

                for t in range(NT):
                    k, f_ = bank_of(BODY, f"qk0_{t}", i)
                    tt(qk[:], k[:], bqkv[:, 0:2 * D], ALU.add).then_inc(f_, 1)
                    then()
                    cos = const_cols("cos").rearrange("p (t x d) -> p t x d", t=NT, x=2)[:, t]
                    heads = lambda z: z[:].rearrange("p (x h d) -> p x h d", x=2, h=H0)
                    for x in range(2):
                        last = tt(heads(rot1)[:, x], heads(qk)[:, x],
                                  cos[:, x, :].unsqueeze(1).to_broadcast([P, H0, HD0]), ALU.mult)
                    last.then_inc(qk_ready, 1)
                    k, f_ = bank_of(BODY, f"v0_{t}", i)
                    pv = k[:, 0:D].rearrange("p (a s d) -> p a s d", s=2, d=HD0)
                    bv = bqkv[:, 2 * D:3 * D].rearrange("p (a s d) -> p a s d", s=2, d=HD0)
                    for s in range(2):
                        last = tt(vpad[:, t, :, 48 * s:48 * s + HD0], pv[:, :, s, :], bv[:, :, s, :], ALU.add)
                    last.then_inc(f_, 1)
                    dve.wait_ge(rot2_ready, NT * i + (t + 1))
                    tt(rot1[:], rot1[:], rot2[:], ALU.add).then_inc(roped, 1)
                    dve.wait_ge(stack_hi, NT * i + (t + 1))
                    for x, (dst, slots) in enumerate(((stack_q, (1, 3)), (stack_k, (2, 3)))):
                        o = dst[:, t % 2, :].rearrange("p (h s d) -> p h s d", h=H0, s=4)
                        for s in slots:
                            last = tt(o[:, :, s, :], rot1[:, D * x:D * (x + 1)].rearrange("p (h d) -> p h d", h=H0),
                                      o[:, :, 0, :].bitcast(F32), ALU.subtract)
                    last.then_inc(stack_ready, 1)
                    if t >= 1:
                        take_stack(t - 1, 1, i)
                        take_stack(t - 1, 3, i)
                take_stack(NT - 1, 1, i)
                take_stack(NT - 1, 3, i)

                attention(0, i)
                dve.wait_ge(resid_ready, 3 * i + 1)
                add_tokens(y, ("proj0_a", "proj0_b"), y, i)
                moments(y)
                normalise(xh, y, i, 3).then_inc(norm_ready, 1)
                ln_out("ln_mlp_T", i, 5, 7)
                dve.wait_ge(resid_ready, 3 * i + 2)
                add_tokens(h, ("down0_a", "down0_b"), x1, i)
                moments(h)
                normalise(xh, h, i, 4).then_inc(norm_ready, 1)
                ln_out("ln_ffn_T", i)
                for m in range(1, FM, 2):
                    k, f_ = bank_of(BODY, f"up1_{m}", i)
                    ts(hidT[:, m, :], k[:, 0:S], cols[:, 4 * DC + FM + m:4 * DC + FM + m + 1], 0.0,
                       ALU.add, ALU.max).then_inc(f_, 1)
                dve.wait_ge(resid_ready, 3 * i + 3)
                add_tokens(h, ("down1_a", "down1_b"), x1, i)
                moments(h)
                normalise(xh, h, i, 5).then_inc(norm_ready, 1)
                ln_out("ln_attn1_T", i)
                for t in range(NT):
                    k, f_ = bank_of(BODY, f"v1_{t}", i)
                    v.tensor_copy(v1[:, t, :], k[:, 0:KV1 * HD1]).then_inc(f_, 1)
                for m in range(1, 8, 2):
                    k, f_ = bank_of(BODY, f"q1_{m}", i)
                    v.tensor_copy(q1T[:, m, :], k[:, 0:S]).then_inc(f_, 1)
                attention(1, i)
                add_tokens(h, ("proj1_a", "proj1_b"), h, i)
                moments(h)
                normalise(xh, h, i, 6).then_inc(norm_ready, 1)
                ln_out("ln_moe_T", i)
                k, f_ = bank_of(BODY, "logits", i)
                v.tensor_copy(logits_all[:].rearrange("p (b t) e -> p b (t e)", b=B)[:, i], k[:, 0:NT * E]) \
                    .then_inc(f_, 1)
            v.nop().then_inc(logits_ready, B)

            then()
            dve.wait_ge(h_stored, 32 * B + 16)
            lt = logits_all[:].rearrange("p n e -> p n e")
            by_token = lambda z: z[:].rearrange("p e n -> p n e")
            bc = lambda z: z.unsqueeze(1).to_broadcast([P, E, TILES])
            v.tensor_reduce(kv[:, 0, :], lt, AX.X, ALU.max)
            then()
            tt(pr[:], logits_all[:].rearrange("p n e -> p e n"), bc(kv[:, 0, :]), ALU.subtract) \
                .then_inc(lse_shift, 1)
            dve.wait_ge(lse_exp, 1)
            v.tensor_reduce(kv[:, 0, :], by_token(pr), AX.X, ALU.add)
            then()
            v.reciprocal(kv[:, 1, :], kv[:, 0, :])
            then()
            tt(pr[:], pr[:], bc(kv[:, 1, :]), ALU.mult)
            then()
            tb = const_cols("tiebreak").rearrange("p (e n) -> p e n", e=E)
            for k, (oh, src) in enumerate(((oh1, pr), (oh2, r_b))):
                v.tensor_reduce(kv[:, 2 + k, :], by_token(src), AX.X, ALU.max)
                then()
                tt(r_a[:], src[:], bc(kv[:, 2 + k, :]), ALU.is_equal)
                then()
                tt(r_a[:], r_a[:], tb, ALU.mult)
                then()
                v.tensor_reduce(kv[:, 4, :], by_token(r_a), AX.X, ALU.max)
                then()
                tt(oh[:], tb, bc(kv[:, 4, :]), ALU.is_equal)
                then()
                if k == 0:
                    stt(r_b[:].rearrange("p e n -> p (e n)"), oh1[:].rearrange("p e n -> p (e n)"), -2.0,
                        pr[:].rearrange("p e n -> p (e n)"), ALU.mult, ALU.add)
                    then()
            tt(kv[:, 4, :], kv[:, 2, :], kv[:, 3, :], ALU.add)
            then()
            ts(kv[:, 4, :], kv[:, 4, :], 1e-9, None, ALU.add)
            then()
            v.reciprocal(kv[:, 5, :], kv[:, 4, :])
            then()
            for k in range(2):
                tt(wk[:, k, :], kv[:, 2 + k, :], kv[:, 5, :], ALU.mult)
            then()
            tt(r_a[:], oh1[:], bc(wk[:, 0, :]), ALU.mult)
            tt(r_b[:], oh2[:], bc(wk[:, 1, :]), ALU.mult)
            then()
            tt(gts[:], r_a[:], r_b[:], ALU.add)
            v.memset(thr[:], 0)
            v.memset(bit[:], 1 << (SEARCH - 1))
            then()
            with dve.Fori(0, SEARCH) as r:
                tt(cand[:], thr[:], bit[:].to_broadcast([P, E]), ALU.bitwise_or)
                then()
                tt(selm[:], gts[:], cand[:].bitcast(F32).unsqueeze(2).to_broadcast([P, E, TILES]), ALU.is_ge)
                then()
                v.tensor_reduce(cnt[:], selm[:], AX.X, ALU.add).then_inc(counts_ready, 1)
                dve.wait_ge(counts_taken, r + 1)
                ts(want[:], ps[7][:, 0:E], float(CAP), None, ALU.is_ge)
                then()
                tt(cand[:], want[:], bit[:].to_broadcast([P, E]), ALU.mult)
                then()
                tt(thr[:], thr[:], cand[:], ALU.bitwise_or)
                ts(bit[:], bit[:], 1, None, ALU.logical_shift_right)
                then()
            t_f = thr[:].bitcast(F32).unsqueeze(2).to_broadcast([P, E, TILES])
            flat = lambda z: z[:].rearrange("p e n -> p (e n)")
            tt(selm[:], gts[:], t_f, ALU.is_gt)
            tt(eqm[:], gts[:], t_f, ALU.is_equal)
            ts(r_a[:], gts[:], 0.0, None, ALU.is_gt)
            then()
            tt(eqm[:], eqm[:], r_a[:], ALU.mult)
            then()
            v.tensor_copy(sel_eq[:, 0, :], flat(eqm))
            v.tensor_copy(sel_eq[:, 1, :], flat(selm)).then_inc(sel_ready, 1)

            def ranks(name):
                w = E * TILES
                k, f_ = bank_of(ROUTE, name)
                v.tensor_copy(flat(r_tot), k[:, 0:w])
                then()
                v.tensor_tensor_scan(flat(r_a), const_cols("scan_keep"), flat(r_tot), 0.0, ALU.mult, ALU.add)
                then()
                tt(flat(r_b), flat(r_a), flat(r_tot), ALU.subtract)
                then()
                tt(flat(r_c), k[:, w:2 * w], flat(r_b), ALU.add).then_inc(f_, 1)
                then()

            ranks("prefix")
            v.tensor_reduce(cnt[:], ps[6][:, 0:E * TILES].rearrange("p (e n) -> p e n", e=E), AX.X, ALU.add)
            then()
            ts(want[:], cnt[:], -1.0, float(CAP), ALU.mult, ALU.add)
            then()
            tt(r_c[:], r_c[:], want[:].unsqueeze(2).to_broadcast([P, E, TILES]), ALU.is_lt)
            then()
            tt(r_c[:], r_c[:], eqm[:], ALU.mult)
            then()
            tt(selm[:], selm[:], r_c[:], ALU.add)
            then()
            v.tensor_copy(sel_eq[:, 0, :], flat(selm)).then_inc(sel_ready, 1)
            ranks("slots")
            tt(flat(r_c), flat(r_c), const_cols("expert_row"), ALU.add)
            then()
            for k, oh in enumerate((oh1, oh2)):
                tt(r_a[:], oh[:], r_c[:], ALU.mult)
                tt(r_b[:], oh[:], selm[:], ALU.mult)
                then()
                v.tensor_reduce(pos_f[:, 2 * k, :], by_token(r_a), AX.X, ALU.add)
                v.tensor_reduce(pos_f[:, 2 * k + 1, :], by_token(r_b), AX.X, ALU.add)
                then()
                tt(gath_i[:, k, :], pos_f[:, 2 * k, :], pos_f[:, 2 * k + 1, :], ALU.mult)
                tt(wk[:, k, :], wk[:, k, :], pos_f[:, 2 * k + 1, :], ALU.mult)
                ts(kv[:, 6, :], pos_f[:, 2 * k + 1, :], -1e6, 1e6, ALU.mult, ALU.add)
                then()
                tt(scat_i[:, k, :], pos_f[:, 2 * k, :], kv[:, 6, :], ALU.add)
                then()
            v.nop().then_inc(index_ready, 1)

            with dve.Fori(0, E) as e:
                for hf in range(2):
                    k, f_ = bank_of(EXPERT, f"xT1_{hf}", e)
                    v.tensor_copy(xeT[:, 1, HALF * hf:HALF * (hf + 1)], k[:, 0:HALF]).then_inc(f_, 1)
                for hf in range(2):
                    for m in range(FM):
                        banks.wait_taken(dve, EXPERT, f"gate{hf}_{m}", e)
                        k, f_ = bank_of(EXPERT, f"up{hf}_{m}", e)
                        tt(hT[:, m, HALF * hf:HALF * (hf + 1)], k[:, 0:HALF], sil[:, (FM * hf + m) % 2, :],
                           ALU.mult).then_inc(f_, 1)
                dve.wait_ge(ye_free, 32 * e + 16)
                for j in range(2, 4):
                    k, f_ = bank_of(EXPERT, f"down{j}", e)
                    v.tensor_copy(ye[0:CP, 2 * j:2 * j + 2, :].rearrange("p j d -> p (j d)"), k[0:CP, :]) \
                        .then_inc(f_, 1)

            dve.wait_ge(h_reloaded, 16)
            for k in range(4):
                dve.wait_ge(gathered[k], 16 * 2 * TILES // 4)
                for n in range(TILES // 4 * k, TILES // 4 * (k + 1)):
                    stt(xall[:, n, :], y1[:, n, :], wk[:, 0, n:n + 1], xall[:, n, :], ALU.mult, ALU.add)
                then()
                for n in range(TILES // 4 * k, TILES // 4 * (k + 1)):
                    last = stt(xall[:, n, :], y2[:, n, :], wk[:, 1, n:n + 1], xall[:, n, :], ALU.mult, ALU.add)
                last.then_inc(out_ready, 1)

        @block.gpsimd
        def _(pool):
            g = nc.gpsimd
            then = g.drain
            pool.wait_ge(loaded, 16 * LOADS)
            for bank in range(8):
                g.nop().then_inc(freed[bank], 1)
            g.nop().then_inc(ye_free, 16)

            banks.wait_taken(pool, SETUP, "txt_index")
            for b in range(B):
                g.indirect_dma_start(emb[:, b, :], None, a["L0_txt_embed_weight"],
                                     bass.IndirectOffsetOnAxis(ap=hash_i[:, b:b + 1], axis=0)) \
                    .then_inc(emb_loaded, 16)
            pool.wait_ge(setup_dve, 1)
            pool.wait_ge(h_stored, 16)

            def inverse_deviation(i, k):
                pool.wait_ge(var_ready, 6 * i + k)
                g.tensor_tensor(rstd[:], mean_var[:, :, 1], eps[:], ALU.add)
                then()
                g.tensor_tensor(rstd[:], rstd[:], power[:], ALU.pow).then_inc(rstd_ready, 1)

            def weigh(layer, i):
                for n in range(HEADS):
                    s = n % 2
                    pool.wait_ge(rinv_ready, 2 * HEADS * i + (HEADS * layer + n + 1))
                    g.tensor_tensor(carrier[:, 1 + n % 4:2 + n % 4], power[:, 0:1], eps[:, 0:1], ALU.add)
                    for t in range(NT):
                        last = g.tensor_scalar(probs[:, s, seg(t)], probs[:, s, seg(t)], rinv[:, s, t:t + 1], None,
                                               ALU.mult)
                    last.then_inc(probs_ready, 1)

            def row(z):
                return z.unsqueeze(1).to_broadcast([P, NT, D])

            with pool.Fori(0, B) as i:
                inverse_deviation(i, 1)
                inverse_deviation(i, 2)
                pool.wait_ge(norm_ready, 5 * i + 1)
                g.tensor_tensor(y[:], x1[:], row(bo_r), ALU.add).then_inc(resid_ready, 1)
                for t in range(NT):
                    pool.wait_ge(qk_ready, NT * i + (t + 1))
                    sin = const_cols("sin").rearrange("p (t x d) -> p t x d", t=NT, x=2)[:, t]
                    heads = lambda z: z[:].rearrange("p (x h d) -> p x h d", x=2, h=H0)
                    for x in range(2):
                        for lo_ in (0, 8):
                            last = g.tensor_tensor(
                                heads(rot2)[:, x, :, lo_:lo_ + 8], heads(qk)[:, x, :, 8 - lo_:16 - lo_],
                                sin[:, x, lo_:lo_ + 8].unsqueeze(1).to_broadcast([P, H0, 8]), ALU.mult)
                    last.then_inc(rot2_ready, 1)
                weigh(0, i)
                inverse_deviation(i, 3)
                pool.wait_ge(norm_ready, 5 * i + 2)
                g.tensor_tensor(x1[:], h[:], y[:], ALU.add)
                then()
                g.tensor_tensor(x1[:], x1[:], row(b2_r), ALU.add).then_inc(resid_ready, 1)
                inverse_deviation(i, 4)
                pool.wait_ge(norm_ready, 5 * i + 3)
                g.tensor_tensor(x1[:], h[:], row(bf2_r), ALU.add).then_inc(resid_ready, 1)
                inverse_deviation(i, 5)
                weigh(1, i)
                inverse_deviation(i, 6)

            pool.wait_ge(index_ready, 1)
            pool.wait_ge(xall_loaded, 16)
            for k in range(2):
                for n in range(TILES):
                    g.indirect_dma_start(xg_dram, bass.IndirectOffsetOnAxis(ap=scat_i[:, k, n:n + 1], axis=0),
                                         xall[:, n, :], None, bounds_check=E * CAP - 1, oob_is_err=False) \
                        .then_inc(scattered, 16)
            pool.wait_ge(ye_free, 32 * E + 16)
            for n in range(TILES):
                for k, dst in enumerate((y1, y2)):
                    g.indirect_dma_start(dst[:, n, :], None, yg_dram,
                                         bass.IndirectOffsetOnAxis(ap=gath_i[:, k, n:n + 1], axis=0)) \
                        .then_inc(gathered[n // (TILES // 4)], 16)


_INS = ["x", "x_txt", "L0_tok_scharr", "L0_txt_embed_weight", "L0_txt_proj_weight", "L0_txt_scale",
        "L0_attn_ln1_g", "L0_attn_ln1_b", "L0_attn_Wqkv", "L0_attn_bqkv", "L0_attn_Wo", "L0_attn_bo",
        "L0_attn_ln2_g", "L0_attn_ln2_b", "L0_attn_W1", "L0_attn_b1", "L0_attn_W2", "L0_attn_b2",
        "L0_ffn_W1", "L0_ffn_b1", "L0_ffn_W2", "L0_ffn_b2", "L1_attn_Wq", "L1_attn_Wk", "L1_attn_Wv",
        "L1_attn_Wo", "L1_attn_q_phase_angle", "L1_attn_alibi_log_slopes", "L1_ffn_router_gate",
        "L1_ffn_gate_w", "L1_ffn_up_w", "L1_ffn_down_w"]


def kernel(**inputs):
    import concourse.bacc as bacc
    from concourse.bass_utils import run_bass_kernel_spmd

    nc = bacc.Bacc("TRN2", target_bir_lowering=False, num_devices=1)
    arrays, aps = {}, {}
    for name in _INS:
        x = np.ascontiguousarray(inputs[name])
        if x.ndim == 0:
            x = x.reshape(1)
        arrays[f"in_{name}"] = x
        aps[name] = nc.dram_tensor(f"in_{name}", x.shape, mybir.dt.from_np(x.dtype), kind="ExternalInput").ap()
    arrays["in_const"] = shape_constants()
    const = nc.dram_tensor("in_const", (P, NC_COLS), F32, kind="ExternalInput").ap()
    out = nc.dram_tensor("out_0", (B, S, D), F32, kind="ExternalOutput").ap()
    early_fusion_kernel(nc, aps, const, out)
    r = run_bass_kernel_spmd(nc, [arrays], core_ids=[0])
    return r.results[0]["out_0"]
```

```python
import math
from contextlib import ExitStack

import numpy as np

import concourse.bass as bass
from concourse import mybir

F32 = mybir.dt.float32
F32R = mybir.dt.float32r
I32 = mybir.dt.int32
ALU = mybir.AluOpType
ACT = mybir.ActivationFunctionType
AX = mybir.AxisListType

P = 128
B = 8
IMG = 256
TXT = 128
D = 256
DC = D // P
S = IMG + TXT
NT = S // P
T = B * S
TILES = T // P
VOCAB_MOD = 262143
HASH_CUR, HASH_PREV = 36313, 27191
EMB = 64
EPS = 1e-5
H0, HD0 = 16, 16
H1, HD1, KV1 = 16, 64, 4
FF = 4 * D
FM = FF // P
E = 8
CAP = 960
CP = 120
CT = CAP // CP
HALF = CAP // 2
BIG = 3.0e38
GRAY = (0.2989, 0.587, 0.114)
HEADS = 16
SEG = [0, P, 3 * P]
TWO_PI_HI, TWO_PI_LO = 6.28125, 2 * math.pi - 6.28125
ROUND = 12582912.0

COLS = {}
NC_COLS = 0
for _name, _n in (("ident", P), ("rel", S), ("mask", S), ("cos", NT * 2 * HD0), ("sin", NT * 2 * HD0),
                  ("shift", 3 * P), ("before", P), ("ones", P), ("tiebreak", E * TILES),
                  ("expert_row", E * TILES), ("scan_keep", E * TILES)):
    COLS[_name] = (NC_COLS, NC_COLS + _n)
    NC_COLS += _n


def shape_constants():
    c = np.zeros((P, NC_COLS), np.float32)

    def put(name, value):
        a, b = COLS[name]
        c[:, a:b] = np.asarray(value, np.float32).reshape(P, b - a)

    p = np.arange(P)
    put("ident", np.eye(P))
    rel = (S - P) + p[:, None] - np.arange(S)[None, :]
    put("rel", rel)
    put("mask", np.where(rel < 0, BIG, 0.0))
    inv_freq = (1.0 / np.float32(10000.0) ** (np.arange(0, HD0, 2, dtype=np.float32) / np.float32(HD0))).astype(np.float32)
    pos = (p[:, None] + P * np.arange(NT)[None, :]).astype(np.float32)
    freqs = pos[..., None] * inv_freq
    cos, sin = np.cos(freqs).astype(np.float32), np.sin(freqs).astype(np.float32)
    cos2 = np.concatenate([cos, cos], -1)
    sin2 = np.concatenate([-sin, sin], -1)
    scale = -np.float32(HD0 ** -0.5)
    put("cos", np.stack([cos2 * scale, cos2], 2))
    put("sin", np.stack([sin2 * scale, sin2], 2))
    put("shift", np.stack([np.eye(P, k=1 - dy) for dy in range(3)], 1))
    put("before", np.triu(np.ones((P, P)), 1))
    put("ones", np.ones((P, P)))
    e = np.repeat(np.arange(E), TILES)
    put("tiebreak", np.broadcast_to(E - e, (P, E * TILES)))
    put("expert_row", np.broadcast_to(e * CAP, (P, E * TILES)))
    put("scan_keep", np.broadcast_to(np.tile(np.arange(TILES) > 0, E), (P, E * TILES)))
    return c


def psum_plan():
    setup = [("txt_index", 0, 1), ("projT", 1, 1)]
    setup += [(f"embT{b}", 2 + b % 2, 1) for b in range(B)]
    setup += [(f"txt{b}", 4 + b % 2, 1) for b in range(B)]
    setup += [("gamma", 6, 1)]
    setup += [(f"f1T{g}", (7, 0, 1, 2)[g], 1) for g in range(4)]
    setup += [(f"f2T{g}", (3, 4, 5, 6)[g], 1) for g in range(4)]

    body = [("conv0", 0, 1), ("conv1", 1, 1)]
    body += [(f"ln_attn0_T{c}", 6 + c, 1) for c in range(DC)]
    for t in range(NT):
        body += [(f"qk0_{t}", 2 * t, 1), (f"v0_{t}", 2 * t + 1, 1)]
    for t in range(NT):
        body += [(f"stack{t}_{g}", (6 + 4 * t + g) % 8, 1) for g in range(4)]
    for layer in range(2):
        if layer == 1:
            body += [(f"ln_attn1_T{c}", 6 + c, 1) for c in range(DC)]
            body += [(f"k1_{m}", m, 1) for m in range(2)]
            body += [(f"v1_{t}", 2 + t, 1) for t in range(NT)]
            body += [(f"q1_{m}", (5 + m) % 8, 1) for m in range(8)]
        for n in range(HEADS):
            body += [(f"scores{layer}_{n}", 2 * (n % 2), 1), (f"scores_b{layer}_{n}", 2 * (n % 2) + 1, 1)]
            body += [(f"probsT{layer}_{n}", 4, 1), (f"probsT_b{layer}_{n}", 5, 1)]
        for c in range(2 if layer == 0 else 8):
            body += [(f"out{layer}_{c}", 6 + c % 2, 1), (f"rinvT{layer}_{c}", 7 - c % 2, 1)]
        if layer == 0:
            body += [("proj0_a", 0, 1), ("proj0_b", 1, 1)]
            body += [(f"ln_mlp_T{c}", 6 + c, 1) for c in range(DC)]
            body += [(f"up0_{m}", m % 6, 1) for m in range(FM)]
            body += [("down0_a", 6, 1), ("down0_b", 7, 1)]
            body += [(f"ln_ffn_T{c}", c, 1) for c in range(DC)]
            body += [(f"up1_{m}", 2 + m % 4, 1) for m in range(FM)]
            body += [("down1_a", 6, 1), ("down1_b", 7, 1)]
    body += [("proj1_a", 0, 1), ("proj1_b", 1, 1)]
    body += [(f"ln_moe_T{c}", 2 + c, 1) for c in range(DC)]
    body += [("logits", 4, 1)]

    route = [("prefix", 0, 1), ("slots", 1, 1)]
    route += [(f"xT{c}_{h}", 2 + 2 * h + c, 1) for h in range(2) for c in range(DC)]

    gates = []
    for q in range(2 * FM):
        gates += [(f"gate{q}", 2 * q % 8, 1), (f"up{q}", 2 * q % 8 + 1, 1)]
    rows_t = [(f"xT{c}_{h}", 2 * h + c, 1) for h in range(2) for c in range(DC)]
    down = [(f"down{j}", 4 + j, 1) for j in range(CT // 2)]
    return setup, body, route, gates + rows_t + down, gates + down


class Banks:

    def __init__(self, filled, freed):
        self.filled, self.freed = filled, freed
        self.at = {}
        fills, takes = [0] * 8, [1] * 8
        for k, (section, times) in enumerate(zip(psum_plan(), (1, B, 1, E - 1, 1))):
            f0, t0 = list(fills), list(takes)
            here = {}
            for name, bank, n in section:
                here[name] = (bank, fills[bank] + 1 - f0[bank], takes[bank] - t0[bank])
                fills[bank] += 1
                takes[bank] += n
            per_f = [a - b for a, b in zip(fills, f0)]
            per_t = [a - b for a, b in zip(takes, t0)]
            for name, (bank, f, t) in here.items():
                self.at[(k, name)] = (bank, f0[bank], per_f[bank], f, t0[bank], per_t[bank], t)
            fills = [a + (times - 1) * n for a, n in zip(fills, per_f)]
            takes = [a + (times - 1) * n for a, n in zip(takes, per_t)]

    def bank(self, section, name):
        return self.at[(section, name)][0]

    def wait_free(self, pe, section, name, i=0):
        bank, _, _, _, base, per, n = self.at[(section, name)]
        pe.wait_ge(self.freed[bank], i * per + (base + n))

    def wait_taken(self, eng, section, name, i=0):
        bank, _, _, _, base, per, n = self.at[(section, name)]
        eng.wait_ge(self.freed[bank], i * per + (base + n + 1))

    def wait_filled(self, eng, section, name, i=0):
        bank, base, per, n, _, _, _ = self.at[(section, name)]
        eng.wait_ge(self.filled[bank], i * per + (base + n))


SETUP, BODY, ROUTE, EXPERT, LAST = range(5)
LOADS = 32
GATE_BITS = 30
STEPS = 3
SEARCH = GATE_BITS // 2


def early_fusion_kernel(nc, a, const, out):
    ctx = ExitStack()
    offsets = {"top": nc.sbuf_base + (-nc.sbuf_base) % 64}

    def width(shape):
        return 4 * int(np.prod(shape[1:]))

    def place(name, shape, dt, at):
        assert at + width(shape) <= nc.sbuf_usable_end, (name, at + width(shape))
        return nc.alloc_sbuf_tensor_at(name, shape, dt, offset=at)

    def sb(name, shape, dt=F32):
        at = offsets["top"]
        offsets["top"] = at + (width(shape) + 31) // 32 * 32
        return place(name, shape, dt, at)

    def region(at, *tensors):
        made = []
        for name, shape, dt in tensors:
            made.append(place(name, shape, dt, at))
            at += (width(shape) + 31) // 32 * 32
        return made, at

    with ctx:
        def sem(name):
            return ctx.enter_context(nc.semaphore(name))

        h_dram = nc.dram_tensor("h_rows", [T, D], F32).ap()
        xn_dram = nc.dram_tensor("xn_rows", [T, D], F32).ap()
        xg_dram = nc.dram_tensor("expert_in", [E * CAP, D], F32).ap()
        yg_dram = nc.dram_tensor("expert_out", [E * CAP, D], F32).ap()

        cst = sb("cst", [P, NC_COLS])

        def const_cols(name):
            x, y = COLS[name]
            return cst[:, x:y]

        ident = const_cols("ident")
        logits_all = sb("logits_all", [P, TILES, E])
        small = sb("small", [P, 96])
        loop_start = offsets["top"]
        wqkv = sb("wqkv", [P, DC, 3 * D])
        wo0 = sb("wo0", [P, DC, D])
        w1 = sb("w1", [P, DC, FF])
        w2 = sb("w2", [P, FM, D])
        f1T = sb("f1T", [P, DC, FF])
        f2T = sb("f2T", [P, FM, D])
        wq1 = sb("wq1", [P, 8, 2, HD1])
        wk1 = sb("wk1", [P, KV1 * HD1])
        wv1 = sb("wv1", [P, KV1 * HD1])
        wo1 = sb("wo1", [P, 8, D])
        wr = sb("wr", [P, DC, E])
        rows = sb("rows", [P, 3 * D + 3 * D])
        bqkv, bo_r, b2_r, bf2_r = rows[:, 0:768], rows[:, 768:1024], rows[:, 1024:1280], rows[:, 1280:1536]
        cols = sb("cols", [P, 4 * DC + 2 * FM])
        band = sb("band", [P, 2, 3, P])
        edge_w = sb("edge_w", [3, 2, 2, P])
        alibi = sb("alibi", [P, H1, S])
        img = sb("img", [P, 3, 2, IMG])
        halo = sb("halo", [3, 3, 2, IMG])
        gray = sb("gray", [P, 2, IMG + 2])
        halo_gray = sb("halo_gray", [3, 2, IMG])
        h = sb("h", [P, NT, D])
        x1 = sb("x1", [P, NT, D])
        xh = sb("xh", [P, NT, D])
        y = sb("y", [P, NT, D])
        xT = sb("xT", [P, DC, S])
        stats = sb("stats", [P, NT, 6])
        mean_var = sb("mean_var", [P, NT, 2])
        rstd = sb("rstd", [P, NT])
        eps = sb("eps", [P, NT])
        carrier = sb("carrier", [P, 4])
        power = sb("power", [P, NT])
        vpad = sb("vpad", [P, NT, 8, 64])
        nmax = sb("nmax", [P, 2, NT])
        rowsum = sb("rowsum", [P, HEADS, NT])
        rinv = sb("rinv", [P, 2, NT, P])
        rinvT = sb("rinvT", [P, 2, S])
        attention_start = offsets["top"]
        masked = sb("masked", [P, 2, 2 * S])
        probs = sb("probs", [P, 2, 2 * S])
        probsT = sb("probsT", [P, 2, 2 * S])
        o0T = sb("o0T", [P, DC, S])
        shared = offsets["top"]
        (qk, rot1, rot2), _ = region(
            attention_start, ("qk", [P, 512], F32), ("rot1", [P, 512], F32), ("rot2", [P, 512], F32))
        (stack_q, stack_k, q0T, k0T), end_shared = region(
            shared, ("stack_q", [P, 2, H0 * 64], F32R), ("stack_k", [P, 2, H0 * 64], F32R),
            ("q0T", [P, 8, S], F32R), ("k0T", [P, 8, S], F32R))
        (q1T, k1T, v1, o1T), _ = region(
            shared, ("q1T", [P, 8, S], F32), ("k1T", [P, 2, S], F32),
            ("v1", [P, NT, KV1 * HD1], F32), ("o1T", [P, 8, S], F32))
        (hidT,), _ = region(shared, ("hidT", [P, FM, S], F32))
        (edge,), _ = region(shared, ("edge", [P, 2, 512], F32))

        (emb, embT, proj_raw, projT, txt_rows, hashf, hash_i, wq1_raw, rot_tmp, ang, scharr_b, scharr_h, zeros,
         tok, by0, by1, by2, by3, t_hi, t_lo, f1_raw, f2_raw, tern, tern_b), _ = region(
            attention_start,
            ("emb", [P, B, EMB], F32), ("embT", [EMB, 2, P], F32), ("proj_raw", [P, 2, EMB], F32),
            ("projT", [EMB, D], F32), ("txt_rows", [P, B, D], F32), ("hashf", [B, 4, TXT], F32),
            ("hash_i", [P, B], I32), ("wq1_raw", [P, H1, HD1 // 2, 2], F32), ("rot_tmp", [P, 2, P], F32),
            ("ang", [P, 8, H1], F32), ("scharr_b", [P, 2, 3, 3], F32), ("scharr_h", [3, 2, 3], F32),
            ("zeros", [P, 1024], F32),
            *[(n, [B, 2, TXT + 1], I32) for n in ("tok", "by0", "by1", "by2", "by3", "t_hi", "t_lo")],
            ("f1_raw", [P, FM, D], F32), ("f2_raw", [P, DC, FF], F32),
            ("tern", [P, 2048], F32), ("tern_b", [P, 2048], F32))
        txt_scale = small[:, 8:9]
        absum, above, below, gsum = small[:, 0:2], small[:, 2:4], small[:, 4:6], small[:, 6:8]

        (gate_raw, up_raw, down_raw, gate_w, up_w, down_w, xe, xeT, sil, prod, ye, wk, scat_i, gath_i), end_e = region(
            loop_start, ("gate_raw", [P, DC * FF], F32), ("up_raw", [P, DC * FF], F32),
            ("down_raw", [P, FM * D], F32), ("gate_w", [P, 2, DC, FF], F32R), ("up_w", [P, 2, DC, FF], F32R),
            ("down_w", [P, 2, FM, D], F32R), ("xe", [P, CT, D], F32), ("xeT", [P, 2, DC, CAP], F32R),
            ("sil", [P, 2, HALF], F32), ("prod", [P, 2, HALF], F32), ("ye", [P, CT, D], F32),
            ("wk", [P, 2, TILES], F32), ("scat_i", [P, 2, TILES], I32), ("gath_i", [P, 2, TILES], I32))
        (hT,), _ = region(end_e, ("hT", [P, 2, FM, CAP], F32R))
        (xall,), end_x = region(end_e, ("xall", [P, TILES, D], F32))
        (pr, oh1, oh2, gts, selm, eqm, r_a, r_b, r_c, r_tot), end_r = region(
            end_x, *[(n, [P, E, TILES], F32) for n in (
                "pr", "oh1", "oh2", "gts", "selm", "eqm", "r_a", "r_b", "r_c", "r_tot")])
        (sel_eq, kv, reach, cand, won, thr, step, bits, cnt, want, pos_f), _ = region(
            end_r, ("sel_eq", [P, 2, E * TILES], F32), ("kv", [P, 8, TILES], F32),
            ("reach", [P, STEPS, E, TILES], F32), ("cand", [P, STEPS, E], I32), ("won", [P, STEPS, E], I32),
            ("thr", [P, E], I32), ("step", [P, E], I32), ("bits", [P, STEPS], I32), ("cnt", [P, STEPS * E], F32),
            ("want", [P, E], F32), ("pos_f", [P, 4, TILES], F32))
        (y1, y2), _ = region(loop_start, ("y1", [P, TILES, D], F32), ("y2", [P, TILES, D], F32))

        ps = [ctx.enter_context(nc.psum_tensor(f"bank{k}", [P, 512], F32)) for k in range(8)]

        filled = [sem(f"bank{k}_filled") for k in range(8)]
        freed = [sem(f"bank{k}_freed") for k in range(8)]
        banks = Banks(filled, freed)
        loaded = sem("loaded")
        tokens_loaded = sem("tokens_loaded")
        zeros_ready = sem("zeros_ready")
        cleared = sem("cleared")
        expert_in_cleared = sem("expert_in_cleared")
        hash_ready = sem("hash_ready")
        emb_loaded = sem("emb_loaded")
        abs_ready = sem("abs_ready")
        ternary_ready = sem("ternary_ready")
        reduced = sem("reduced")
        angles_ready = sem("angles_ready")
        setup_dve = sem("setup_dve")
        img_loaded = sem("img_loaded")
        gray_ready = sem("gray_ready")
        txt_row_loaded = sem("txt_row_loaded")
        h_stored = sem("h_stored")
        var_ready = sem("var_ready")
        rstd_ready = sem("rstd_ready")
        norm_ready = sem("norm_ready")
        qk_ready = sem("qk_ready")
        rot2_ready = sem("rot2_ready")
        roped = sem("roped")
        stack_hi = sem("stack_hi")
        stack_ready = sem("stack_ready")
        exp_done = sem("exp_done")
        rinv_ready = sem("rinv_ready")
        resid_ready = sem("resid_ready")
        logits_ready = sem("logits_ready")
        xall_loaded = sem("xall_loaded")
        lse_shift = sem("lse_shift")
        lse_exp = sem("lse_exp")
        counts_ready = sem("counts_ready")
        counts_taken = sem("counts_taken")
        sel_ready = sem("sel_ready")
        index_ready = sem("index_ready")
        scattered = sem("scattered")
        expert_gate_loaded = sem("expert_gate_loaded")
        gate_upper = sem("gate_upper")
        gate_split = sem("gate_split")
        down_upper = sem("down_upper")
        down_split = sem("down_split")
        x_upper = sem("x_upper")
        x_split = sem("x_split")
        h_upper = sem("h_upper")
        h_split = sem("h_split")
        expert_down_loaded = sem("expert_down_loaded")
        xe_loaded = sem("xe_loaded")
        ye_free = sem("ye_free")
        gathered = [sem(f"gathered{k}") for k in range(4)]
        h_reloaded = sem("h_reloaded")
        out_ready = sem("out_ready")
        out_stored = sem("out_stored")

        block = ctx.enter_context(nc.Block())

        def scores_place(layer, n, t):
            if t == 1:
                return ps[banks.bank(BODY, f"scores_b{layer}_{n}")][:, 0:2 * P]
            return ps[banks.bank(BODY, f"scores{layer}_{n}")][:, (0, 0, P)[t]:(P, 0, 4 * P)[t]]

        def pair_head(n):
            m, s = divmod(n, 2)
            return 8 * (m // 4) + 4 * s + m % 4

        def seg(t):
            return slice(SEG[t], SEG[t] + P * (t + 1))

        @block.sync
        def _(sp):
            sp.dma_start(cst[:], const).then_inc(loaded, 16)
            for s in range(2):
                sp.dma_start(tok[:, s, 1:], a["x_txt"]).then_inc(tokens_loaded, 16)
            n = 1
            for dst, src in (
                (f1_raw[:], a["L0_ffn_W1"].rearrange("(m p) d -> p m d", p=P)),
                (f2_raw[:], a["L0_ffn_W2"].rearrange("(c p) f -> p c f", p=P)),
                (proj_raw[:], a["L0_txt_proj_weight"].rearrange("(c p) e -> p c e", p=P)),
                (wq1_raw[:].rearrange("p h i r -> p (h i r)"), a["L1_attn_Wq"]),
                (wqkv[:], a["L0_attn_Wqkv"].rearrange("(c p) n -> p c n", p=P)),
                (wo0[:], a["L0_attn_Wo"].rearrange("(c p) n -> p c n", p=P)),
                (w1[:], a["L0_attn_W1"].rearrange("(c p) n -> p c n", p=P)),
                (w2[:], a["L0_attn_W2"].rearrange("(m p) n -> p m n", p=P)),
                (wk1[:], a["L1_attn_Wk"]),
                (wv1[:], a["L1_attn_Wv"]),
                (bqkv, a["L0_attn_bqkv"].partition_broadcast(P)),
                (bo_r, a["L0_attn_bo"].partition_broadcast(P)),
                (b2_r, a["L0_attn_b2"].partition_broadcast(P)),
                (bf2_r, a["L0_ffn_b2"].partition_broadcast(P)),
                (ang[:, 0, :], a["L1_attn_q_phase_angle"].partition_broadcast(P)),
                (ang[:, 1, :], a["L1_attn_alibi_log_slopes"].partition_broadcast(P)),
                (scharr_b[:].rearrange("p k a b -> p (k a b)"),
                 a["L0_tok_scharr"].rearrange("k o a b -> (k o a b)").partition_broadcast(P)),
                (txt_scale, a["L0_txt_scale"].partition_broadcast(P)),
                (wr[:], a["L1_ffn_router_gate"].rearrange("(c p) e -> p c e", p=P)),
            ):
                sp.dma_start(dst, src).then_inc(loaded, 16)
                n += 1
            wo1_src = a["L1_attn_Wo"].rearrange("(g s r d) n -> g s d r n", g=2, s=2, r=4, d=HD1)
            for g in range(2):
                for s in range(2):
                    sp.dma_start(wo1[64 * s:64 * s + 64, 4 * g:4 * g + 4, :], wo1_src[g, s]).then_inc(loaded, 16)
                    n += 1
            for k, name in enumerate(("L0_attn_ln1_g", "L0_attn_ln1_b", "L0_attn_ln2_g", "L0_attn_ln2_b")):
                sp.dma_start(cols[:, DC * k:DC * k + DC], a[name].rearrange("(c p) -> p c", p=P),
                             allow_slow_non_contiguous=True).then_inc(loaded, 16)
                n += 1
            for k, name in enumerate(("L0_attn_b1", "L0_ffn_b1")):
                sp.dma_start(cols[:, 4 * DC + FM * k:4 * DC + FM * k + FM], a[name].rearrange("(m p) -> p m", p=P),
                             allow_slow_non_contiguous=True).then_inc(loaded, 16)
                n += 1
            for k in range(2):
                sp.dma_start(scharr_h[:, k, :], a["L0_tok_scharr"][k, 0].rearrange("a b -> b a"),
                             allow_slow_non_contiguous=True).then_inc(loaded, 16)
                n += 1
            assert n == LOADS
            sp.wait_ge(zeros_ready, 1)
            for r in range(E * CAP // (4 * P)):
                sp.dma_start(xg_dram[4 * P * r:4 * P * (r + 1)].rearrange("(p q) d -> p (q d)", q=4), zeros[:]) \
                    .then_inc(expert_in_cleared, 16)
            banks.wait_taken(sp, SETUP, f"txt{B - 1}")
            sp.dma_start(h_dram.rearrange("(b t p) d -> p b t d", b=B, t=NT)[:, :, NT - 1, :],
                         txt_rows[:]).then_inc(h_stored, 16)
            sp.wait_ge(h_stored, 16)

            def load_image(i):
                x = a["x"]
                sp.dma_start(img[:].rearrange("p c h w -> p (c h) w"),
                             x[i].rearrange("c (h p) w -> p (c h) w", p=P)).then_inc(img_loaded, 16)
                for dx in range(3):
                    lo, hi = max(0, 1 - dx), min(IMG, IMG + 1 - dx)
                    sp.dma_start(halo[dx:dx + 1, :, :, lo:hi],
                                 x[i, :, P - 1:P + 1, lo + dx - 1:hi + dx - 1].unsqueeze(0)).then_inc(img_loaded, 16)

            def load_text(i):
                sp.dma_start(h[:, NT - 1, :], h_dram.rearrange("(b t p) d -> b t p d", b=B, t=NT)[i, NT - 1]) \
                    .then_inc(txt_row_loaded, 16)

            def store_tokens(i):
                sp.wait_ge(norm_ready, 5 * i + 5)
                sp.dma_start(xn_dram.rearrange("(b t p) d -> b p t d", b=B, t=NT)[i], xh[:]).then_inc(h_stored, 16)
                sp.dma_start(h_dram.rearrange("(b t p) d -> b p t d", b=B, t=NT)[i], h[:]).then_inc(h_stored, 16)
                sp.wait_ge(h_stored, 32 * i + 48)

            sp.wait_ge(cleared, 1)
            load_image(0)
            load_text(0)
            with sp.Fori(0, B - 1) as i:
                sp.wait_ge(gray_ready, i + 1)
                load_image(i + 1)
                store_tokens(i)
                load_text(i + 1)
            store_tokens(B - 1)

            sp.wait_ge(logits_ready, B)
            sp.dma_start(xall[:], xn_dram.rearrange("(n p) d -> p n d", p=P)).then_inc(xall_loaded, 16)

            def load_gate_up(e):
                sp.dma_start(gate_raw[:].rearrange("p (c n) -> p c n", c=DC), a["L1_ffn_gate_w"][e].rearrange("(c p) n -> p c n", p=P)) \
                    .then_inc(expert_gate_loaded, 16)
                sp.dma_start(up_raw[:].rearrange("p (c n) -> p c n", c=DC), a["L1_ffn_up_w"][e].rearrange("(c p) n -> p c n", p=P)) \
                    .then_inc(expert_gate_loaded, 16)

            def load_down(e):
                sp.dma_start(down_raw[:].rearrange("p (m n) -> p m n", m=FM), a["L1_ffn_down_w"][e].rearrange("(m p) n -> p m n", p=P)) \
                    .then_inc(expert_down_loaded, 16)

            def load_rows(e):
                sp.dma_start(xe[0:CP], xg_dram.rearrange("(e j p) d -> e p j d", e=E, j=CT)[e]).then_inc(xe_loaded, 16)

            yg_view = yg_dram.rearrange("(e s j p) d -> e s p j d", e=E, s=2, p=CP)

            def store_rows(section, e, i):
                for s in range(2):
                    banks.wait_taken(sp, section, f"down{2 * s + 1}", i)
                    sp.dma_start(yg_view[e, s], ye[0:CP, CT // 2 * s:CT // 2 * (s + 1)]).then_inc(ye_free, 16)

            load_gate_up(0)
            load_down(0)
            sp.wait_ge(scattered, 16 * 2 * TILES)
            load_rows(0)
            with sp.Fori(0, E - 1) as e:
                sp.wait_ge(gate_split, e + 1)
                load_gate_up(e + 1)
                sp.wait_ge(x_split, 2 * DC * e + 2 * DC)
                load_rows(e + 1)
                sp.wait_ge(down_split, e + 1)
                load_down(e + 1)
                store_rows(EXPERT, e, e)
            store_rows(LAST, E - 1, 0)

            sp.wait_ge(ye_free, 32 * E + 16)
            sp.dma_start(xall[:], h_dram.rearrange("(n p) d -> p n d", p=P)).then_inc(h_reloaded, 16)
            for k in range(4):
                sp.wait_ge(out_ready, k + 1)
                n0, n1 = TILES // 4 * k, TILES // 4 * (k + 1)
                sp.dma_start(out.rearrange("b (t p) d -> p (b t) d", p=P)[:, n0:n1], xall[:, n0:n1]) \
                    .then_inc(out_stored, 16)
            sp.wait_ge(out_stored, 64)

        @block.tensor
        def _(pe):
            mm, tr = nc.tensor.matmul, nc.tensor.transpose

            def transposed(section, prefix, src, i, what, count):
                pe.wait_ge(what, count)
                for c in range(DC):
                    name = f"{prefix}{c}"
                    banks.wait_free(pe, section, name, i)
                    bank = banks.bank(section, name)
                    for t in range(NT):
                        last = tr(ps[bank][:, P * t:P * (t + 1)], src[:, t, P * c:P * (c + 1)], ident)
                    last.then_inc(filled[bank], 1)

            pe.wait_ge(loaded, 16 * LOADS)
            banks.wait_free(pe, SETUP, "projT")
            for c in range(DC):
                last = tr(ps[1][0:EMB, P * c:P * (c + 1)], proj_raw[:, c, :], ident)
            last.then_inc(filled[1], 1)
            pe.wait_ge(hash_ready, 1)
            banks.wait_free(pe, SETUP, "txt_index")
            tr(ps[0][:, 0:B], hashf[:, 0, :], ident[0:B, 0:B]).then_inc(filled[0], 1)
            pe.wait_ge(abs_ready, 1)
            banks.wait_free(pe, SETUP, "gamma")
            mm(ps[6][:, 0:2], const_cols("ones"), absum, start=True, stop=True).then_inc(filled[6], 1)
            pe.wait_ge(emb_loaded, 16 * B)
            banks.wait_taken(pe, SETUP, "projT")
            for b in range(B + 1):
                if b < B:
                    k = banks.bank(SETUP, f"embT{b}")
                    banks.wait_free(pe, SETUP, f"embT{b}")
                    tr(ps[k][0:EMB, 0:P], emb[:, b, :], ident).then_inc(filled[k], 1)
                if b > 0:
                    k = banks.bank(SETUP, f"txt{b - 1}")
                    banks.wait_free(pe, SETUP, f"txt{b - 1}")
                    banks.wait_taken(pe, SETUP, f"embT{b - 1}")
                    mm(ps[k][:, 0:D], embT[:, (b - 1) % 2, :], projT[:], start=True, stop=True) \
                        .then_inc(filled[k], 1)
            for g in range(4):
                k = banks.bank(SETUP, f"f1T{g}")
                banks.wait_free(pe, SETUP, f"f1T{g}")
                pe.wait_ge(ternary_ready, 1)
                c, m0 = divmod(g, 2)
                for q in range(4):
                    m = 4 * m0 + q
                    last = tr(ps[k][:, P * q:P * (q + 1)], tern[:, D * m + P * c:D * m + P * (c + 1)], ident)
                last.then_inc(filled[k], 1)
            for g in range(4):
                k = banks.bank(SETUP, f"f2T{g}")
                banks.wait_free(pe, SETUP, f"f2T{g}")
                pe.wait_ge(ternary_ready, 2)
                for q in range(4):
                    m, c = 2 * g + q // 2, q % 2
                    last = tr(ps[k][:, P * q:P * (q + 1)], tern_b[:, FF * c + P * m:FF * c + P * (m + 1)], ident)
                last.then_inc(filled[k], 1)
            pe.wait_ge(setup_dve, 1)
            banks.wait_taken(pe, SETUP, "f2T3")

            def head_scores(layer, n, i):
                ba, bb = banks.bank(BODY, f"scores{layer}_{n}"), banks.bank(BODY, f"scores_b{layer}_{n}")
                banks.wait_free(pe, BODY, f"scores{layer}_{n}", i)
                banks.wait_free(pe, BODY, f"scores_b{layer}_{n}", i)
                for t in (0, 2, 1):
                    if layer == 0:
                        half = slice(64 * (n % 2), 64 * (n % 2) + 64)
                        q, k = q0T[half, n // 2, :], k0T[half, n // 2, :]
                    else:
                        half = slice(64 * (n % 2), 64 * (n % 2) + 64)
                        q, k = q1T[half, n // 2, :], k1T[half, n // 8, :]
                    last = mm(scores_place(layer, n, t), q[:, P * t:P * (t + 1)], k[:, 0:P * (t + 1)],
                              start=True, stop=True)
                    if t == 2:
                        last.then_inc(filled[ba], 1)
                last.then_inc(filled[bb], 1)

            def probs_transposed(layer, n, i):
                ba, bb = banks.bank(BODY, f"probsT{layer}_{n}"), banks.bank(BODY, f"probsT_b{layer}_{n}")
                pe.wait_ge(exp_done, 2 * HEADS * i + (HEADS * layer + n + 1))
                p = probs[:, n % 2, :]
                banks.wait_free(pe, BODY, f"probsT{layer}_{n}", i)
                for t in range(NT):
                    last = tr(ps[ba][:, P * t:P * (t + 1)], p[:, SEG[t]:SEG[t] + P], ident)
                last.then_inc(filled[ba], 1)
                banks.wait_free(pe, BODY, f"probsT_b{layer}_{n}", i)
                for q, (t, j) in enumerate(((1, 1), (2, 1), (2, 2))):
                    last = tr(ps[bb][:, P * q:P * (q + 1)], p[:, SEG[t] + P * j:SEG[t] + P * (j + 1)], ident)
                last.then_inc(filled[bb], 1)

            def denominators_transposed(layer, c, i):
                bank = banks.bank(BODY, f"rinvT{layer}_{c}")
                pe.wait_ge(rinv_ready, 10 * i + (2 * layer + c + 1))
                banks.wait_free(pe, BODY, f"rinvT{layer}_{c}", i)
                for t in range(NT):
                    last = tr(ps[bank][:, P * t:P * (t + 1)], rinv[:, c % 2, t, :], ident)
                last.then_inc(filled[bank], 1)

            def head_out(layer, n, i):
                c = n // 8 if layer == 0 else n // 2
                bank = banks.bank(BODY, f"out{layer}_{c}")
                if n == c * (8 if layer == 0 else 2):
                    banks.wait_free(pe, BODY, f"out{layer}_{c}", i)
                banks.wait_taken(pe, BODY, f"probsT{layer}_{n}", i)
                banks.wait_taken(pe, BODY, f"probsT_b{layer}_{n}", i)
                pT = probsT[:, n % 2, :]
                for j, cols_j in enumerate((slice(0, 3 * P), slice(3 * P, 5 * P), slice(5 * P, 6 * P))):
                    if layer == 0:
                        rows_o = slice(32 * (n % 8 // 2), 32 * (n % 8 // 2) + 32)
                        v = vpad[:, j, n // 2, 32 * (n % 2):32 * (n % 2) + 32]
                        first, final = n % 2 == 0 and j == 0, n % 2 == 1 and j == 2
                    else:
                        rows_o = slice(64 * (n % 2), 64 * (n % 2) + 64)
                        kv = pair_head(n) // 4
                        v = v1[:, j, HD1 * kv:HD1 * (kv + 1)]
                        first, final = j == 0, j == 2
                    last = mm(ps[bank][rows_o, P * j:S], v, pT[:, cols_j], start=first, stop=final)
                if n % (8 if layer == 0 else 2) == (7 if layer == 0 else 1):
                    last.then_inc(filled[bank], 1)

            def attention(layer, i):
                head_scores(layer, 0, i)
                head_scores(layer, 1, i)
                for n in range(HEADS):
                    if n + 2 < HEADS:
                        head_scores(layer, n + 2, i)
                    probs_transposed(layer, n, i)
                    if n >= 1:
                        head_out(layer, n - 1, i)
                    per = 8 if layer == 0 else 2
                    if n % per == per - 1:
                        denominators_transposed(layer, n // per, i)
                head_out(layer, HEADS - 1, i)

            def token_major(names, i, lhs, weights, chunks, n_cols=D):
                for t in range(NT):
                    name = names[t // 2]
                    bank = banks.bank(BODY, name)
                    if t != 1:
                        banks.wait_free(pe, BODY, name, i)
                    o = ps[bank][:, n_cols * (t % 2):n_cols * (t % 2) + n_cols]
                    for m in range(chunks):
                        last = mm(o, lhs[:, m, P * t:P * (t + 1)], weights[:, m, :],
                                  start=(m == 0), stop=(m == chunks - 1))
                    if t != 0:
                        last.then_inc(filled[bank], 1)

            def xT_wait(i, name):
                for c in range(DC):
                    banks.wait_taken(pe, BODY, f"{name}{c}", i)

            def up(names, i, w):
                for m in range(FM):
                    bank = banks.bank(BODY, names + str(m))
                    banks.wait_free(pe, BODY, names + str(m), i)
                    for c in range(DC):
                        last = mm(ps[bank][:, 0:S], w[:, c, P * m:P * (m + 1)], xT[:, c, :],
                                  start=(c == 0), stop=(c == DC - 1))
                    last.then_inc(filled[bank], 1)

            with pe.Fori(0, B) as i:
                pe.wait_ge(gray_ready, i + 1)
                for hf in range(2):
                    name = f"conv{hf}"
                    bank = banks.bank(BODY, name)
                    banks.wait_free(pe, BODY, name, i)
                    for k in range(2):
                        o = ps[bank][:, IMG * k:IMG * (k + 1)]
                        for dx in range(3):
                            mm(o, band[:, k, dx, :], gray[:, hf, dx:dx + IMG], start=(dx == 0), stop=False)
                        last = mm(o, edge_w[:, hf, k, :], halo_gray[:, 1 - hf, :], start=False, stop=True)
                    last.then_inc(filled[bank], 1)

                transposed(BODY, "ln_attn0_T", xh, i, norm_ready, 5 * i + 1)
                xT_wait(i, "ln_attn0_T")
                for t in range(NT):
                    bq, bv = banks.bank(BODY, f"qk0_{t}"), banks.bank(BODY, f"v0_{t}")
                    banks.wait_free(pe, BODY, f"qk0_{t}", i)
                    for c in range(DC):
                        last = mm(ps[bq][:], xT[:, c, P * t:P * (t + 1)], wqkv[:, c, 0:2 * D],
                                  start=(c == 0), stop=(c == DC - 1))
                    last.then_inc(filled[bq], 1)
                    banks.wait_free(pe, BODY, f"v0_{t}", i)
                    for c in range(DC):
                        last = mm(ps[bv][:, 0:D], xT[:, c, P * t:P * (t + 1)], wqkv[:, c, 2 * D:3 * D],
                                  start=(c == 0), stop=(c == DC - 1))
                    last.then_inc(filled[bv], 1)
                for t in range(NT):
                    pe.wait_ge(stack_ready, NT * i + (t + 1))
                    for g in range(4):
                        bank = banks.bank(BODY, f"stack{t}_{g}")
                        banks.wait_free(pe, BODY, f"stack{t}_{g}", i)
                        src = (stack_q, stack_k)[g // 2][:, t % 2, :].bitcast(F32)
                        for q in range(4):
                            hp = 4 * (g % 2) + q
                            last = tr(ps[bank][:, P * q:P * (q + 1)], src[:, P * hp:P * (hp + 1)], ident)
                        last.then_inc(filled[bank], 1)
                for g in (2, 3):
                    banks.wait_taken(pe, BODY, f"stack{NT - 1}_{g}", i)
                attention(0, i)
                banks.wait_taken(pe, BODY, "out0_1", i)
                token_major(("proj0_a", "proj0_b"), i, o0T, wo0, DC)

                transposed(BODY, "ln_mlp_T", xh, i, norm_ready, 5 * i + 2)
                xT_wait(i, "ln_mlp_T")
                up("up0_", i, w1)
                banks.wait_taken(pe, BODY, f"up0_{FM - 1}", i)
                token_major(("down0_a", "down0_b"), i, hidT, w2, FM)

                transposed(BODY, "ln_ffn_T", xh, i, norm_ready, 5 * i + 3)
                xT_wait(i, "ln_ffn_T")
                up("up1_", i, f1T)
                for m in (FM - 2, FM - 1):
                    banks.wait_taken(pe, BODY, f"up1_{m}", i)
                token_major(("down1_a", "down1_b"), i, hidT, f2T, FM)

                transposed(BODY, "ln_attn1_T", xh, i, norm_ready, 5 * i + 4)
                xT_wait(i, "ln_attn1_T")
                for m in range(2):
                    bank = banks.bank(BODY, f"k1_{m}")
                    banks.wait_free(pe, BODY, f"k1_{m}", i)
                    mm(ps[bank][:, 0:S], wk1[:, P * m:P * (m + 1)], xT[:, 1, :], start=True, stop=True) \
                        .then_inc(filled[bank], 1)
                for t in range(NT):
                    bank = banks.bank(BODY, f"v1_{t}")
                    banks.wait_free(pe, BODY, f"v1_{t}", i)
                    mm(ps[bank][:, 0:KV1 * HD1], xT[:, 0, P * t:P * (t + 1)], wv1[:], start=True, stop=True) \
                        .then_inc(filled[bank], 1)
                for m in range(8):
                    bank = banks.bank(BODY, f"q1_{m}")
                    banks.wait_free(pe, BODY, f"q1_{m}", i)
                    mm(ps[bank][:, 0:S], wq1[:, m].rearrange("p s d -> p (s d)"), xT[:, 1, :],
                       start=True, stop=True).then_inc(filled[bank], 1)
                for m in (6, 7):
                    banks.wait_taken(pe, BODY, f"q1_{m}", i)
                attention(1, i)
                banks.wait_taken(pe, BODY, "out1_7", i)
                token_major(("proj1_a", "proj1_b"), i, o1T, wo1, 8)

                transposed(BODY, "ln_moe_T", xh, i, norm_ready, 5 * i + 5)
                xT_wait(i, "ln_moe_T")
                bank = banks.bank(BODY, "logits")
                banks.wait_free(pe, BODY, "logits", i)
                for t in range(NT):
                    for c in range(DC):
                        last = mm(ps[bank][:, E * t:E * (t + 1)], xT[:, c, P * t:P * (t + 1)], wr[:, c, :],
                                  start=(c == 0), stop=(c == DC - 1))
                last.then_inc(filled[bank], 1)

            with pe.Fori(0, SEARCH) as r:
                pe.wait_ge(counts_ready, r + 1)
                mm(ps[7][:, 0:STEPS * E], const_cols("ones"), cnt[:], start=True, stop=True) \
                    .then_inc(counts_taken, 1)
            for k, name in enumerate(("prefix", "slots")):
                bank = banks.bank(ROUTE, name)
                pe.wait_ge(sel_ready, k + 1)
                banks.wait_free(pe, ROUTE, name)
                w = E * TILES
                if k == 0:
                    mm(ps[6][:, 0:w], const_cols("ones"), sel_eq[:, 1, :], start=True, stop=True)
                mm(ps[bank][:, 0:w], const_cols("ones"), sel_eq[:, 0, :], start=True, stop=True)
                mm(ps[bank][:, w:2 * w], const_cols("before"), sel_eq[:, 0, :], start=True, stop=True) \
                    .then_inc(filled[bank], 1)

            PASSES = ((0, 0), (0, 1), (1, 0))

            def rows_transposed(section, e, i):
                pe.wait_ge(xe_loaded, 16 * e + 16)
                for hf in range(2):
                    for c in range(DC):
                        bank = banks.bank(section, f"xT{c}_{hf}")
                        banks.wait_free(pe, section, f"xT{c}_{hf}", i)
                        for q in range(4):
                            last = tr(ps[bank][:, CP * q:CP * (q + 1)], xe[0:CP, 4 * hf + q, P * c:P * (c + 1)],
                                      ident[0:CP, 0:CP])
                        last.then_inc(filled[bank], 1)

            def gates(section, e, i):
                pe.wait_ge(gate_split, e + 1)
                for q in range(2 * FM):
                    hf, m = divmod(q, FM)
                    if m == 0:
                        pe.wait_ge(x_split, 2 * DC * e + DC * (hf + 1))
                    for name, w in ((f"gate{q}", gate_w), (f"up{q}", up_w)):
                        bank = banks.bank(section, name)
                        banks.wait_free(pe, section, name, i)
                        for c in range(DC):
                            for k, (wp, xp) in enumerate(PASSES):
                                last = mm(ps[bank][:, 0:HALF], w[:, wp, c, P * m:P * (m + 1)],
                                          xeT[:, xp, c, HALF * hf:HALF * (hf + 1)],
                                          start=(c == 0 and k == 0), stop=(c == DC - 1 and k == 2))
                        last.then_inc(filled[bank], 1)

            def down(section, e, i):
                pe.wait_ge(down_split, e + 1)
                for j in range(CT):
                    bank = banks.bank(section, f"down{j // 2}")
                    if j % 2 == 0:
                        banks.wait_free(pe, section, f"down{j // 2}", i)
                    if j in (0, 4):
                        pe.wait_ge(h_split, 2 * FM * e + FM * (j // 4 + 1))
                    for m in range(FM):
                        for k, (hp, wp) in enumerate(PASSES):
                            last = mm(ps[bank][:, D * (j % 2):D * (j % 2) + D][0:CP], hT[:, hp, m, CP * j:CP * (j + 1)],
                                      down_w[:, wp, m, :], start=(m == 0 and k == 0), stop=(m == FM - 1 and k == 2))
                    if j % 2 == 1:
                        last.then_inc(filled[bank], 1)

            rows_transposed(ROUTE, 0, 0)
            with pe.Fori(0, E - 1) as e:
                gates(EXPERT, e, e)
                rows_transposed(EXPERT, e + 1, e)
                down(EXPERT, e, e)
            gates(LAST, E - 1, 0)
            down(LAST, E - 1, 0)

        @block.scalar
        def _(act):
            f = nc.scalar.activation

            def take(section, name, i, dst, fn, width, rows_p=P, **kw):
                banks.wait_filled(act, section, name, i)
                bank = banks.bank(section, name)
                src = ps[bank][0:rows_p, 0:width]
                if fn is None:
                    ins = nc.scalar.copy(dst, src)
                else:
                    ins = f(dst, src, fn, **kw)
                ins.then_inc(freed[bank], 1)

            act.wait_ge(loaded, 16 * LOADS)
            take(SETUP, "projT", 0, projT[:], None, D, EMB)
            for b in range(B):
                if b >= 2:
                    banks.wait_filled(act, SETUP, f"txt{b - 2}")
                take(SETUP, f"embT{b}", 0, embT[:, b % 2, :], None, P, EMB)
            act.wait_ge(reduced, 1)
            f(ang[:, 4, :], ang[:, 2, :], ACT.Sin)
            f(ang[:, 5, :], ang[:, 3, :], ACT.Sin)
            f(ang[:, 6, :], ang[:, 1, :], ACT.Exp).then_inc(angles_ready, 1)
            for g in range(4):
                c, m0 = divmod(g, 2)
                take(SETUP, f"f1T{g}", 0, f1T[:, c, 4 * P * m0:4 * P * (m0 + 1)], None, 4 * P)
            for g in range(4):
                take(SETUP, f"f2T{g}", 0, f2T[:, 2 * g:2 * g + 2, :].rearrange("p m n -> p (m n)"), None, 4 * P)
            act.wait_ge(setup_dve, 1)
            act.wait_ge(h_stored, 16)
            act.wait_ge(expert_in_cleared, 16 * (E * CAP // (4 * P)))

            def ln_out(name, i, g=None, b=None):
                if g is None:
                    take(BODY, f"{name}0", i, xT[:, 0, :], None, S)
                else:
                    take(BODY, f"{name}0", i, xT[:, 0, :], ACT.Identity, S,
                         bias=cols[:, b:b + 1], scale=cols[:, g:g + 1])

            def take_stack(t, g, i):
                name = f"stack{t}_{g}"
                banks.wait_filled(act, BODY, name, i)
                bank = banks.bank(BODY, name)
                nc.scalar.copy((q0T, k0T)[g // 2][:, 4 * (g % 2):4 * (g % 2) + 4, P * t:P * (t + 1)],
                               ps[bank][:].rearrange("p (q n) -> p q n", q=4)).then_inc(freed[bank], 1)

            def exps(layer, n, i):
                banks.wait_taken(act, BODY, f"scores_b{layer}_{n}", i)
                s = n % 2
                if n >= 2:
                    banks.wait_filled(act, BODY, f"probsT_b{layer}_{n - 2}", i)
                for t in range(NT):
                    last = f(probs[:, s, seg(t)], masked[:, s, seg(t)], ACT.Exp, bias=nmax[:, s, t:t + 1],
                             scale=-1.0, accum_out=rowsum[:, n, t:t + 1])
                last.then_inc(exp_done, 1)

            def attention(layer, i):
                per = 8 if layer == 0 else 2
                exps(layer, 0, i)
                for n in range(HEADS):
                    if n + 1 < HEADS:
                        exps(layer, n + 1, i)
                    if n % per == 0 and n > 0:
                        take_denominators(layer, n // per - 1, i)
                    take(BODY, f"probsT{layer}_{n}", i, probsT[:, n % 2, 0:3 * P], None, 3 * P)
                take_denominators(layer, HEADS // per - 1, i)

            def take_denominators(layer, c, i):
                if c >= 2:
                    banks.wait_taken(act, BODY, f"out{layer}_{c - 2}", i)
                take(BODY, f"rinvT{layer}_{c}", i, rinvT[:, c % 2, :], None, S)

            with act.Fori(0, B) as i:
                for hf in range(2):
                    take(BODY, f"conv{hf}", i, edge[:, hf, :], ACT.Abs, 2 * IMG)
                ln_out("ln_attn0_T", i, 0, 2)
                for t in range(NT):
                    act.wait_ge(roped, NT * i + (t + 1))
                    if t >= 2:
                        banks.wait_filled(act, BODY, f"stack{t - 2}_3", i)
                    for x, (dst, slots) in enumerate(((stack_q, (0, 2)), (stack_k, (0, 1)))):
                        o = dst[:, t % 2, :].rearrange("p (h s d) -> p h s d", h=H0, s=4)
                        for s in slots:
                            last = nc.scalar.copy(o[:, :, s, :], rot1[:, D * x:D * (x + 1)].rearrange(
                                "p (h d) -> p h d", h=H0))
                    last.then_inc(stack_hi, 1)
                    if t >= 1:
                        take_stack(t - 1, 0, i)
                        take_stack(t - 1, 2, i)
                take_stack(NT - 1, 0, i)
                take_stack(NT - 1, 2, i)
                attention(0, i)
                ln_out("ln_mlp_T", i, 4, 6)
                for m in range(FM):
                    take(BODY, f"up0_{m}", i, hidT[:, m, :], ACT.Gelu, S,
                         bias=cols[:, 4 * DC + m:4 * DC + m + 1])
                ln_out("ln_ffn_T", i)
                for m in range(0, FM, 2):
                    take(BODY, f"up1_{m}", i, hidT[:, m, :], ACT.Relu, S,
                         bias=cols[:, 4 * DC + FM + m:4 * DC + FM + m + 1])
                ln_out("ln_attn1_T", i)
                for m in range(2):
                    take(BODY, f"k1_{m}", i, k1T[:, m, :], None, S)
                for m in range(0, 8, 2):
                    take(BODY, f"q1_{m}", i, q1T[:, m, :], None, S)
                attention(1, i)
                ln_out("ln_moe_T", i)

            act.wait_ge(lse_shift, 1)
            f(pr[:], pr[:], ACT.Exp).then_inc(lse_exp, 1)

            def gate_uppers(e):
                act.wait_ge(expert_gate_loaded, 32 * e + 32)
                nc.scalar.copy(gate_w[:, 0].rearrange("p c n -> p (c n)"), gate_raw[:])
                nc.scalar.copy(up_w[:, 0].rearrange("p c n -> p (c n)"), up_raw[:]).then_inc(gate_upper, 1)

            def down_uppers(e):
                act.wait_ge(expert_down_loaded, 16 * e + 16)
                nc.scalar.copy(down_w[:, 0].rearrange("p m n -> p (m n)"), down_raw[:]).then_inc(down_upper, 1)

            def x_uppers(section, i):
                for hf in range(2):
                    for c in range(DC):
                        banks.wait_filled(act, section, f"xT{c}_{hf}", i)
                        bank = banks.bank(section, f"xT{c}_{hf}")
                        nc.scalar.copy(xeT[:, 0, c, HALF * hf:HALF * (hf + 1)], ps[bank][:, 0:HALF]) \
                            .then_inc(x_upper, 1)

            def hidden(section, i):
                for q in range(2 * FM + 1):
                    if q < 2 * FM:
                        if q >= 2:
                            banks.wait_taken(act, section, f"up{q - 2}", i)
                        take(section, f"gate{q}", i, sil[:, q % 2, :], ACT.Silu, HALF)
                    if q >= 1:
                        hf, m = divmod(q - 1, FM)
                        banks.wait_taken(act, section, f"up{q - 1}", i)
                        nc.scalar.copy(hT[:, 0, m, HALF * hf:HALF * (hf + 1)], prod[:, (q - 1) % 2, :]) \
                            .then_inc(h_upper, 1)

            def take_down(section, e, i):
                act.wait_ge(ye_free, 32 * e + 16)
                for j in range(2, 4):
                    take(section, f"down{j}", i, ye[0:CP, 2 * j:2 * j + 2, :].rearrange("p j d -> p (j d)"),
                         None, 2 * D, CP)

            act.wait_ge(index_ready, 1)
            gate_uppers(0)
            x_uppers(ROUTE, 0)
            with act.Fori(0, E - 1) as e:
                down_uppers(e)
                hidden(EXPERT, e)
                gate_uppers(e + 1)
                x_uppers(EXPERT, e)
                take_down(EXPERT, e, e)
            down_uppers(E - 1)
            hidden(LAST, 0)
            take_down(LAST, E - 1, 0)

        @block.vector
        def _(dve):
            v = nc.vector
            ts, tt, stt = v.tensor_scalar, v.tensor_tensor, v.scalar_tensor_tensor
            then = v.drain

            def bank_of(section, name, i=0):
                banks.wait_filled(dve, section, name, i)
                k = banks.bank(section, name)
                return ps[k], freed[k]

            v.memset(tok[:, :, 0:1], 0)
            v.memset(zeros[:], 0.0).then_inc(zeros_ready, 1)
            v.memset(halo[:], 0.0)
            v.memset(gray[:], 0.0)
            v.memset(edge_w[:], 0.0)
            v.memset(vpad[:], 0.0)
            v.memset(eps[:], EPS)
            v.memset(power[:], -0.5).then_inc(cleared, 1)
            dve.wait_ge(tokens_loaded, 32)
            then()
            for dst, shift in ((by0, 0), (by1, 8), (by2, 16), (by3, 24)):
                ts(dst[:], tok[:], shift, 255, ALU.logical_shift_right, ALU.bitwise_and)
            then()
            for s, factor in ((0, HASH_CUR), (1, HASH_PREV)):
                for dst in (by0, by1, by2, by3):
                    ts(dst[:, s, :], dst[:, s, :], float(factor), None, ALU.mult)
            then()
            ts(t_lo[:], by1[:], 255, 8, ALU.bitwise_and, ALU.logical_shift_left)
            ts(t_hi[:], by0[:], 0xFFFF, None, ALU.bitwise_and)
            then()
            tt(t_lo[:], t_lo[:], t_hi[:], ALU.add)
            ts(by1[:], by1[:], 8, None, ALU.logical_shift_right)
            ts(by2[:], by2[:], 0xFFFF, None, ALU.bitwise_and)
            ts(by3[:], by3[:], 255, 8, ALU.bitwise_and, ALU.logical_shift_left)
            then()
            ts(t_hi[:], by0[:], 16, None, ALU.logical_shift_right)
            then()
            ts(by0[:], t_lo[:], 16, None, ALU.logical_shift_right)
            for part in (by1, by2, by3, by0):
                then()
                tt(t_hi[:], t_hi[:], part[:], ALU.add)
            then()
            for limb in (t_hi, t_lo):
                ts(limb[:], limb[:], 0xFFFF, None, ALU.bitwise_and)
            then()
            hi, lo = by0[:, 0, 0:TXT], by1[:, 0, 0:TXT]
            tt(hi, t_hi[:, 0, 1:TXT + 1], t_hi[:, 1, 0:TXT], ALU.bitwise_xor)
            tt(lo, t_lo[:, 0, 1:TXT + 1], t_lo[:, 1, 0:TXT], ALU.bitwise_xor)
            then()
            ts(by2[:, 0, 0:TXT], hi, 3, 16, ALU.bitwise_and, ALU.logical_shift_left)
            ts(by3[:, 0, 0:TXT], hi, 2, None, ALU.logical_shift_right)
            ts(by2[:, 1, 0:TXT], hi, 15, None, ALU.logical_shift_right)
            then()
            tt(by2[:, 0, 0:TXT], by2[:, 0, 0:TXT], lo, ALU.bitwise_or)
            then()
            tt(hashf[:, 0, :], by2[:, 0, 0:TXT], by3[:, 0, 0:TXT], ALU.add)
            then()
            stt(hashf[:, 1, :], by2[:, 1, 0:TXT], -16384.0, hashf[:, 0, :], ALU.mult, ALU.add)
            then()
            ts(hashf[:, 2, :], hashf[:, 1, :], 0.0, float(VOCAB_MOD), ALU.is_lt, ALU.mult)
            then()
            tt(hashf[:, 3, :], hashf[:, 1, :], hashf[:, 2, :], ALU.add)
            then()
            ts(hashf[:, 2, :], hashf[:, 3, :], float(VOCAB_MOD), -float(VOCAB_MOD), ALU.is_ge, ALU.mult)
            then()
            tt(hashf[:, 0, :], hashf[:, 3, :], hashf[:, 2, :], ALU.add)
            then()
            v.memset(hashf[:, 0, 0:1], float(VOCAB_MOD)).then_inc(hash_ready, 1)
            k, f_ = bank_of(SETUP, "txt_index")
            v.tensor_copy(hash_i[:], k[:, 0:B]).then_inc(f_, 1)

            dve.wait_ge(loaded, 16 * LOADS)
            v.tensor_reduce(absum[:, 0:1], f1_raw[:].rearrange("p m d -> p (m d)"), AX.X, ALU.add,
                            apply_absolute_value=True)
            v.tensor_reduce(absum[:, 1:2], f2_raw[:].rearrange("p m d -> p (m d)"), AX.X, ALU.add,
                            apply_absolute_value=True).then_inc(abs_ready, 1)
            ts(ang[:, 7, :], ang[:, 0, :], 1.0 / (2 * math.pi), ROUND, ALU.mult, ALU.add)
            then()
            ts(ang[:, 7, :], ang[:, 7, :], ROUND, None, ALU.subtract)
            then()
            stt(ang[:, 2, :], ang[:, 7, :], -TWO_PI_HI, ang[:, 0, :], ALU.mult, ALU.add)
            then()
            stt(ang[:, 2, :], ang[:, 7, :], -TWO_PI_LO, ang[:, 2, :], ALU.mult, ALU.add)
            then()
            ts(ang[:, 2, :], ang[:, 2, :], -math.pi, math.pi, ALU.max, ALU.min)
            then()
            ts(ang[:, 3, :], ang[:, 2, :], -1.0, None, ALU.mult)
            then()
            tt(ang[:, 3, :], ang[:, 3, :], ang[:, 2, :], ALU.max)
            then()
            ts(ang[:, 3, :], ang[:, 3, :], -1.0, math.pi / 2, ALU.mult, ALU.add).then_inc(reduced, 1)
            k, f_ = bank_of(SETUP, "gamma")
            ts(above, k[:, 0:2], 1.0 / (D * FF), EPS, ALU.mult, ALU.add).then_inc(f_, 1)
            then()
            ts(below, above, -0.5, None, ALU.mult)
            then()
            ts(above, below, -1.0, None, ALU.mult)
            then()
            for k, (raw, dst) in enumerate(((f1_raw, tern), (f2_raw, tern_b))):
                flat = raw[:].rearrange("p m d -> p (m d)")
                ts(dst[:], flat, above[:, k:k + 1], None, ALU.is_gt)
                ts(flat, flat, below[:, k:k + 1], None, ALU.is_lt)
                then()
                tt(dst[:], dst[:], flat, ALU.subtract).then_inc(ternary_ready, 1)

            ts(scharr_b[:], scharr_b[:], 0.5, None, ALU.mult)
            then()
            shift = const_cols("shift").rearrange("p (y m) -> p y m", y=3)
            for y_ in range(3):
                for k in range(2):
                    for dx in range(3):
                        w = scharr_b[:, k, y_, dx:dx + 1]
                        if y_ == 0:
                            ts(band[:, k, dx, :], shift[:, 0, :], w, None, ALU.mult)
                        else:
                            stt(band[:, k, dx, :], shift[:, y_, :], w, band[:, k, dx, :], ALU.mult, ALU.add)
                then()
            for k in range(2):
                ts(edge_w[:, 0, k, P - 1:P], scharr_h[:, k, 2:3], 0.5, None, ALU.mult)
                ts(edge_w[:, 1, k, 0:1], scharr_h[:, k, 0:1], 0.5, None, ALU.mult)

            for b in range(B):
                k, f_ = bank_of(SETUP, f"txt{b}")
                ts(txt_rows[:, b, :], k[:, 0:D], txt_scale, None, ALU.mult).then_inc(f_, 1)

            dve.wait_ge(angles_ready, 1)
            ts(ang[:, 4:6, :], ang[:, 4:6, :], -HD1 ** -0.5, None, ALU.mult)
            then()
            for g in range(2):
                for s in range(2):
                    h0 = 8 * g + 4 * s
                    q0 = wq1_raw[:, h0:h0 + 4, :, 0]
                    q1 = wq1_raw[:, h0:h0 + 4, :, 1]
                    dst = wq1[:, 4 * g:4 * g + 4, s, :].rearrange("p r (i z) -> p r i z", z=2)
                    sn = ang[:, 4, h0:h0 + 4].unsqueeze(2).to_broadcast([P, 4, HD1 // 2])
                    cs = ang[:, 5, h0:h0 + 4].unsqueeze(2).to_broadcast([P, 4, HD1 // 2])
                    t1 = rot_tmp[:, 0, :].rearrange("p (r i) -> p r i", r=4)
                    t2 = rot_tmp[:, 1, :].rearrange("p (r i) -> p r i", r=4)
                    for z, (m0, m1, op) in enumerate(((cs, sn, ALU.subtract), (sn, cs, ALU.add))):
                        tt(t1, q0, m0, ALU.mult)
                        tt(t2, q1, m1, ALU.mult)
                        then()
                        tt(dst[:, :, :, z], t1, t2, op)
                        then()
            ts(ang[:, 6, :], ang[:, 6, :], -1.0, None, ALU.mult)
            then()
            for hh in range(H1):
                stt(alibi[:, hh, :], const_cols("rel"), ang[:, 6, hh:hh + 1], const_cols("mask"), ALU.mult, ALU.add)

            then()
            v.nop().then_inc(setup_dve, 1)
            dve.wait_ge(expert_in_cleared, 16 * (E * CAP // (4 * P)))

            def moments(src):
                for t in range(NT):
                    v.bn_stats(stats[:, t, :], src[:, t, :])
                then()
                for t in range(NT):
                    last = v.bn_aggr(mean_var[:, t, :], stats[:, t, :])
                last.then_inc(var_ready, 1)

            def normalise(dst, src, i, k):
                dve.wait_ge(rstd_ready, 6 * i + k)
                for t in range(NT):
                    last = ts(dst[:, t, :], src[:, t, :], mean_var[:, t, 0:1], rstd[:, t:t + 1],
                              ALU.subtract, ALU.mult)
                return last

            def ln_out(name, i, g=None, b=None):
                k, f_ = bank_of(BODY, f"{name}1", i)
                if g is None:
                    v.tensor_copy(xT[:, 1, :], k[:, 0:S]).then_inc(f_, 1)
                else:
                    ts(xT[:, 1, :], k[:, 0:S], cols[:, g:g + 1], cols[:, b:b + 1], ALU.mult, ALU.add) \
                        .then_inc(f_, 1)

            def add_tokens(dst, names, other, i):
                for name, t0, t1 in ((names[0], 0, 2), (names[1], 2, 3)):
                    k, f_ = bank_of(BODY, name, i)
                    tt(dst[:, t0:t1, :], k[:, 0:D * (t1 - t0)].rearrange("p (t d) -> p t d", d=D),
                       other[:, t0:t1, :], ALU.add).then_inc(f_, 1)
                then()

            def mask_max(layer, n, i):
                s = n % 2
                if n >= 2:
                    dve.wait_ge(exp_done, 2 * HEADS * i + (HEADS * layer + n - 1))
                bias = const_cols("mask") if layer == 0 else alibi[:, pair_head(n), :]
                _, f_a = bank_of(BODY, f"scores{layer}_{n}", i)
                _, f_b = bank_of(BODY, f"scores_b{layer}_{n}", i)
                v.memset(carrier[:, n % 4:n % 4 + 1], 0.0)
                for t in (0, 2, 1):
                    last = v.tensor_tensor_reduce(
                        out=masked[:, s, seg(t)], in0=scores_place(layer, n, t), in1=bias[:, P * (2 - t):S],
                        scale=1.0, scalar=BIG, op0=ALU.add, op1=ALU.min, accum_out=nmax[:, s, t:t + 1])
                    if t != 0:
                        last.then_inc(f_a if t == 2 else f_b, 1)

            def denominators(layer, c, i):
                per = 8 if layer == 0 else 2
                sums = rowsum[:, per * c:per * (c + 1), :]
                dve.wait_ge(exp_done, 2 * HEADS * i + (HEADS * layer + per * (c + 1)))
                if layer == 1:
                    ts(sums, sums, 1.0, None, ALU.add)
                    then()
                if c >= 2:
                    banks.wait_filled(dve, BODY, f"rinvT{layer}_{c - 2}", i)
                v.reciprocal(sums, sums)
                then()
                v.tensor_copy(rinv[:, c % 2].rearrange("p t (h d) -> p t h d", h=per),
                              sums.rearrange("p h t -> p t h").unsqueeze(3).to_broadcast([P, NT, per, P // per])) \
                    .then_inc(rinv_ready, 1)

            def weigh(layer, c, i):
                banks.wait_taken(dve, BODY, f"rinvT{layer}_{c}", i)
                k, f_ = bank_of(BODY, f"out{layer}_{c}", i)
                tt((o0T, o1T)[layer][:, c, :], k[:, 0:S], rinvT[:, c % 2, :], ALU.mult).then_inc(f_, 1)

            def attention(layer, i):
                per = 8 if layer == 0 else 2
                mask_max(layer, 0, i)
                mask_max(layer, 1, i)
                for n in range(HEADS):
                    if n + 2 < HEADS:
                        mask_max(layer, n + 2, i)
                    if n > per and n % per == 1:
                        weigh(layer, n // per - 1, i)
                    if n % per == per - 1:
                        denominators(layer, n // per, i)
                    k, f_ = bank_of(BODY, f"probsT_b{layer}_{n}", i)
                    v.tensor_copy(probsT[:, n % 2, 3 * P:6 * P], k[:, 0:3 * P]).then_inc(f_, 1)
                weigh(layer, HEADS // per - 1, i)

            def take_stack(t, g, i):
                k, f_ = bank_of(BODY, f"stack{t}_{g}", i)
                v.tensor_copy((q0T, k0T)[g // 2][:, 4 * (g % 2):4 * (g % 2) + 4, P * t:P * (t + 1)],
                              k[:].rearrange("p (q n) -> p q n", q=4)).then_inc(f_, 1)

            with dve.Fori(0, B) as i:
                dve.wait_ge(img_loaded, 64 * i + 64)
                for c, weight in enumerate(GRAY):
                    pairs = ((gray[:, :, 1:IMG + 1], img[:, c]), (halo_gray[:], halo[:, c]))
                    for g_, x_ in pairs:
                        if c == 0:
                            last = ts(g_, x_, weight, None, ALU.mult)
                        else:
                            last = stt(g_, x_, weight, g_, ALU.mult, ALU.add)
                    if c < 2:
                        then()
                last.then_inc(gray_ready, 1)
                dve.wait_ge(h_stored, 32 * i + 16)
                for hf in range(2):
                    banks.wait_taken(dve, BODY, f"conv{hf}", i)
                    tt(h[:, hf, :], edge[:, hf, 0:IMG], edge[:, hf, IMG:2 * IMG], ALU.add)
                then()
                dve.wait_ge(txt_row_loaded, 16 * i + 16)
                moments(h)
                normalise(x1, h, i, 1)
                then()
                moments(x1)
                normalise(xh, x1, i, 2).then_inc(norm_ready, 1)
                ln_out("ln_attn0_T", i, 1, 3)

                for t in range(NT):
                    k, f_ = bank_of(BODY, f"qk0_{t}", i)
                    tt(qk[:], k[:], bqkv[:, 0:2 * D], ALU.add).then_inc(f_, 1)
                    then()
                    cos = const_cols("cos").rearrange("p (t x d) -> p t x d", t=NT, x=2)[:, t]
                    heads = lambda z: z[:].rearrange("p (x h d) -> p x h d", x=2, h=H0)
                    for x in range(2):
                        last = tt(heads(rot1)[:, x], heads(qk)[:, x],
                                  cos[:, x, :].unsqueeze(1).to_broadcast([P, H0, HD0]), ALU.mult)
                    last.then_inc(qk_ready, 1)
                    k, f_ = bank_of(BODY, f"v0_{t}", i)
                    pv = k[:, 0:D].rearrange("p (a s d) -> p a s d", s=2, d=HD0)
                    bv = bqkv[:, 2 * D:3 * D].rearrange("p (a s d) -> p a s d", s=2, d=HD0)
                    for s in range(2):
                        last = tt(vpad[:, t, :, 48 * s:48 * s + HD0], pv[:, :, s, :], bv[:, :, s, :], ALU.add)
                    last.then_inc(f_, 1)
                    dve.wait_ge(rot2_ready, NT * i + (t + 1))
                    tt(rot1[:], rot1[:], rot2[:], ALU.add).then_inc(roped, 1)
                    dve.wait_ge(stack_hi, NT * i + (t + 1))
                    for x, (dst, slots) in enumerate(((stack_q, (1, 3)), (stack_k, (2, 3)))):
                        o = dst[:, t % 2, :].rearrange("p (h s d) -> p h s d", h=H0, s=4)
                        for s in slots:
                            last = tt(o[:, :, s, :], rot1[:, D * x:D * (x + 1)].rearrange("p (h d) -> p h d", h=H0),
                                      o[:, :, 0, :].bitcast(F32), ALU.subtract)
                    last.then_inc(stack_ready, 1)
                    if t >= 1:
                        take_stack(t - 1, 1, i)
                        take_stack(t - 1, 3, i)
                take_stack(NT - 1, 1, i)
                take_stack(NT - 1, 3, i)

                attention(0, i)
                dve.wait_ge(resid_ready, 3 * i + 1)
                add_tokens(y, ("proj0_a", "proj0_b"), y, i)
                moments(y)
                normalise(xh, y, i, 3).then_inc(norm_ready, 1)
                ln_out("ln_mlp_T", i, 5, 7)
                dve.wait_ge(resid_ready, 3 * i + 2)
                add_tokens(h, ("down0_a", "down0_b"), x1, i)
                moments(h)
                normalise(xh, h, i, 4).then_inc(norm_ready, 1)
                ln_out("ln_ffn_T", i)
                for m in range(1, FM, 2):
                    k, f_ = bank_of(BODY, f"up1_{m}", i)
                    ts(hidT[:, m, :], k[:, 0:S], cols[:, 4 * DC + FM + m:4 * DC + FM + m + 1], 0.0,
                       ALU.add, ALU.max).then_inc(f_, 1)
                dve.wait_ge(resid_ready, 3 * i + 3)
                add_tokens(h, ("down1_a", "down1_b"), x1, i)
                moments(h)
                normalise(xh, h, i, 5).then_inc(norm_ready, 1)
                ln_out("ln_attn1_T", i)
                for t in range(NT):
                    k, f_ = bank_of(BODY, f"v1_{t}", i)
                    v.tensor_copy(v1[:, t, :], k[:, 0:KV1 * HD1]).then_inc(f_, 1)
                for m in range(1, 8, 2):
                    k, f_ = bank_of(BODY, f"q1_{m}", i)
                    v.tensor_copy(q1T[:, m, :], k[:, 0:S]).then_inc(f_, 1)
                attention(1, i)
                add_tokens(h, ("proj1_a", "proj1_b"), h, i)
                moments(h)
                normalise(xh, h, i, 6).then_inc(norm_ready, 1)
                ln_out("ln_moe_T", i)
                k, f_ = bank_of(BODY, "logits", i)
                v.tensor_copy(logits_all[:].rearrange("p (b t) e -> p b (t e)", b=B)[:, i], k[:, 0:NT * E]) \
                    .then_inc(f_, 1)
            v.nop().then_inc(logits_ready, B)

            then()
            dve.wait_ge(h_stored, 32 * B + 16)
            lt = logits_all[:].rearrange("p n e -> p n e")
            by_token = lambda z: z[:].rearrange("p e n -> p n e")
            bc = lambda z: z.unsqueeze(1).to_broadcast([P, E, TILES])
            v.tensor_reduce(kv[:, 0, :], lt, AX.X, ALU.max)
            then()
            tt(pr[:], logits_all[:].rearrange("p n e -> p e n"), bc(kv[:, 0, :]), ALU.subtract) \
                .then_inc(lse_shift, 1)
            dve.wait_ge(lse_exp, 1)
            v.tensor_reduce(kv[:, 0, :], by_token(pr), AX.X, ALU.add)
            then()
            v.reciprocal(kv[:, 1, :], kv[:, 0, :])
            then()
            tt(pr[:], pr[:], bc(kv[:, 1, :]), ALU.mult)
            then()
            tb = const_cols("tiebreak").rearrange("p (e n) -> p e n", e=E)
            for k, (oh, src) in enumerate(((oh1, pr), (oh2, r_b))):
                v.tensor_reduce(kv[:, 2 + k, :], by_token(src), AX.X, ALU.max)
                then()
                tt(r_a[:], src[:], bc(kv[:, 2 + k, :]), ALU.is_equal)
                then()
                tt(r_a[:], r_a[:], tb, ALU.mult)
                then()
                v.tensor_reduce(kv[:, 4, :], by_token(r_a), AX.X, ALU.max)
                then()
                tt(oh[:], tb, bc(kv[:, 4, :]), ALU.is_equal)
                then()
                if k == 0:
                    stt(r_b[:].rearrange("p e n -> p (e n)"), oh1[:].rearrange("p e n -> p (e n)"), -2.0,
                        pr[:].rearrange("p e n -> p (e n)"), ALU.mult, ALU.add)
                    then()
            tt(kv[:, 4, :], kv[:, 2, :], kv[:, 3, :], ALU.add)
            then()
            ts(kv[:, 4, :], kv[:, 4, :], 1e-9, None, ALU.add)
            then()
            v.reciprocal(kv[:, 5, :], kv[:, 4, :])
            then()
            for k in range(2):
                tt(wk[:, k, :], kv[:, 2 + k, :], kv[:, 5, :], ALU.mult)
            then()
            tt(r_a[:], oh1[:], bc(wk[:, 0, :]), ALU.mult)
            tt(r_b[:], oh2[:], bc(wk[:, 1, :]), ALU.mult)
            then()
            tt(gts[:], r_a[:], r_b[:], ALU.add)
            v.memset(thr[:], 0)
            for k in range(STEPS):
                v.memset(bits[:, k:k + 1], (k + 1) << (GATE_BITS - 2))
            then()
            by_expert = lambda z: z.unsqueeze(2).to_broadcast([P, STEPS, E])
            with dve.Fori(0, SEARCH) as r:
                tt(cand[:], thr[:].unsqueeze(1).to_broadcast([P, STEPS, E]), by_expert(bits[:]), ALU.bitwise_or)
                then()
                tt(reach[:], gts[:].unsqueeze(1).to_broadcast([P, STEPS, E, TILES]),
                   cand[:].bitcast(F32).unsqueeze(3).to_broadcast([P, STEPS, E, TILES]), ALU.is_ge)
                then()
                v.tensor_reduce(cnt[:].rearrange("p (k e) -> p k e", e=E), reach[:], AX.X, ALU.add) \
                    .then_inc(counts_ready, 1)
                dve.wait_ge(counts_taken, r + 1)
                stt(won[:], ps[7][:, 0:STEPS * E].rearrange("p (k e) -> p k e", e=E), float(CAP), by_expert(bits[:]),
                    ALU.is_ge, ALU.mult)
                then()
                v.tensor_reduce(step[:], won[:].rearrange("p k e -> p e k"), AX.X, ALU.max)
                ts(bits[:], bits[:], 2, None, ALU.logical_shift_right)
                then()
                tt(thr[:], thr[:], step[:], ALU.bitwise_or)
                then()
            t_f = thr[:].bitcast(F32).unsqueeze(2).to_broadcast([P, E, TILES])
            flat = lambda z: z[:].rearrange("p e n -> p (e n)")
            tt(selm[:], gts[:], t_f, ALU.is_gt)
            tt(eqm[:], gts[:], t_f, ALU.is_equal)
            ts(r_a[:], gts[:], 0.0, None, ALU.is_gt)
            then()
            tt(eqm[:], eqm[:], r_a[:], ALU.mult)
            then()
            v.tensor_copy(sel_eq[:, 0, :], flat(eqm))
            v.tensor_copy(sel_eq[:, 1, :], flat(selm)).then_inc(sel_ready, 1)

            def ranks(name):
                w = E * TILES
                k, f_ = bank_of(ROUTE, name)
                v.tensor_copy(flat(r_tot), k[:, 0:w])
                then()
                v.tensor_tensor_scan(flat(r_a), const_cols("scan_keep"), flat(r_tot), 0.0, ALU.mult, ALU.add)
                then()
                tt(flat(r_b), flat(r_a), flat(r_tot), ALU.subtract)
                then()
                tt(flat(r_c), k[:, w:2 * w], flat(r_b), ALU.add).then_inc(f_, 1)
                then()

            ranks("prefix")
            v.tensor_reduce(cnt[:, 0:E], ps[6][:, 0:E * TILES].rearrange("p (e n) -> p e n", e=E), AX.X, ALU.add)
            then()
            ts(want[:], cnt[:, 0:E], -1.0, float(CAP), ALU.mult, ALU.add)
            then()
            tt(r_c[:], r_c[:], want[:].unsqueeze(2).to_broadcast([P, E, TILES]), ALU.is_lt)
            then()
            tt(r_c[:], r_c[:], eqm[:], ALU.mult)
            then()
            tt(selm[:], selm[:], r_c[:], ALU.add)
            then()
            v.tensor_copy(sel_eq[:, 0, :], flat(selm)).then_inc(sel_ready, 1)
            ranks("slots")
            tt(flat(r_c), flat(r_c), const_cols("expert_row"), ALU.add)
            then()
            for k, oh in enumerate((oh1, oh2)):
                tt(r_a[:], oh[:], r_c[:], ALU.mult)
                tt(r_b[:], oh[:], selm[:], ALU.mult)
                then()
                v.tensor_reduce(pos_f[:, 2 * k, :], by_token(r_a), AX.X, ALU.add)
                v.tensor_reduce(pos_f[:, 2 * k + 1, :], by_token(r_b), AX.X, ALU.add)
                then()
                tt(gath_i[:, k, :], pos_f[:, 2 * k, :], pos_f[:, 2 * k + 1, :], ALU.mult)
                tt(wk[:, k, :], wk[:, k, :], pos_f[:, 2 * k + 1, :], ALU.mult)
                ts(kv[:, 6, :], pos_f[:, 2 * k + 1, :], -1e6, 1e6, ALU.mult, ALU.add)
                then()
                tt(scat_i[:, k, :], pos_f[:, 2 * k, :], kv[:, 6, :], ALU.add)
                then()
            v.nop().then_inc(index_ready, 1)

            def gate_lowers(e):
                dve.wait_ge(gate_upper, e + 1)
                for w, raw in ((gate_w, gate_raw), (up_w, up_raw)):
                    last = tt(w[:, 1].rearrange("p c n -> p (c n)"), raw[:],
                              w[:, 0].rearrange("p c n -> p (c n)").bitcast(F32), ALU.subtract)
                last.then_inc(gate_split, 1)

            def down_lowers(e):
                dve.wait_ge(down_upper, e + 1)
                tt(down_w[:, 1].rearrange("p m n -> p (m n)"), down_raw[:],
                   down_w[:, 0].rearrange("p m n -> p (m n)").bitcast(F32), ALU.subtract).then_inc(down_split, 1)

            def x_lowers(section, e, i):
                for hf in range(2):
                    for c in range(DC):
                        dve.wait_ge(x_upper, 2 * DC * e + (DC * hf + c + 1))
                        bank = banks.bank(section, f"xT{c}_{hf}")
                        half = slice(HALF * hf, HALF * (hf + 1))
                        tt(xeT[:, 1, c, half], ps[bank][:, 0:HALF], xeT[:, 0, c, half].bitcast(F32), ALU.subtract) \
                            .then_inc(freed[bank], 1)
                then()
                v.nop().then_inc(x_split, 2 * DC)

            def hidden(section, e, i):
                for q in range(2 * FM + 1):
                    if q < 2 * FM:
                        banks.wait_taken(dve, section, f"gate{q}", i)
                        k, f_ = bank_of(section, f"up{q}", i)
                        tt(prod[:, q % 2, :], k[:, 0:HALF], sil[:, q % 2, :], ALU.mult).then_inc(f_, 1)
                    if q >= 1:
                        hf, m = divmod(q - 1, FM)
                        dve.wait_ge(h_upper, 2 * FM * e + q)
                        half = slice(HALF * hf, HALF * (hf + 1))
                        tt(hT[:, 1, m, half], prod[:, (q - 1) % 2, :], hT[:, 0, m, half].bitcast(F32),
                           ALU.subtract).then_inc(h_split, 1)
                        then()

            def take_down(section, e, i):
                dve.wait_ge(ye_free, 32 * e + 16)
                for j in range(0, 2):
                    k, f_ = bank_of(section, f"down{j}", i)
                    v.tensor_copy(ye[0:CP, 2 * j:2 * j + 2, :].rearrange("p j d -> p (j d)"), k[0:CP, :]) \
                        .then_inc(f_, 1)

            gate_lowers(0)
            x_lowers(ROUTE, 0, 0)
            with dve.Fori(0, E - 1) as e:
                down_lowers(e)
                hidden(EXPERT, e, e)
                gate_lowers(e + 1)
                x_lowers(EXPERT, e + 1, e)
                take_down(EXPERT, e, e)
            down_lowers(E - 1)
            hidden(LAST, E - 1, 0)
            take_down(LAST, E - 1, 0)

            dve.wait_ge(h_reloaded, 16)
            for k in range(4):
                dve.wait_ge(gathered[k], 16 * 2 * TILES // 4)
                for n in range(TILES // 4 * k, TILES // 4 * (k + 1)):
                    stt(xall[:, n, :], y1[:, n, :], wk[:, 0, n:n + 1], xall[:, n, :], ALU.mult, ALU.add)
                then()
                for n in range(TILES // 4 * k, TILES // 4 * (k + 1)):
                    last = stt(xall[:, n, :], y2[:, n, :], wk[:, 1, n:n + 1], xall[:, n, :], ALU.mult, ALU.add)
                last.then_inc(out_ready, 1)

        @block.gpsimd
        def _(pool):
            g = nc.gpsimd
            then = g.drain
            pool.wait_ge(loaded, 16 * LOADS)
            for bank in range(8):
                g.nop().then_inc(freed[bank], 1)
            g.nop().then_inc(ye_free, 16)

            banks.wait_taken(pool, SETUP, "txt_index")
            for b in range(B):
                g.indirect_dma_start(emb[:, b, :], None, a["L0_txt_embed_weight"],
                                     bass.IndirectOffsetOnAxis(ap=hash_i[:, b:b + 1], axis=0)) \
                    .then_inc(emb_loaded, 16)
            pool.wait_ge(setup_dve, 1)
            pool.wait_ge(h_stored, 16)

            def inverse_deviation(i, k):
                pool.wait_ge(var_ready, 6 * i + k)
                g.tensor_tensor(rstd[:], mean_var[:, :, 1], eps[:], ALU.add)
                then()
                g.tensor_tensor(rstd[:], rstd[:], power[:], ALU.pow).then_inc(rstd_ready, 1)

            def row(z):
                return z.unsqueeze(1).to_broadcast([P, NT, D])

            with pool.Fori(0, B) as i:
                inverse_deviation(i, 1)
                inverse_deviation(i, 2)
                pool.wait_ge(norm_ready, 5 * i + 1)
                g.tensor_tensor(y[:], x1[:], row(bo_r), ALU.add).then_inc(resid_ready, 1)
                for t in range(NT):
                    pool.wait_ge(qk_ready, NT * i + (t + 1))
                    sin = const_cols("sin").rearrange("p (t x d) -> p t x d", t=NT, x=2)[:, t]
                    heads = lambda z: z[:].rearrange("p (x h d) -> p x h d", x=2, h=H0)
                    for x in range(2):
                        for lo_ in (0, 8):
                            last = g.tensor_tensor(
                                heads(rot2)[:, x, :, lo_:lo_ + 8], heads(qk)[:, x, :, 8 - lo_:16 - lo_],
                                sin[:, x, lo_:lo_ + 8].unsqueeze(1).to_broadcast([P, H0, 8]), ALU.mult)
                    last.then_inc(rot2_ready, 1)
                inverse_deviation(i, 3)
                pool.wait_ge(norm_ready, 5 * i + 2)
                g.tensor_tensor(x1[:], h[:], y[:], ALU.add)
                then()
                g.tensor_tensor(x1[:], x1[:], row(b2_r), ALU.add).then_inc(resid_ready, 1)
                inverse_deviation(i, 4)
                pool.wait_ge(norm_ready, 5 * i + 3)
                g.tensor_tensor(x1[:], h[:], row(bf2_r), ALU.add).then_inc(resid_ready, 1)
                inverse_deviation(i, 5)
                inverse_deviation(i, 6)

            pool.wait_ge(index_ready, 1)
            pool.wait_ge(xall_loaded, 16)
            for k in range(2):
                for n in range(TILES):
                    g.indirect_dma_start(xg_dram, bass.IndirectOffsetOnAxis(ap=scat_i[:, k, n:n + 1], axis=0),
                                         xall[:, n, :], None, bounds_check=E * CAP - 1, oob_is_err=False) \
                        .then_inc(scattered, 16)
            pool.wait_ge(ye_free, 32 * E + 16)
            for n in range(TILES):
                for k, dst in enumerate((y1, y2)):
                    g.indirect_dma_start(dst[:, n, :], None, yg_dram,
                                         bass.IndirectOffsetOnAxis(ap=gath_i[:, k, n:n + 1], axis=0)) \
                        .then_inc(gathered[n // (TILES // 4)], 16)


_INS = ["x", "x_txt", "L0_tok_scharr", "L0_txt_embed_weight", "L0_txt_proj_weight", "L0_txt_scale",
        "L0_attn_ln1_g", "L0_attn_ln1_b", "L0_attn_Wqkv", "L0_attn_bqkv", "L0_attn_Wo", "L0_attn_bo",
        "L0_attn_ln2_g", "L0_attn_ln2_b", "L0_attn_W1", "L0_attn_b1", "L0_attn_W2", "L0_attn_b2",
        "L0_ffn_W1", "L0_ffn_b1", "L0_ffn_W2", "L0_ffn_b2", "L1_attn_Wq", "L1_attn_Wk", "L1_attn_Wv",
        "L1_attn_Wo", "L1_attn_q_phase_angle", "L1_attn_alibi_log_slopes", "L1_ffn_router_gate",
        "L1_ffn_gate_w", "L1_ffn_up_w", "L1_ffn_down_w"]


def kernel(**inputs):
    import concourse.bacc as bacc
    from concourse.bass_utils import run_bass_kernel_spmd

    nc = bacc.Bacc("TRN2", target_bir_lowering=False, num_devices=1)
    arrays, aps = {}, {}
    for name in _INS:
        x = np.ascontiguousarray(inputs[name])
        if x.ndim == 0:
            x = x.reshape(1)
        arrays[f"in_{name}"] = x
        aps[name] = nc.dram_tensor(f"in_{name}", x.shape, mybir.dt.from_np(x.dtype), kind="ExternalInput").ap()
    arrays["in_const"] = shape_constants()
    const = nc.dram_tensor("in_const", (P, NC_COLS), F32, kind="ExternalInput").ap()
    out = nc.dram_tensor("out_0", (B, S, D), F32, kind="ExternalOutput").ap()
    early_fusion_kernel(nc, aps, const, out)
    r = run_bass_kernel_spmd(nc, [arrays], core_ids=[0])
    return r.results[0]["out_0"]
```

```python
import math
from contextlib import ExitStack

import numpy as np

import concourse.bass as bass
from concourse import mybir

F32 = mybir.dt.float32
F32R = mybir.dt.float32r
I32 = mybir.dt.int32
ALU = mybir.AluOpType
ACT = mybir.ActivationFunctionType
AX = mybir.AxisListType

P = 128
B = 8
IMG = 256
TXT = 128
D = 256
DC = D // P
S = IMG + TXT
NT = S // P
T = B * S
TILES = T // P
VOCAB_MOD = 262143
HASH_CUR, HASH_PREV = 36313, 27191
EMB = 64
EPS = 1e-5
H0, HD0 = 16, 16
H1, HD1, KV1 = 16, 64, 4
FF = 4 * D
FM = FF // P
E = 8
CAP = 960
CP = 120
CT = CAP // CP
HALF = CAP // 2
BIG = 3.0e38
GRAY = (0.2989, 0.587, 0.114)
HEADS = 16
SEG = [0, P, 3 * P]
TWO_PI_HI, TWO_PI_LO = 6.28125, 2 * math.pi - 6.28125
ROUND = 12582912.0

COLS = {}
NC_COLS = 0
for _name, _n in (("ident", P), ("rel", S), ("mask", S), ("cos", NT * 2 * HD0), ("sin", NT * 2 * HD0),
                  ("shift", 3 * P), ("before", P), ("ones", P), ("tiebreak", E * TILES),
                  ("expert_row", E * TILES), ("scan_keep", E * TILES)):
    COLS[_name] = (NC_COLS, NC_COLS + _n)
    NC_COLS += _n


def shape_constants():
    c = np.zeros((P, NC_COLS), np.float32)

    def put(name, value):
        a, b = COLS[name]
        c[:, a:b] = np.asarray(value, np.float32).reshape(P, b - a)

    p = np.arange(P)
    put("ident", np.eye(P))
    rel = (S - P) + p[:, None] - np.arange(S)[None, :]
    put("rel", rel)
    put("mask", np.where(rel < 0, BIG, 0.0))
    inv_freq = (1.0 / np.float32(10000.0) ** (np.arange(0, HD0, 2, dtype=np.float32) / np.float32(HD0))).astype(np.float32)
    pos = (p[:, None] + P * np.arange(NT)[None, :]).astype(np.float32)
    freqs = pos[..., None] * inv_freq
    cos, sin = np.cos(freqs).astype(np.float32), np.sin(freqs).astype(np.float32)
    cos2 = np.concatenate([cos, cos], -1)
    sin2 = np.concatenate([-sin, sin], -1)
    scale = -np.float32(HD0 ** -0.5)
    put("cos", np.stack([cos2 * scale, cos2], 2))
    put("sin", np.stack([sin2 * scale, sin2], 2))
    put("shift", np.stack([np.eye(P, k=1 - dy) for dy in range(3)], 1))
    put("before", np.triu(np.ones((P, P)), 1))
    put("ones", np.ones((P, P)))
    e = np.repeat(np.arange(E), TILES)
    put("tiebreak", np.broadcast_to(E - e, (P, E * TILES)))
    put("expert_row", np.broadcast_to(e * CAP, (P, E * TILES)))
    put("scan_keep", np.broadcast_to(np.tile(np.arange(TILES) > 0, E), (P, E * TILES)))
    return c


def psum_plan():
    setup = [("txt_index", 0, 1), ("projT", 1, 1)]
    setup += [(f"embT{b}", 2 + b % 2, 1) for b in range(B)]
    setup += [(f"txt{b}", 4 + b % 2, 1) for b in range(B)]
    setup += [("gamma", 6, 1)]
    setup += [(f"f1T{g}", (7, 0, 1, 2)[g], 1) for g in range(4)]
    setup += [(f"f2T{g}", (3, 4, 5, 6)[g], 1) for g in range(4)]
    setup += [("conv0", 0, 1), ("conv1", 1, 1)]

    body = [(f"ln_attn0_T{c}", 6 + c, 1) for c in range(DC)]
    body += [(f"qk0_{t}", 2 * t, 1) for t in range(NT)]
    body += [(f"v0_{t}", 2 * t + 1, 1) for t in range(NT)]
    for t in range(NT):
        body += [(f"stack{t}_{g}", (6, 7, 0, 2, 4)[(4 * t + g) % 5], 1) for g in range(4)]
    for layer in range(2):
        if layer == 1:
            body += [("conv1", 3, 1)]
            body += [(f"ln_attn1_T{c}", 4 + c, 1) for c in range(DC)]
            body += [(f"k1_{m}", 6 + m, 1) for m in range(2)]
            body += [(f"v1_{t}", t, 1) for t in range(NT)]
            body += [(f"q1_{m}", (3 + m) % 8, 1) for m in range(8)]
        for n in range(HEADS):
            body += [(f"scores{layer}_{n}", 2 * (n % 2), 1), (f"scores_b{layer}_{n}", 2 * (n % 2) + 1, 1)]
            body += [(f"probsT{layer}_{n}", 4, 1), (f"probsT_b{layer}_{n}", 5, 1)]
        for c in range(2 if layer == 0 else 8):
            body += [(f"out{layer}_{c}", 6 + c % 2, 1), (f"rinvT{layer}_{c}", 7 - c % 2, 1)]
        if layer == 0:
            body += [(f"proj0_{t}", t, 1) for t in range(NT)]
            body += [(f"ln_mlp_T{c}", 6 + c, 1) for c in range(DC)]
            body += [(f"up0_{m}", m % 6, 1) for m in range(FM)]
            body += [(f"down0_{t}", (6, 7, 0)[t], 1) for t in range(NT)]
            body += [("conv0", 5, 1)]
            body += [(f"ln_ffn_T{c}", 1 + c, 1) for c in range(DC)]
            body += [(f"up1_{m}", 3 + m % 4, 1) for m in range(FM)]
            body += [(f"down1_{t}", (7, 0, 1)[t], 1) for t in range(NT)]
    body += [(f"proj1_{t}", t, 1) for t in range(NT)]
    body += [(f"ln_moe_T{c}", 3 + c, 1) for c in range(DC)]
    body += [("logits", 5, 1)]

    route = [("prefix", 0, 1), ("slots", 1, 1)]
    route += [(f"xT{c}_{h}", 2 + 2 * h + c, 1) for h in range(2) for c in range(DC)]

    gates = []
    for q in range(2 * FM):
        gates += [(f"gate{q}", 2 * q % 8, 1), (f"up{q}", 2 * q % 8 + 1, 1)]
    rows_t = [(f"xT{c}_{h}", 2 * h + c, 1) for h in range(2) for c in range(DC)]
    down = [(f"down{j}", 4 + j, 1) for j in range(CT // 2)]
    return setup, body, route, gates + rows_t + down, gates + down


class Banks:

    def __init__(self, filled, freed):
        self.filled, self.freed = filled, freed
        self.at = {}
        fills, takes = [0] * 8, [1] * 8
        for k, (section, times) in enumerate(zip(psum_plan(), (1, B, 1, E - 1, 1))):
            f0, t0 = list(fills), list(takes)
            here = {}
            for name, bank, n in section:
                here[name] = (bank, fills[bank] + 1 - f0[bank], takes[bank] - t0[bank])
                fills[bank] += 1
                takes[bank] += n
            per_f = [a - b for a, b in zip(fills, f0)]
            per_t = [a - b for a, b in zip(takes, t0)]
            for name, (bank, f, t) in here.items():
                self.at[(k, name)] = (bank, f0[bank], per_f[bank], f, t0[bank], per_t[bank], t)
            fills = [a + (times - 1) * n for a, n in zip(fills, per_f)]
            takes = [a + (times - 1) * n for a, n in zip(takes, per_t)]

    def bank(self, section, name):
        return self.at[(section, name)][0]

    def wait_free(self, pe, section, name, i=0):
        bank, _, _, _, base, per, n = self.at[(section, name)]
        pe.wait_ge(self.freed[bank], i * per + (base + n))

    def wait_taken(self, eng, section, name, i=0):
        bank, _, _, _, base, per, n = self.at[(section, name)]
        eng.wait_ge(self.freed[bank], i * per + (base + n + 1))

    def wait_filled(self, eng, section, name, i=0):
        bank, base, per, n, _, _, _ = self.at[(section, name)]
        eng.wait_ge(self.filled[bank], i * per + (base + n))


SETUP, BODY, ROUTE, EXPERT, LAST = range(5)
LN_MLP, LN_FFN, LN_ATTN1, LN_FIRST, LN_ATTN0, LN_MOE = range(6)


def ln_count(i, k, t):
    return i * (6 * NT) + (2 * NT + NT * k + t + 1)


def norm_count(i, k, t):
    return i * (5 * NT) + (NT + NT * (k - (k > LN_FIRST)) + t + 1)
FIRST_LOADS = 11
LOADS = 21
GATE_BITS = 30
STEPS = 3
SEARCH = GATE_BITS // 2


def early_fusion_kernel(nc, a, const, out):
    ctx = ExitStack()
    offsets = {"top": nc.sbuf_base + (-nc.sbuf_base) % 64}

    def width(shape):
        return 4 * int(np.prod(shape[1:]))

    def place(name, shape, dt, at):
        assert at + width(shape) <= nc.sbuf_usable_end, (name, at + width(shape))
        return nc.alloc_sbuf_tensor_at(name, shape, dt, offset=at)

    def sb(name, shape, dt=F32):
        at = offsets["top"]
        offsets["top"] = at + (width(shape) + 31) // 32 * 32
        return place(name, shape, dt, at)

    def region(at, *tensors):
        made = []
        for name, shape, dt in tensors:
            made.append(place(name, shape, dt, at))
            at += (width(shape) + 31) // 32 * 32
        return made, at

    with ctx:
        def sem(name):
            return ctx.enter_context(nc.semaphore(name))

        h_dram = nc.dram_tensor("h_rows", [T, D], F32).ap()
        xn_dram = nc.dram_tensor("xn_rows", [T, D], F32).ap()
        xg_dram = nc.dram_tensor("expert_in", [E * CAP, D], F32).ap()
        yg_dram = nc.dram_tensor("expert_out", [E * CAP, D], F32).ap()

        cst = sb("cst", [P, NC_COLS])

        def const_cols(name):
            x, y = COLS[name]
            return cst[:, x:y]

        ident = const_cols("ident")
        logits_all = sb("logits_all", [P, TILES, E])
        small = sb("small", [P, 96])
        loop_start = offsets["top"]
        wqkv = sb("wqkv", [P, DC, 3 * D])
        wo0 = sb("wo0", [P, DC, D])
        w1 = sb("w1", [P, DC, FF])
        w2 = sb("w2", [P, FM, D])
        f1T = sb("f1T", [P, DC, FF], F32R)
        f2T = sb("f2T", [P, FM, D], F32R)
        wq1 = sb("wq1", [P, 8, 2, HD1])
        wk1 = sb("wk1", [P, KV1 * HD1])
        wv1 = sb("wv1", [P, KV1 * HD1])
        wo1 = sb("wo1", [P, 8, D])
        wr = sb("wr", [P, DC, E])
        rows = sb("rows", [P, 3 * D + 3 * D])
        bqkv, bo_r, b2_r, bf2_r = rows[:, 0:768], rows[:, 768:1024], rows[:, 1024:1280], rows[:, 1280:1536]
        cols = sb("cols", [P, 4 * DC + 2 * FM])
        band = sb("band", [P, 2, 3, P])
        edge_w = sb("edge_w", [3, 2, 2, P])
        alibi = sb("alibi", [P, H1, S])
        img = sb("img", [P, 3, 2, IMG])
        halo = sb("halo", [3, 3, 2, IMG])
        gray = sb("gray", [P, 2, IMG + 2])
        halo_gray = sb("halo_gray", [3, 2, IMG])
        h = sb("h", [P, NT, D])
        h_in = sb("h_in", [P, NT, D])
        x1 = sb("x1", [P, NT, D])
        xh = sb("xh", [P, NT, D])
        y = sb("y", [P, NT, D])
        xT = sb("xT", [P, DC, S])
        stats = sb("stats", [P, NT, 6])
        mean_var = sb("mean_var", [P, NT, 2])
        rstd = sb("rstd", [P, NT])
        eps = sb("eps", [P, NT])
        carrier = sb("carrier", [P, 4])
        power = sb("power", [P, NT])
        vpad = sb("vpad", [P, NT, 8, 64])
        nmax = sb("nmax", [P, 2, NT])
        rowsum = sb("rowsum", [P, HEADS, NT])
        rinv = sb("rinv", [P, 2, NT, P])
        rinvT = sb("rinvT", [P, 2, S])
        zeros = sb("zeros", [P, D])
        attention_start = offsets["top"]
        masked = sb("masked", [P, 2, 2 * S])
        probs = sb("probs", [P, 2, 2 * S])
        probsT = sb("probsT", [P, 2, 2 * S])
        o0T = sb("o0T", [P, DC, S])
        shared = offsets["top"]
        (qk, rot1, rot2), end_rope = region(
            attention_start, *[(n, [P, NT, 512], F32) for n in ("qk", "rot1", "rot2")])
        assert end_rope <= attention_start + 3 * 4 * 2 * 2 * S
        (stack_q, stack_k, q0T, k0T), _ = region(
            shared, ("stack_q", [P, 2, H0 * 64], F32R), ("stack_k", [P, 2, H0 * 64], F32R),
            ("q0T", [P, 8, S], F32R), ("k0T", [P, 8, S], F32R))
        (q1T, k1T, v1, o1T), end_second = region(
            shared, ("q1T", [P, 8, S], F32), ("k1T", [P, 2, S], F32),
            ("v1", [P, NT, KV1 * HD1], F32), ("o1T", [P, 8, S], F32))
        (hidT,), _ = region(shared, ("hidT", [P, FM, S], F32))
        (hid_parts, x_parts), end_parts = region(
            shared, ("hid_parts", [P, 2, FM, S], F32R), ("x_parts", [P, 2, DC, S], F32R))
        assert end_parts <= end_second
        (relu,), _ = region(attention_start, ("relu", [P, FM, S], F32))
        (edge, x_moe), _ = region(end_second, ("edge", [P, 2, 512], F32), ("x_moe", [P, NT, D], F32))

        (emb, embT, proj_raw, projT, txt_rows, hashf, hash_i, wq1_raw, rot_tmp, ang, scharr_b, scharr_h,
         tok, by0, by1, by2, by3, t_hi, t_lo, f1_raw, f2_raw, tern, tern_b), _ = region(
            attention_start,
            ("emb", [P, B, EMB], F32), ("embT", [EMB, 2, P], F32), ("proj_raw", [P, 2, EMB], F32),
            ("projT", [EMB, D], F32), ("txt_rows", [P, B, D], F32), ("hashf", [B, 4, TXT], F32),
            ("hash_i", [P, B], I32), ("wq1_raw", [P, H1, HD1 // 2, 2], F32), ("rot_tmp", [P, 2, P], F32),
            ("ang", [P, 8, H1], F32), ("scharr_b", [P, 2, 3, 3], F32), ("scharr_h", [3, 2, 3], F32),
            *[(n, [B, 2, TXT + 1], I32) for n in ("tok", "by0", "by1", "by2", "by3", "t_hi", "t_lo")],
            ("f1_raw", [P, FM, D], F32), ("f2_raw", [P, DC, FF], F32),
            ("tern", [P, 2048], F32), ("tern_b", [P, 2048], F32))
        txt_scale = small[:, 8:9]
        absum, above, below, gsum = small[:, 0:2], small[:, 2:4], small[:, 4:6], small[:, 6:8]

        (gate_raw, up_raw, down_raw, gate_w, up_w, down_w, xe, xeT, sil, prod, ye, wk, scat_i, gath_i), end_e = region(
            loop_start, ("gate_raw", [P, DC * FF], F32), ("up_raw", [P, DC * FF], F32),
            ("down_raw", [P, FM * D], F32), ("gate_w", [P, 2, DC, FF], F32R), ("up_w", [P, 2, DC, FF], F32R),
            ("down_w", [P, 2, FM, D], F32R), ("xe", [P, CT, D], F32), ("xeT", [P, 2, DC, CAP], F32R),
            ("sil", [P, 2, HALF], F32), ("prod", [P, 2, HALF], F32), ("ye", [P, CT, D], F32),
            ("wk", [P, 2, TILES], F32), ("scat_i", [P, 2, TILES], I32), ("gath_i", [P, 2, TILES], I32))
        (hT,), _ = region(end_e, ("hT", [P, 2, FM, CAP], F32R))
        (xall,), end_x = region(end_e, ("xall", [P, TILES, D], F32))
        (pr, oh1, oh2, gts, selm, eqm, r_a, r_b, r_c, r_tot), end_r = region(
            end_x, *[(n, [P, E, TILES], F32) for n in (
                "pr", "oh1", "oh2", "gts", "selm", "eqm", "r_a", "r_b", "r_c", "r_tot")])
        (sel_eq, kv, reach, cand, won, thr, best, bits, cnt, want, pos_f), _ = region(
            end_r, ("sel_eq", [P, 2, E * TILES], F32), ("kv", [P, 8, TILES], F32),
            ("reach", [P, STEPS, E, TILES], F32), ("cand", [P, STEPS, E], I32), ("won", [P, STEPS, E], I32),
            ("thr", [P, E], I32), ("best", [P, E], I32), ("bits", [P, STEPS], I32), ("cnt", [P, STEPS * E], F32),
            ("want", [P, E], F32), ("pos_f", [P, 4, TILES], F32))
        (y1, y2), _ = region(loop_start, ("y1", [P, TILES, D], F32), ("y2", [P, TILES, D], F32))

        ps = [ctx.enter_context(nc.psum_tensor(f"bank{k}", [P, 512], F32)) for k in range(8)]

        filled = [sem(f"bank{k}_filled") for k in range(8)]
        freed = [sem(f"bank{k}_freed") for k in range(8)]
        banks = Banks(filled, freed)
        first_loaded = sem("first_loaded")
        loaded = sem("loaded")
        tokens_loaded = sem("tokens_loaded")
        cleared = sem("cleared")
        expert_in_cleared = sem("expert_in_cleared")
        hash_ready = sem("hash_ready")
        emb_loaded = sem("emb_loaded")
        abs_ready = sem("abs_ready")
        ternary_ready = sem("ternary_ready")
        reduced = sem("reduced")
        angles_ready = sem("angles_ready")
        setup_dve = sem("setup_dve")
        img_loaded = sem("img_loaded")
        gray_ready = sem("gray_ready")
        txt_row_loaded = sem("txt_row_loaded")
        h_stored = sem("h_stored")
        var_ready = sem("var_ready")
        rstd_ready = sem("rstd_ready")
        norm_ready = sem("norm_ready")
        rot2_ready = sem("rot2_ready")
        roped = sem("roped")
        stack_hi = sem("stack_hi")
        stack_ready = sem("stack_ready")
        exp_done = sem("exp_done")
        rinv_ready = sem("rinv_ready")
        resid_ready = sem("resid_ready")
        x_part_upper = sem("x_part_upper")
        hid_split = sem("hid_split")
        logits_ready = sem("logits_ready")
        xall_loaded = sem("xall_loaded")
        lse_shift = sem("lse_shift")
        lse_exp = sem("lse_exp")
        counts_ready = sem("counts_ready")
        counts_taken = sem("counts_taken")
        sel_ready = sem("sel_ready")
        index_ready = sem("index_ready")
        scattered = sem("scattered")
        expert_gate_loaded = sem("expert_gate_loaded")
        gate_upper = sem("gate_upper")
        gate_split = sem("gate_split")
        down_upper = sem("down_upper")
        down_split = sem("down_split")
        x_upper = sem("x_upper")
        x_split = sem("x_split")
        h_upper = sem("h_upper")
        h_split = sem("h_split")
        expert_down_loaded = sem("expert_down_loaded")
        xe_loaded = sem("xe_loaded")
        ye_free = sem("ye_free")
        gathered = [sem(f"gathered{k}") for k in range(4)]
        h_reloaded = sem("h_reloaded")
        out_ready = sem("out_ready")
        out_stored = sem("out_stored")

        block = ctx.enter_context(nc.Block())

        def scores_place(layer, n, t):
            if t == 1:
                return ps[banks.bank(BODY, f"scores_b{layer}_{n}")][:, 0:2 * P]
            return ps[banks.bank(BODY, f"scores{layer}_{n}")][:, (0, 0, P)[t]:(P, 0, 4 * P)[t]]

        def pair_head(n):
            m, s = divmod(n, 2)
            return 8 * (m // 4) + 4 * s + m % 4

        def dve_takes_both(layer, n):
            return layer == 0 and n % 3 == 2

        def seg(t):
            return slice(SEG[t], SEG[t] + P * (t + 1))

        @block.sync
        def _(sp):
            def load_image(i):
                x = a["x"]
                sp.dma_start(img[:].rearrange("p c h w -> p (c h) w"),
                             x[i].rearrange("c (h p) w -> p (c h) w", p=P)).then_inc(img_loaded, 16)
                for dx in range(3):
                    lo, hi = max(0, 1 - dx), min(IMG, IMG + 1 - dx)
                    sp.dma_start(halo[dx:dx + 1, :, :, lo:hi],
                                 x[i, :, P - 1:P + 1, lo + dx - 1:hi + dx - 1].unsqueeze(0)).then_inc(img_loaded, 16)

            for s in range(2):
                sp.dma_start(tok[:, s, 1:], a["x_txt"]).then_inc(tokens_loaded, 16)
            sp.dma_start(cst[:], const).then_inc(first_loaded, 16)
            n = 0
            for k, (dst, src) in enumerate((
                (f1_raw[:], a["L0_ffn_W1"].rearrange("(m p) d -> p m d", p=P)),
                (f2_raw[:], a["L0_ffn_W2"].rearrange("(c p) f -> p c f", p=P)),
                (proj_raw[:], a["L0_txt_proj_weight"].rearrange("(c p) e -> p c e", p=P)),
                (wq1_raw[:].rearrange("p h i r -> p (h i r)"), a["L1_attn_Wq"]),
                (ang[:, 0, :], a["L1_attn_q_phase_angle"].partition_broadcast(P)),
                (ang[:, 1, :], a["L1_attn_alibi_log_slopes"].partition_broadcast(P)),
                (scharr_b[:].rearrange("p k a b -> p (k a b)"),
                 a["L0_tok_scharr"].rearrange("k o a b -> (k o a b)").partition_broadcast(P)),
                (txt_scale, a["L0_txt_scale"].partition_broadcast(P)),
                (scharr_h[:, 0, :], a["L0_tok_scharr"][0, 0].rearrange("a b -> b a")),
                (scharr_h[:, 1, :], a["L0_tok_scharr"][1, 0].rearrange("a b -> b a")),
                (wqkv[:], a["L0_attn_Wqkv"].rearrange("(c p) n -> p c n", p=P)),
                (wo0[:], a["L0_attn_Wo"].rearrange("(c p) n -> p c n", p=P)),
                (w1[:], a["L0_attn_W1"].rearrange("(c p) n -> p c n", p=P)),
                (w2[:], a["L0_attn_W2"].rearrange("(m p) n -> p m n", p=P)),
                (wk1[:], a["L1_attn_Wk"]),
                (wv1[:], a["L1_attn_Wv"]),
                (bqkv, a["L0_attn_bqkv"].partition_broadcast(P)),
                (bo_r, a["L0_attn_bo"].partition_broadcast(P)),
                (b2_r, a["L0_attn_b2"].partition_broadcast(P)),
                (bf2_r, a["L0_ffn_b2"].partition_broadcast(P)),
                (wr[:], a["L1_ffn_router_gate"].rearrange("(c p) e -> p c e", p=P)),
            )):
                if k < FIRST_LOADS - 1:
                    sp.dma_start(dst, src, allow_slow_non_contiguous=True).then_inc(first_loaded, 16)
                else:
                    if k == FIRST_LOADS - 1:
                        sp.wait_ge(cleared, 1)
                        load_image(0)
                        sp.wait_ge(emb_loaded, 16 * B)
                    sp.dma_start(dst, src).then_inc(loaded, 16)
                    n += 1
            wo1_src = a["L1_attn_Wo"].rearrange("(g s r d) n -> g s d r n", g=2, s=2, r=4, d=HD1)
            for g in range(2):
                for s in range(2):
                    sp.dma_start(wo1[64 * s:64 * s + 64, 4 * g:4 * g + 4, :], wo1_src[g, s]).then_inc(loaded, 16)
                    n += 1
            for k, name in enumerate(("L0_attn_ln1_g", "L0_attn_ln1_b", "L0_attn_ln2_g", "L0_attn_ln2_b")):
                sp.dma_start(cols[:, DC * k:DC * k + DC], a[name].rearrange("(c p) -> p c", p=P),
                             allow_slow_non_contiguous=True).then_inc(loaded, 16)
                n += 1
            for k, name in enumerate(("L0_attn_b1", "L0_ffn_b1")):
                sp.dma_start(cols[:, 4 * DC + FM * k:4 * DC + FM * k + FM], a[name].rearrange("(m p) -> p m", p=P),
                             allow_slow_non_contiguous=True).then_inc(loaded, 16)
                n += 1
            assert n == LOADS
            banks.wait_taken(sp, SETUP, f"txt{B - 1}")
            sp.dma_start(h_dram.rearrange("(b t p) d -> p b t d", b=B, t=NT)[:, :, NT - 1, :],
                         txt_rows[:]).then_inc(h_stored, 16)
            sp.wait_ge(h_stored, 16)

            def load_text(i):
                sp.dma_start(h_in[:, NT - 1, :], h_dram.rearrange("(b t p) d -> b t p d", b=B, t=NT)[i, NT - 1]) \
                    .then_inc(txt_row_loaded, 16)

            def store_tokens(i):
                sp.wait_ge(norm_ready, norm_count(i, LN_MOE, NT - 1))
                sp.dma_start(xn_dram.rearrange("(b t p) d -> b p t d", b=B, t=NT)[i], x_moe[:]).then_inc(h_stored, 16)
                sp.dma_start(h_dram.rearrange("(b t p) d -> b p t d", b=B, t=NT)[i], h[:]).then_inc(h_stored, 16)

            def turn(i, text_row, image):
                sp.wait_ge(resid_ready, 3 * i + 2)
                load_text(text_row)
                sp.wait_ge(gray_ready, i + 2)
                load_image(image)
                store_tokens(i)

            load_text(0)
            sp.wait_ge(gray_ready, 1)
            load_image(1)
            n = E * CAP // P
            sp.dma_start(xg_dram.rearrange("(p n) d -> p n d", p=P), zeros[:].unsqueeze(1).to_broadcast([P, n, D])) \
                .then_inc(expert_in_cleared, 16)
            with sp.Fori(0, B - 2) as i:
                turn(i, i + 1, i + 2)
            turn(B - 2, B - 1, B - 1)
            sp.wait_ge(resid_ready, 3 * B - 1)
            load_text(B - 1)
            store_tokens(B - 1)
            sp.wait_ge(h_stored, 32 * B + 16)

            sp.wait_ge(logits_ready, B)
            sp.dma_start(xall[:], xn_dram.rearrange("(n p) d -> p n d", p=P)).then_inc(xall_loaded, 16)

            def load_gate_up(e):
                sp.dma_start(gate_raw[:].rearrange("p (c n) -> p c n", c=DC), a["L1_ffn_gate_w"][e].rearrange("(c p) n -> p c n", p=P)) \
                    .then_inc(expert_gate_loaded, 16)
                sp.dma_start(up_raw[:].rearrange("p (c n) -> p c n", c=DC), a["L1_ffn_up_w"][e].rearrange("(c p) n -> p c n", p=P)) \
                    .then_inc(expert_gate_loaded, 16)

            def load_down(e):
                sp.dma_start(down_raw[:].rearrange("p (m n) -> p m n", m=FM), a["L1_ffn_down_w"][e].rearrange("(m p) n -> p m n", p=P)) \
                    .then_inc(expert_down_loaded, 16)

            def load_rows(e):
                sp.dma_start(xe[0:CP], xg_dram.rearrange("(e j p) d -> e p j d", e=E, j=CT)[e]).then_inc(xe_loaded, 16)

            yg_view = yg_dram.rearrange("(e s j p) d -> e s p j d", e=E, s=2, p=CP)

            def store_rows(section, e, i):
                for s in range(2):
                    banks.wait_taken(sp, section, f"down{2 * s + 1}", i)
                    sp.dma_start(yg_view[e, s], ye[0:CP, CT // 2 * s:CT // 2 * (s + 1)]).then_inc(ye_free, 16)

            load_gate_up(0)
            load_down(0)
            sp.wait_ge(scattered, 16 * 2 * TILES)
            load_rows(0)
            with sp.Fori(0, E - 1) as e:
                sp.wait_ge(gate_split, e + 1)
                load_gate_up(e + 1)
                sp.wait_ge(x_split, 2 * DC * e + 2 * DC)
                load_rows(e + 1)
                sp.wait_ge(down_split, e + 1)
                load_down(e + 1)
                store_rows(EXPERT, e, e)
            store_rows(LAST, E - 1, 0)

            sp.wait_ge(ye_free, 32 * E + 16)
            sp.dma_start(xall[:], h_dram.rearrange("(n p) d -> p n d", p=P)).then_inc(h_reloaded, 16)
            for k in range(4):
                sp.wait_ge(out_ready, k + 1)
                n0, n1 = TILES // 4 * k, TILES // 4 * (k + 1)
                sp.dma_start(out.rearrange("b (t p) d -> p (b t) d", p=P)[:, n0:n1], xall[:, n0:n1]) \
                    .then_inc(out_stored, 16)
            sp.wait_ge(out_stored, 64)

        @block.tensor
        def _(pe):
            mm, tr = nc.tensor.matmul, nc.tensor.transpose

            def transposed(prefix, src, i, k):
                for t in range(NT):
                    pe.wait_ge(norm_ready, i * (5 * NT) + NT if k == LN_ATTN0 else norm_count(i, k, t))
                    for c in range(DC):
                        name = f"{prefix}{c}"
                        if t == 0:
                            banks.wait_free(pe, BODY, name, i)
                        bank = banks.bank(BODY, name)
                        last = tr(ps[bank][:, P * t:P * (t + 1)], src[:, t, P * c:P * (c + 1)], ident)
                        if t == NT - 1:
                            last.then_inc(filled[bank], 1)

            def convolve(section, i, count, halves):
                pe.wait_ge(gray_ready, count)
                for hf in halves:
                    name = f"conv{hf}"
                    bank = banks.bank(section, name)
                    banks.wait_free(pe, section, name, i)
                    for k in range(2):
                        o = ps[bank][:, IMG * k:IMG * (k + 1)]
                        for dx in range(3):
                            mm(o, band[:, k, dx, :], gray[:, hf, dx:dx + IMG], start=(dx == 0), stop=False)
                        last = mm(o, edge_w[:, hf, k, :], halo_gray[:, 1 - hf, :], start=False, stop=True)
                    last.then_inc(filled[bank], 1)

            pe.wait_ge(first_loaded, 16 * FIRST_LOADS)
            banks.wait_free(pe, SETUP, "projT")
            for c in range(DC):
                last = tr(ps[1][0:EMB, P * c:P * (c + 1)], proj_raw[:, c, :], ident)
            last.then_inc(filled[1], 1)
            pe.wait_ge(hash_ready, 1)
            banks.wait_free(pe, SETUP, "txt_index")
            tr(ps[0][:, 0:B], hashf[:, 0, :], ident[0:B, 0:B]).then_inc(filled[0], 1)
            pe.wait_ge(abs_ready, 1)
            banks.wait_free(pe, SETUP, "gamma")
            mm(ps[6][:, 0:2], const_cols("ones"), absum, start=True, stop=True).then_inc(filled[6], 1)
            pe.wait_ge(emb_loaded, 16 * B)
            banks.wait_taken(pe, SETUP, "projT")
            for b in range(B + 1):
                if b < B:
                    k = banks.bank(SETUP, f"embT{b}")
                    banks.wait_free(pe, SETUP, f"embT{b}")
                    tr(ps[k][0:EMB, 0:P], emb[:, b, :], ident).then_inc(filled[k], 1)
                if b > 0:
                    k = banks.bank(SETUP, f"txt{b - 1}")
                    banks.wait_free(pe, SETUP, f"txt{b - 1}")
                    banks.wait_taken(pe, SETUP, f"embT{b - 1}")
                    mm(ps[k][:, 0:D], embT[:, (b - 1) % 2, :], projT[:], start=True, stop=True) \
                        .then_inc(filled[k], 1)
            for g in range(4):
                k = banks.bank(SETUP, f"f1T{g}")
                banks.wait_free(pe, SETUP, f"f1T{g}")
                pe.wait_ge(ternary_ready, 1)
                c, m0 = divmod(g, 2)
                for q in range(4):
                    m = 4 * m0 + q
                    last = tr(ps[k][:, P * q:P * (q + 1)], tern[:, D * m + P * c:D * m + P * (c + 1)], ident)
                last.then_inc(filled[k], 1)
            for g in range(4):
                k = banks.bank(SETUP, f"f2T{g}")
                banks.wait_free(pe, SETUP, f"f2T{g}")
                pe.wait_ge(ternary_ready, 2)
                for q in range(4):
                    m, c = 2 * g + q // 2, q % 2
                    last = tr(ps[k][:, P * q:P * (q + 1)], tern_b[:, FF * c + P * m:FF * c + P * (m + 1)], ident)
                last.then_inc(filled[k], 1)
            convolve(SETUP, 0, 1, range(2))
            pe.wait_ge(setup_dve, 1)
            pe.wait_ge(loaded, 16 * LOADS)
            banks.wait_taken(pe, SETUP, "f2T3")

            def head_scores(layer, n, i):
                ba, bb = banks.bank(BODY, f"scores{layer}_{n}"), banks.bank(BODY, f"scores_b{layer}_{n}")
                banks.wait_free(pe, BODY, f"scores{layer}_{n}", i)
                banks.wait_free(pe, BODY, f"scores_b{layer}_{n}", i)
                for t in (0, 2, 1):
                    if layer == 0:
                        half = slice(64 * (n % 2), 64 * (n % 2) + 64)
                        q, k = q0T[half, n // 2, :], k0T[half, n // 2, :]
                    else:
                        half = slice(64 * (n % 2), 64 * (n % 2) + 64)
                        q, k = q1T[half, n // 2, :], k1T[half, n // 8, :]
                    last = mm(scores_place(layer, n, t), q[:, P * t:P * (t + 1)], k[:, 0:P * (t + 1)],
                              start=True, stop=True)
                    if t == 2:
                        last.then_inc(filled[ba], 1)
                last.then_inc(filled[bb], 1)

            def probs_transposed(layer, n, i):
                ba, bb = banks.bank(BODY, f"probsT{layer}_{n}"), banks.bank(BODY, f"probsT_b{layer}_{n}")
                pe.wait_ge(exp_done, 2 * HEADS * i + (HEADS * layer + n + 1))
                p = probs[:, n % 2, :]
                banks.wait_free(pe, BODY, f"probsT{layer}_{n}", i)
                for t in range(NT):
                    last = tr(ps[ba][:, P * t:P * (t + 1)], p[:, SEG[t]:SEG[t] + P], ident)
                last.then_inc(filled[ba], 1)
                banks.wait_free(pe, BODY, f"probsT_b{layer}_{n}", i)
                for q, (t, j) in enumerate(((1, 1), (2, 1), (2, 2))):
                    last = tr(ps[bb][:, P * q:P * (q + 1)], p[:, SEG[t] + P * j:SEG[t] + P * (j + 1)], ident)
                last.then_inc(filled[bb], 1)

            def denominators_transposed(layer, c, i):
                bank = banks.bank(BODY, f"rinvT{layer}_{c}")
                pe.wait_ge(rinv_ready, 10 * i + (2 * layer + c + 1))
                banks.wait_free(pe, BODY, f"rinvT{layer}_{c}", i)
                for t in range(NT):
                    last = tr(ps[bank][:, P * t:P * (t + 1)], rinv[:, c % 2, t, :], ident)
                last.then_inc(filled[bank], 1)

            def head_out(layer, n, i):
                c = n // 8 if layer == 0 else n // 2
                bank = banks.bank(BODY, f"out{layer}_{c}")
                if n == c * (8 if layer == 0 else 2):
                    banks.wait_free(pe, BODY, f"out{layer}_{c}", i)
                banks.wait_taken(pe, BODY, f"probsT{layer}_{n}", i)
                banks.wait_taken(pe, BODY, f"probsT_b{layer}_{n}", i)
                pT = probsT[:, n % 2, :]
                for j, cols_j in enumerate((slice(0, 3 * P), slice(3 * P, 5 * P), slice(5 * P, 6 * P))):
                    if layer == 0:
                        rows_o = slice(32 * (n % 8 // 2), 32 * (n % 8 // 2) + 32)
                        v = vpad[:, j, n // 2, 32 * (n % 2):32 * (n % 2) + 32]
                        first, final = n % 2 == 0 and j == 0, n % 2 == 1 and j == 2
                    else:
                        rows_o = slice(64 * (n % 2), 64 * (n % 2) + 64)
                        kv = pair_head(n) // 4
                        v = v1[:, j, HD1 * kv:HD1 * (kv + 1)]
                        first, final = j == 0, j == 2
                    last = mm(ps[bank][rows_o, P * j:S], v, pT[:, cols_j], start=first, stop=final)
                if n % (8 if layer == 0 else 2) == (7 if layer == 0 else 1):
                    last.then_inc(filled[bank], 1)

            def attention(layer, i):
                per = 8 if layer == 0 else 2
                head_scores(layer, 0, i)
                head_scores(layer, 1, i)
                for n in range(HEADS):
                    if n + 2 < HEADS:
                        head_scores(layer, n + 2, i)
                    probs_transposed(layer, n, i)
                    if n >= 1:
                        head_out(layer, n - 1, i)
                    if n % per == 0 and n > 0:
                        denominators_transposed(layer, n // per - 1, i)
                denominators_transposed(layer, HEADS // per - 1, i)
                head_out(layer, HEADS - 1, i)

            def token_major(name, i, lhs, weights, chunks):
                for t in range(NT):
                    bank = banks.bank(BODY, f"{name}_{t}")
                    banks.wait_free(pe, BODY, f"{name}_{t}", i)
                    for m in range(chunks):
                        last = mm(ps[bank][:, 0:D], lhs[:, m, P * t:P * (t + 1)], weights[:, m, :],
                                  start=(m == 0), stop=(m == chunks - 1))
                    last.then_inc(filled[bank], 1)

            def xT_wait(i, name):
                for c in range(DC):
                    banks.wait_taken(pe, BODY, f"{name}{c}", i)

            def up(names, i, w):
                for m in range(FM):
                    bank = banks.bank(BODY, names + str(m))
                    banks.wait_free(pe, BODY, names + str(m), i)
                    for c in range(DC):
                        last = mm(ps[bank][:, 0:S], w[:, c, P * m:P * (m + 1)], xT[:, c, :],
                                  start=(c == 0), stop=(c == DC - 1))
                    last.then_inc(filled[bank], 1)

            with pe.Fori(0, B) as i:
                transposed("ln_attn0_T", xh, i, LN_ATTN0)
                xT_wait(i, "ln_attn0_T")
                for name, cols_w in (("qk0", slice(0, 2 * D)), ("v0", slice(2 * D, 3 * D))):
                    for t in range(NT):
                        bank = banks.bank(BODY, f"{name}_{t}")
                        banks.wait_free(pe, BODY, f"{name}_{t}", i)
                        for c in range(DC):
                            last = mm(ps[bank][:, 0:cols_w.stop - cols_w.start], xT[:, c, P * t:P * (t + 1)],
                                      wqkv[:, c, cols_w], start=(c == 0), stop=(c == DC - 1))
                        last.then_inc(filled[bank], 1)
                for t in range(NT):
                    pe.wait_ge(stack_ready, NT * i + (t + 1))
                    for g in range(4):
                        bank = banks.bank(BODY, f"stack{t}_{g}")
                        banks.wait_free(pe, BODY, f"stack{t}_{g}", i)
                        src = (stack_q, stack_k)[g // 2][:, t % 2, :].bitcast(F32)
                        for q in range(4):
                            hp = 4 * (g % 2) + q
                            last = tr(ps[bank][:, P * q:P * (q + 1)], src[:, P * hp:P * (hp + 1)], ident)
                        last.then_inc(filled[bank], 1)
                for g in (2, 3):
                    banks.wait_taken(pe, BODY, f"stack{NT - 1}_{g}", i)
                attention(0, i)
                banks.wait_taken(pe, BODY, "out0_1", i)
                token_major("proj0", i, o0T, wo0, DC)

                transposed("ln_mlp_T", xh, i, LN_MLP)
                xT_wait(i, "ln_mlp_T")
                up("up0_", i, w1)
                banks.wait_taken(pe, BODY, f"up0_{FM - 1}", i)
                token_major("down0", i, hidT, w2, FM)

                convolve(BODY, i, i + 2, (0,))

                transposed("ln_ffn_T", xh, i, LN_FFN)
                xT_wait(i, "ln_ffn_T")
                for m in range(FM):
                    bank = banks.bank(BODY, f"up1_{m}")
                    banks.wait_free(pe, BODY, f"up1_{m}", i)
                    for c in range(DC):
                        for part in range(2):
                            last = mm(ps[bank][:, 0:S], f1T[:, c, P * m:P * (m + 1)], x_parts[:, part, c, :],
                                      start=(c == 0 and part == 0), stop=(c == DC - 1 and part == 1))
                    last.then_inc(filled[bank], 1)
                for t in range(NT):
                    bank = banks.bank(BODY, f"down1_{t}")
                    banks.wait_free(pe, BODY, f"down1_{t}", i)
                    for m in range(FM):
                        if t == 0:
                            pe.wait_ge(hid_split, FM * i + (m + 1))
                        for part in range(2):
                            last = mm(ps[bank][:, 0:D], hid_parts[:, part, m, P * t:P * (t + 1)], f2T[:, m, :],
                                      start=(m == 0 and part == 0), stop=(m == FM - 1 and part == 1))
                    last.then_inc(filled[bank], 1)

                convolve(BODY, i, i + 2, (1,))

                transposed("ln_attn1_T", xh, i, LN_ATTN1)
                xT_wait(i, "ln_attn1_T")
                for m in range(2):
                    bank = banks.bank(BODY, f"k1_{m}")
                    banks.wait_free(pe, BODY, f"k1_{m}", i)
                    mm(ps[bank][:, 0:S], wk1[:, P * m:P * (m + 1)], xT[:, 1, :], start=True, stop=True) \
                        .then_inc(filled[bank], 1)
                for t in range(NT):
                    bank = banks.bank(BODY, f"v1_{t}")
                    banks.wait_free(pe, BODY, f"v1_{t}", i)
                    mm(ps[bank][:, 0:KV1 * HD1], xT[:, 0, P * t:P * (t + 1)], wv1[:], start=True, stop=True) \
                        .then_inc(filled[bank], 1)
                for m in range(8):
                    bank = banks.bank(BODY, f"q1_{m}")
                    banks.wait_free(pe, BODY, f"q1_{m}", i)
                    mm(ps[bank][:, 0:S], wq1[:, m].rearrange("p s d -> p (s d)"), xT[:, 1, :],
                       start=True, stop=True).then_inc(filled[bank], 1)
                for m in (6, 7):
                    banks.wait_taken(pe, BODY, f"q1_{m}", i)
                attention(1, i)
                banks.wait_taken(pe, BODY, "out1_7", i)
                token_major("proj1", i, o1T, wo1, 8)

                transposed("ln_moe_T", x_moe, i, LN_MOE)
                xT_wait(i, "ln_moe_T")
                bank = banks.bank(BODY, "logits")
                banks.wait_free(pe, BODY, "logits", i)
                for t in range(NT):
                    for c in range(DC):
                        last = mm(ps[bank][:, E * t:E * (t + 1)], xT[:, c, P * t:P * (t + 1)], wr[:, c, :],
                                  start=(c == 0), stop=(c == DC - 1))
                last.then_inc(filled[bank], 1)

            with pe.Fori(0, SEARCH // 3) as r:
                for u in range(3):
                    pe.wait_ge(counts_ready, r * 3 + (u + 1))
                    mm(ps[7][:, 0:STEPS * E], const_cols("ones"), cnt[:], start=True, stop=True) \
                        .then_inc(counts_taken, 1)
            for k, name in enumerate(("prefix", "slots")):
                bank = banks.bank(ROUTE, name)
                pe.wait_ge(sel_ready, k + 1)
                banks.wait_free(pe, ROUTE, name)
                w = E * TILES
                if k == 0:
                    mm(ps[6][:, 0:w], const_cols("ones"), sel_eq[:, 1, :], start=True, stop=True)
                mm(ps[bank][:, 0:w], const_cols("ones"), sel_eq[:, 0, :], start=True, stop=True)
                mm(ps[bank][:, w:2 * w], const_cols("before"), sel_eq[:, 0, :], start=True, stop=True) \
                    .then_inc(filled[bank], 1)

            PASSES = ((0, 0), (0, 1), (1, 0))

            def rows_transposed(section, e, i):
                pe.wait_ge(xe_loaded, 16 * e + 16)
                for hf in range(2):
                    for c in range(DC):
                        bank = banks.bank(section, f"xT{c}_{hf}")
                        banks.wait_free(pe, section, f"xT{c}_{hf}", i)
                        for q in range(4):
                            last = tr(ps[bank][:, CP * q:CP * (q + 1)], xe[0:CP, 4 * hf + q, P * c:P * (c + 1)],
                                      ident[0:CP, 0:CP])
                        last.then_inc(filled[bank], 1)

            def gates(section, e, i):
                pe.wait_ge(gate_split, e + 1)
                for q in range(2 * FM):
                    hf, m = divmod(q, FM)
                    if m == 0:
                        pe.wait_ge(x_split, 2 * DC * e + DC * (hf + 1))
                    for name, w in ((f"gate{q}", gate_w), (f"up{q}", up_w)):
                        bank = banks.bank(section, name)
                        banks.wait_free(pe, section, name, i)
                        for c in range(DC):
                            for k, (wp, xp) in enumerate(PASSES):
                                last = mm(ps[bank][:, 0:HALF], w[:, wp, c, P * m:P * (m + 1)],
                                          xeT[:, xp, c, HALF * hf:HALF * (hf + 1)],
                                          start=(c == 0 and k == 0), stop=(c == DC - 1 and k == 2))
                        last.then_inc(filled[bank], 1)

            def down(section, e, i):
                pe.wait_ge(down_split, e + 1)
                for j in range(CT):
                    bank = banks.bank(section, f"down{j // 2}")
                    if j % 2 == 0:
                        banks.wait_free(pe, section, f"down{j // 2}", i)
                    if j in (0, 4):
                        pe.wait_ge(h_split, 2 * FM * e + FM * (j // 4 + 1))
                    for m in range(FM):
                        for k, (hp, wp) in enumerate(PASSES):
                            last = mm(ps[bank][:, D * (j % 2):D * (j % 2) + D][0:CP], hT[:, hp, m, CP * j:CP * (j + 1)],
                                      down_w[:, wp, m, :], start=(m == 0 and k == 0), stop=(m == FM - 1 and k == 2))
                    if j % 2 == 1:
                        last.then_inc(filled[bank], 1)

            rows_transposed(ROUTE, 0, 0)
            with pe.Fori(0, E - 1) as e:
                gates(EXPERT, e, e)
                rows_transposed(EXPERT, e + 1, e)
                down(EXPERT, e, e)
            gates(LAST, E - 1, 0)
            down(LAST, E - 1, 0)

        @block.scalar
        def _(act):
            f = nc.scalar.activation

            def take(section, name, i, dst, fn, width, rows_p=P, **kw):
                banks.wait_filled(act, section, name, i)
                bank = banks.bank(section, name)
                src = ps[bank][0:rows_p, 0:width]
                if fn is None:
                    ins = nc.scalar.copy(dst, src)
                else:
                    ins = f(dst, src, fn, **kw)
                ins.then_inc(freed[bank], 1)

            act.wait_ge(first_loaded, 16 * FIRST_LOADS)
            take(SETUP, "projT", 0, projT[:], None, D, EMB)
            act.wait_ge(reduced, 1)
            f(ang[:, 4, :], ang[:, 2, :], ACT.Sin)
            f(ang[:, 5, :], ang[:, 3, :], ACT.Sin)
            f(ang[:, 6, :], ang[:, 1, :], ACT.Exp).then_inc(angles_ready, 1)
            for b in range(B):
                if b >= 2:
                    banks.wait_filled(act, SETUP, f"txt{b - 2}")
                take(SETUP, f"embT{b}", 0, embT[:, b % 2, :], None, P, EMB)
            for g in range(4):
                c, m0 = divmod(g, 2)
                take(SETUP, f"f1T{g}", 0, f1T[:, c, 4 * P * m0:4 * P * (m0 + 1)], None, 4 * P)
            for g in range(4):
                take(SETUP, f"f2T{g}", 0, f2T[:, 2 * g:2 * g + 2, :].rearrange("p m n -> p (m n)"), None, 4 * P)
            act.wait_ge(setup_dve, 1)
            act.wait_ge(h_stored, 16)

            def ln_out(name, i, g=None, b=None):
                if g is None:
                    take(BODY, f"{name}0", i, xT[:, 0, :], None, S)
                else:
                    take(BODY, f"{name}0", i, xT[:, 0, :], ACT.Identity, S,
                         bias=cols[:, b:b + 1], scale=cols[:, g:g + 1])

            def take_stack(t, g, i):
                name = f"stack{t}_{g}"
                banks.wait_filled(act, BODY, name, i)
                bank = banks.bank(BODY, name)
                nc.scalar.copy((q0T, k0T)[g // 2][:, 4 * (g % 2):4 * (g % 2) + 4, P * t:P * (t + 1)],
                               ps[bank][:].rearrange("p (q n) -> p q n", q=4)).then_inc(freed[bank], 1)

            def exps(layer, n, i):
                banks.wait_taken(act, BODY, f"scores_b{layer}_{n}", i)
                s = n % 2
                if n >= 2:
                    banks.wait_filled(act, BODY, f"probsT_b{layer}_{n - 2}", i)
                for t in range(NT):
                    last = f(probs[:, s, seg(t)], masked[:, s, seg(t)], ACT.Exp, bias=nmax[:, s, t:t + 1],
                             scale=-1.0, accum_out=rowsum[:, n, t:t + 1])
                last.then_inc(exp_done, 1)

            def attention(layer, i):
                per = 8 if layer == 0 else 2
                exps(layer, 0, i)
                for n in range(HEADS):
                    if n + 1 < HEADS:
                        exps(layer, n + 1, i)
                    if n % per == 1 and n > per:
                        take_denominators(layer, n // per - 1, i)
                    if not dve_takes_both(layer, n):
                        take(BODY, f"probsT{layer}_{n}", i, probsT[:, n % 2, 0:3 * P], None, 3 * P)
                take_denominators(layer, HEADS // per - 1, i)

            def take_denominators(layer, c, i):
                if c >= 2:
                    banks.wait_taken(act, BODY, f"out{layer}_{c - 2}", i)
                take(BODY, f"rinvT{layer}_{c}", i, rinvT[:, c % 2, :], None, S)

            def edges(section, i, halves):
                for hf in halves:
                    take(section, f"conv{hf}", i, edge[:, hf, :], ACT.Abs, 2 * IMG)

            act.wait_ge(loaded, 16 * LOADS)
            edges(SETUP, 0, range(2))
            with act.Fori(0, B) as i:
                ln_out("ln_attn0_T", i, 0, 2)
                for t in range(NT):
                    act.wait_ge(roped, NT * i + (t + 1))
                    if t >= 2:
                        banks.wait_filled(act, BODY, f"stack{t - 2}_3", i)
                    for x, (dst, slots) in enumerate(((stack_q, (0, 2)), (stack_k, (0, 1)))):
                        o = dst[:, t % 2, :].rearrange("p (h s d) -> p h s d", h=H0, s=4)
                        for s in slots:
                            last = nc.scalar.copy(o[:, :, s, :], rot1[:, t, D * x:D * (x + 1)].rearrange(
                                "p (h d) -> p h d", h=H0))
                    last.then_inc(stack_hi, 1)
                    if t >= 1:
                        take_stack(t - 1, 0, i)
                        take_stack(t - 1, 2, i)
                take_stack(NT - 1, 0, i)
                take_stack(NT - 1, 2, i)
                attention(0, i)
                ln_out("ln_mlp_T", i, 4, 6)
                for m in range(FM):
                    take(BODY, f"up0_{m}", i, hidT[:, m, :], ACT.Gelu, S,
                         bias=cols[:, 4 * DC + m:4 * DC + m + 1])
                edges(BODY, i, (0,))
                for c in range(DC):
                    banks.wait_filled(act, BODY, f"ln_ffn_T{c}", i)
                    nc.scalar.copy(x_parts[:, 0, c, :], ps[banks.bank(BODY, f"ln_ffn_T{c}")][:, 0:S]) \
                        .then_inc(x_part_upper, 1)
                for m in range(FM):
                    bias = cols[:, 4 * DC + FM + m:4 * DC + FM + m + 1]
                    if m % 2 == 0:
                        banks.wait_filled(act, BODY, f"up1_{m}", i)
                        f(hid_parts[:, 0, m, :], ps[banks.bank(BODY, f"up1_{m}")][:, 0:S], ACT.Relu, bias=bias)
                    take(BODY, f"up1_{m}", i, relu[:, m, :], ACT.Relu, S, bias=bias)
                edges(BODY, i, (1,))
                ln_out("ln_attn1_T", i)
                for m in range(2):
                    take(BODY, f"k1_{m}", i, k1T[:, m, :], None, S)
                for m in range(0, 8, 2):
                    take(BODY, f"q1_{m}", i, q1T[:, m, :], None, S)
                attention(1, i)
                ln_out("ln_moe_T", i)

            act.wait_ge(lse_shift, 1)
            f(pr[:], pr[:], ACT.Exp).then_inc(lse_exp, 1)

            def gate_uppers(e):
                act.wait_ge(expert_gate_loaded, 32 * e + 32)
                nc.scalar.copy(gate_w[:, 0].rearrange("p c n -> p (c n)"), gate_raw[:])
                nc.scalar.copy(up_w[:, 0].rearrange("p c n -> p (c n)"), up_raw[:]).then_inc(gate_upper, 1)

            def down_uppers(e):
                act.wait_ge(expert_down_loaded, 16 * e + 16)
                nc.scalar.copy(down_w[:, 0].rearrange("p m n -> p (m n)"), down_raw[:]).then_inc(down_upper, 1)

            def x_uppers(section, i):
                for hf in range(2):
                    for c in range(DC):
                        banks.wait_filled(act, section, f"xT{c}_{hf}", i)
                        bank = banks.bank(section, f"xT{c}_{hf}")
                        nc.scalar.copy(xeT[:, 0, c, HALF * hf:HALF * (hf + 1)], ps[bank][:, 0:HALF]) \
                            .then_inc(x_upper, 1)

            def hidden(section, i):
                for q in range(2 * FM + 1):
                    if q < 2 * FM:
                        if q >= 2:
                            banks.wait_taken(act, section, f"up{q - 2}", i)
                        take(section, f"gate{q}", i, sil[:, q % 2, :], ACT.Silu, HALF)
                    if q >= 1:
                        hf, m = divmod(q - 1, FM)
                        banks.wait_taken(act, section, f"up{q - 1}", i)
                        nc.scalar.copy(hT[:, 0, m, HALF * hf:HALF * (hf + 1)], prod[:, (q - 1) % 2, :]) \
                            .then_inc(h_upper, 1)

            def take_down(section, e, i):
                act.wait_ge(ye_free, 32 * e + 16)
                for j in range(2, 4):
                    take(section, f"down{j}", i, ye[0:CP, 2 * j:2 * j + 2, :].rearrange("p j d -> p (j d)"),
                         None, 2 * D, CP)

            act.wait_ge(index_ready, 1)
            gate_uppers(0)
            x_uppers(ROUTE, 0)
            with act.Fori(0, E - 1) as e:
                down_uppers(e)
                hidden(EXPERT, e)
                gate_uppers(e + 1)
                x_uppers(EXPERT, e)
                take_down(EXPERT, e, e)
            down_uppers(E - 1)
            hidden(LAST, 0)
            take_down(LAST, E - 1, 0)

        @block.vector
        def _(dve):
            v = nc.vector
            ts, tt, stt = v.tensor_scalar, v.tensor_tensor, v.scalar_tensor_tensor
            then = v.drain

            def bank_of(section, name, i=0):
                banks.wait_filled(dve, section, name, i)
                k = banks.bank(section, name)
                return ps[k], freed[k]

            v.memset(tok[:, :, 0:1], 0)
            v.memset(edge_w[:], 0.0)
            v.memset(eps[:], EPS)
            v.memset(power[:], -0.5)
            dve.wait_ge(tokens_loaded, 32)
            then()
            for dst, shift in ((by0, 0), (by1, 8), (by2, 16), (by3, 24)):
                ts(dst[:], tok[:], shift, 255, ALU.logical_shift_right, ALU.bitwise_and)
            then()
            for s, factor in ((0, HASH_CUR), (1, HASH_PREV)):
                for dst in (by0, by1, by2, by3):
                    ts(dst[:, s, :], dst[:, s, :], float(factor), None, ALU.mult)
            then()
            ts(t_lo[:], by1[:], 255, 8, ALU.bitwise_and, ALU.logical_shift_left)
            ts(t_hi[:], by0[:], 0xFFFF, None, ALU.bitwise_and)
            then()
            tt(t_lo[:], t_lo[:], t_hi[:], ALU.add)
            ts(by1[:], by1[:], 8, None, ALU.logical_shift_right)
            ts(by2[:], by2[:], 0xFFFF, None, ALU.bitwise_and)
            ts(by3[:], by3[:], 255, 8, ALU.bitwise_and, ALU.logical_shift_left)
            then()
            ts(t_hi[:], by0[:], 16, None, ALU.logical_shift_right)
            then()
            ts(by0[:], t_lo[:], 16, None, ALU.logical_shift_right)
            for part in (by1, by2, by3, by0):
                then()
                tt(t_hi[:], t_hi[:], part[:], ALU.add)
            then()
            for limb in (t_hi, t_lo):
                ts(limb[:], limb[:], 0xFFFF, None, ALU.bitwise_and)
            then()
            hi, lo = by0[:, 0, 0:TXT], by1[:, 0, 0:TXT]
            tt(hi, t_hi[:, 0, 1:TXT + 1], t_hi[:, 1, 0:TXT], ALU.bitwise_xor)
            tt(lo, t_lo[:, 0, 1:TXT + 1], t_lo[:, 1, 0:TXT], ALU.bitwise_xor)
            then()
            ts(by2[:, 0, 0:TXT], hi, 3, 16, ALU.bitwise_and, ALU.logical_shift_left)
            ts(by3[:, 0, 0:TXT], hi, 2, None, ALU.logical_shift_right)
            ts(by2[:, 1, 0:TXT], hi, 15, None, ALU.logical_shift_right)
            then()
            tt(by2[:, 0, 0:TXT], by2[:, 0, 0:TXT], lo, ALU.bitwise_or)
            then()
            tt(hashf[:, 0, :], by2[:, 0, 0:TXT], by3[:, 0, 0:TXT], ALU.add)
            then()
            stt(hashf[:, 1, :], by2[:, 1, 0:TXT], -16384.0, hashf[:, 0, :], ALU.mult, ALU.add)
            then()
            ts(hashf[:, 2, :], hashf[:, 1, :], 0.0, float(VOCAB_MOD), ALU.is_lt, ALU.mult)
            then()
            tt(hashf[:, 3, :], hashf[:, 1, :], hashf[:, 2, :], ALU.add)
            then()
            ts(hashf[:, 2, :], hashf[:, 3, :], float(VOCAB_MOD), -float(VOCAB_MOD), ALU.is_ge, ALU.mult)
            then()
            tt(hashf[:, 0, :], hashf[:, 3, :], hashf[:, 2, :], ALU.add)
            then()
            v.memset(hashf[:, 0, 0:1], float(VOCAB_MOD)).then_inc(hash_ready, 1)
            k, f_ = bank_of(SETUP, "txt_index")
            v.tensor_copy(hash_i[:], k[:, 0:B]).then_inc(f_, 1)

            dve.wait_ge(first_loaded, 16 * FIRST_LOADS)
            v.tensor_reduce(absum[:, 0:1], f1_raw[:].rearrange("p m d -> p (m d)"), AX.X, ALU.add,
                            apply_absolute_value=True)
            v.tensor_reduce(absum[:, 1:2], f2_raw[:].rearrange("p m d -> p (m d)"), AX.X, ALU.add,
                            apply_absolute_value=True).then_inc(abs_ready, 1)
            ts(ang[:, 7, :], ang[:, 0, :], 1.0 / (2 * math.pi), ROUND, ALU.mult, ALU.add)
            then()
            ts(ang[:, 7, :], ang[:, 7, :], ROUND, None, ALU.subtract)
            then()
            stt(ang[:, 2, :], ang[:, 7, :], -TWO_PI_HI, ang[:, 0, :], ALU.mult, ALU.add)
            then()
            stt(ang[:, 2, :], ang[:, 7, :], -TWO_PI_LO, ang[:, 2, :], ALU.mult, ALU.add)
            then()
            ts(ang[:, 2, :], ang[:, 2, :], -math.pi, math.pi, ALU.max, ALU.min)
            then()
            ts(ang[:, 3, :], ang[:, 2, :], -1.0, None, ALU.mult)
            then()
            tt(ang[:, 3, :], ang[:, 3, :], ang[:, 2, :], ALU.max)
            then()
            ts(ang[:, 3, :], ang[:, 3, :], -1.0, math.pi / 2, ALU.mult, ALU.add).then_inc(reduced, 1)
            k, f_ = bank_of(SETUP, "gamma")
            ts(above, k[:, 0:2], 1.0 / (D * FF), EPS, ALU.mult, ALU.add).then_inc(f_, 1)
            then()
            ts(below, above, -0.5, None, ALU.mult)
            then()
            ts(above, below, -1.0, None, ALU.mult)
            then()
            for k, (raw, dst) in enumerate(((f1_raw, tern), (f2_raw, tern_b))):
                flat = raw[:].rearrange("p m d -> p (m d)")
                ts(dst[:], flat, above[:, k:k + 1], None, ALU.is_gt)
                ts(flat, flat, below[:, k:k + 1], None, ALU.is_lt)
                then()
                tt(dst[:], dst[:], flat, ALU.subtract).then_inc(ternary_ready, 1)

            for b in range(B):
                k, f_ = bank_of(SETUP, f"txt{b}")
                ts(txt_rows[:, b, :], k[:, 0:D], txt_scale, None, ALU.mult).then_inc(f_, 1)

            ts(scharr_b[:], scharr_b[:], 0.5, None, ALU.mult)
            then()
            shift = const_cols("shift").rearrange("p (y m) -> p y m", y=3)
            for y_ in range(3):
                for k in range(2):
                    for dx in range(3):
                        w = scharr_b[:, k, y_, dx:dx + 1]
                        if y_ == 0:
                            ts(band[:, k, dx, :], shift[:, 0, :], w, None, ALU.mult)
                        else:
                            stt(band[:, k, dx, :], shift[:, y_, :], w, band[:, k, dx, :], ALU.mult, ALU.add)
                then()
            for k in range(2):
                ts(edge_w[:, 0, k, P - 1:P], scharr_h[:, k, 2:3], 0.5, None, ALU.mult)
                ts(edge_w[:, 1, k, 0:1], scharr_h[:, k, 0:1], 0.5, None, ALU.mult)


            def gray_step(c, count):
                if c == 0:
                    dve.wait_ge(img_loaded, count)
                for g_, x_ in ((gray[:, :, 1:IMG + 1], img[:, c]), (halo_gray[:], halo[:, c])):
                    if c == 0:
                        last = ts(g_, x_, GRAY[c], None, ALU.mult)
                    else:
                        last = stt(g_, x_, GRAY[c], g_, ALU.mult, ALU.add)
                if c < 2:
                    then()
                else:
                    last.then_inc(gray_ready, 1)

            dve.wait_ge(cleared, 1)
            for c in range(3):
                gray_step(c, 64)

            dve.wait_ge(angles_ready, 1)
            ts(ang[:, 4:6, :], ang[:, 4:6, :], -HD1 ** -0.5, None, ALU.mult)
            then()
            for g in range(2):
                for s in range(2):
                    h0 = 8 * g + 4 * s
                    q0 = wq1_raw[:, h0:h0 + 4, :, 0]
                    q1 = wq1_raw[:, h0:h0 + 4, :, 1]
                    dst = wq1[:, 4 * g:4 * g + 4, s, :].rearrange("p r (i z) -> p r i z", z=2)
                    sn = ang[:, 4, h0:h0 + 4].unsqueeze(2).to_broadcast([P, 4, HD1 // 2])
                    cs = ang[:, 5, h0:h0 + 4].unsqueeze(2).to_broadcast([P, 4, HD1 // 2])
                    t1 = rot_tmp[:, 0, :].rearrange("p (r i) -> p r i", r=4)
                    t2 = rot_tmp[:, 1, :].rearrange("p (r i) -> p r i", r=4)
                    for z, (m0, m1, op) in enumerate(((cs, sn, ALU.subtract), (sn, cs, ALU.add))):
                        tt(t1, q0, m0, ALU.mult)
                        tt(t2, q1, m1, ALU.mult)
                        then()
                        tt(dst[:, :, :, z], t1, t2, op)
                        then()
            ts(ang[:, 6, :], ang[:, 6, :], -1.0, None, ALU.mult)
            then()
            for hh in range(H1):
                stt(alibi[:, hh, :], const_cols("rel"), ang[:, 6, hh:hh + 1], const_cols("mask"), ALU.mult, ALU.add)

            then()
            v.nop().then_inc(setup_dve, 1)

            def moments(src, t):
                v.bn_stats(stats[:, t, :], src[:, t, :])
                then()
                v.bn_aggr(mean_var[:, t, :], stats[:, t, :]).then_inc(var_ready, 1)

            def normalise(dst, src, i, k, t):
                dve.wait_ge(rstd_ready, ln_count(i, k, t))
                return ts(dst[:, t, :], src[:, t, :], mean_var[:, t, 0:1], rstd[:, t:t + 1],
                          ALU.subtract, ALU.mult)

            def ln_out(name, i, g=None, b=None):
                k, f_ = bank_of(BODY, f"{name}1", i)
                if g is None:
                    v.tensor_copy(xT[:, 1, :], k[:, 0:S]).then_inc(f_, 1)
                else:
                    ts(xT[:, 1, :], k[:, 0:S], cols[:, g:g + 1], cols[:, b:b + 1], ALU.mult, ALU.add) \
                        .then_inc(f_, 1)

            def add_norm(dst, name, other, i, k, normed):
                for t in range(NT + 1):
                    if t < NT:
                        bank, f_ = bank_of(BODY, f"{name}_{t}", i)
                        tt(dst[:, t, :], bank[:, 0:D], other[:, t, :], ALU.add).then_inc(f_, 1)
                        then()
                        moments(dst, t)
                    if t >= 1:
                        normalise(normed, dst, i, k, t - 1).then_inc(norm_ready, 1)

            def embed_step(step, section, i, first, second):
                if step == 0:
                    for hf in range(2):
                        banks.wait_taken(dve, section, f"conv{hf}", i)
                        tt(h_in[:, hf, :], edge[:, hf, 0:IMG], edge[:, hf, IMG:2 * IMG], ALU.add)
                    then()
                for t in range(NT):
                    if step == 0:
                        moments(h_in, t)
                    elif step == 1:
                        normalise(x1, h_in, i, first, t)
                        then()
                        moments(x1, t)
                    else:
                        normalise(xh, x1, i, second, t).then_inc(norm_ready, 1)

            def mask_max(layer, n, i):
                s = n % 2
                if n >= 2:
                    dve.wait_ge(exp_done, 2 * HEADS * i + (HEADS * layer + n - 1))
                bias = const_cols("mask") if layer == 0 else alibi[:, pair_head(n), :]
                _, f_a = bank_of(BODY, f"scores{layer}_{n}", i)
                _, f_b = bank_of(BODY, f"scores_b{layer}_{n}", i)
                v.memset(carrier[:, n % 4:n % 4 + 1], 0.0)
                for t in (0, 2, 1):
                    last = v.tensor_tensor_reduce(
                        out=masked[:, s, seg(t)], in0=scores_place(layer, n, t), in1=bias[:, P * (2 - t):S],
                        scale=1.0, scalar=BIG, op0=ALU.add, op1=ALU.min, accum_out=nmax[:, s, t:t + 1])
                    if t != 0:
                        last.then_inc(f_a if t == 2 else f_b, 1)

            def denominators(layer, c, i):
                per = 8 if layer == 0 else 2
                sums = rowsum[:, per * c:per * (c + 1), :]
                dve.wait_ge(exp_done, 2 * HEADS * i + (HEADS * layer + per * (c + 1)))
                if layer == 1:
                    ts(sums, sums, 1.0, None, ALU.add)
                    then()
                if c >= 2:
                    banks.wait_filled(dve, BODY, f"rinvT{layer}_{c - 2}", i)
                v.reciprocal(sums, sums)
                then()
                v.tensor_copy(rinv[:, c % 2].rearrange("p t (h d) -> p t h d", h=per),
                              sums.rearrange("p h t -> p t h").unsqueeze(3).to_broadcast([P, NT, per, P // per])) \
                    .then_inc(rinv_ready, 1)

            def weigh(layer, c, i):
                banks.wait_taken(dve, BODY, f"rinvT{layer}_{c}", i)
                k, f_ = bank_of(BODY, f"out{layer}_{c}", i)
                tt((o0T, o1T)[layer][:, c, :], k[:, 0:S], rinvT[:, c % 2, :], ALU.mult).then_inc(f_, 1)

            def attention(layer, i):
                per = 8 if layer == 0 else 2
                EMBED_AT = {2: 0, 4: 1, 6: 2}
                mask_max(layer, 0, i)
                mask_max(layer, 1, i)
                for n in range(HEADS):
                    if n >= per + 2 and (n - 2) % per == 0:
                        weigh(layer, (n - 2) // per - 1, i)
                    if n + 2 < HEADS:
                        mask_max(layer, n + 2, i)
                    if n % per == per - 1:
                        denominators(layer, n // per, i)
                    if dve_takes_both(layer, n):
                        k, f_ = bank_of(BODY, f"probsT{layer}_{n}", i)
                        v.tensor_copy(probsT[:, n % 2, 0:3 * P], k[:, 0:3 * P]).then_inc(f_, 1)
                    k, f_ = bank_of(BODY, f"probsT_b{layer}_{n}", i)
                    v.tensor_copy(probsT[:, n % 2, 3 * P:6 * P], k[:, 0:3 * P]).then_inc(f_, 1)
                    if layer == 1 and n in EMBED_AT:
                        if n == 2:
                            dve.wait_ge(txt_row_loaded, 16 * i + 32)
                        embed_step(EMBED_AT[n], BODY, i, LN_FIRST, LN_ATTN0)
                if layer == 1:
                    weigh(layer, HEADS // per - 2, i)
                weigh(layer, HEADS // per - 1, i)

            def cosines(t, i):
                bank, f_ = bank_of(BODY, f"qk0_{t}", i)
                tt(qk[:, t, :], bank[:], bqkv[:, 0:2 * D], ALU.add).then_inc(f_, 1)
                then()
                cos = const_cols("cos").rearrange("p (t x d) -> p t x d", t=NT, x=2)[:, t]
                heads = lambda z: z.rearrange("p (x h d) -> p x h d", x=2, h=H0)
                for x in range(2):
                    tt(heads(rot1[:, t])[:, x], heads(qk[:, t])[:, x],
                       cos[:, x, :].unsqueeze(1).to_broadcast([P, H0, HD0]), ALU.mult)

            def rotated(t, i):
                then()
                dve.wait_ge(rot2_ready, NT * i + (t + 1))
                tt(rot1[:, t, :], rot1[:, t, :], rot2[:, t, :], ALU.add).then_inc(roped, 1)

            def lower_halves(t, i):
                dve.wait_ge(stack_hi, NT * i + (t + 1))
                for x, (dst, slots) in enumerate(((stack_q, (1, 3)), (stack_k, (2, 3)))):
                    o = dst[:, t % 2, :].rearrange("p (h s d) -> p h s d", h=H0, s=4)
                    for s in slots:
                        last = tt(o[:, :, s, :], rot1[:, t, D * x:D * (x + 1)].rearrange("p (h d) -> p h d", h=H0),
                                  o[:, :, 0, :].bitcast(F32), ALU.subtract)
                last.then_inc(stack_ready, 1)

            def take_stacks(t, i):
                for g in (1, 3):
                    k, f_ = bank_of(BODY, f"stack{t}_{g}", i)
                    v.tensor_copy((q0T, k0T)[g // 2][:, 4 * (g % 2):4 * (g % 2) + 4, P * t:P * (t + 1)],
                                  k[:].rearrange("p (q n) -> p q n", q=4)).then_inc(f_, 1)

            def values(t, i):
                k, f_ = bank_of(BODY, f"v0_{t}", i)
                pv = k[:, 0:D].rearrange("p (a s d) -> p a s d", s=2, d=HD0)
                bv = bqkv[:, 2 * D:3 * D].rearrange("p (a s d) -> p a s d", s=2, d=HD0)
                for s in range(2):
                    last = tt(vpad[:, t, :, 48 * s:48 * s + HD0], pv[:, :, s, :], bv[:, :, s, :], ALU.add)
                last.then_inc(f_, 1)

            dve.wait_ge(txt_row_loaded, 16)
            for stage in range(3):
                embed_step(stage, SETUP, 0, -2, -1)
            dve.wait_ge(loaded, 16 * LOADS)
            with dve.Fori(0, B) as i:
                dve.wait_ge(h_stored, 32 * i + 16)
                ln_out("ln_attn0_T", i, 1, 3)

                for t, step in ((0, cosines), (1, cosines), (0, rotated), (2, cosines), (1, rotated),
                                (0, lower_halves), (2, rotated), (1, lower_halves), (0, take_stacks),
                                (2, lower_halves), (0, values), (1, take_stacks), (1, values), (2, take_stacks),
                                (2, values)):
                    step(t, i)

                attention(0, i)
                dve.wait_ge(resid_ready, 3 * i + 1)
                add_norm(y, "proj0", y, i, LN_MLP, xh)
                ln_out("ln_mlp_T", i, 5, 7)
                for c in range(3):
                    gray_step(c, 64 * i + 128)
                dve.wait_ge(resid_ready, 3 * i + 2)
                add_norm(h, "down0", x1, i, LN_FFN, xh)
                for c in range(DC):
                    dve.wait_ge(x_part_upper, DC * i + (c + 1))
                    bank = banks.bank(BODY, f"ln_ffn_T{c}")
                    tt(x_parts[:, 1, c, :], ps[bank][:, 0:S], x_parts[:, 0, c, :].bitcast(F32), ALU.subtract) \
                        .then_inc(freed[bank], 1)
                for m in range(FM):
                    banks.wait_taken(dve, BODY, f"up1_{m}", i)
                    if m % 2 == 1:
                        v.tensor_copy(hid_parts[:, 0, m, :], relu[:, m, :])
                        then()
                    tt(hid_parts[:, 1, m, :], relu[:, m, :], hid_parts[:, 0, m, :].bitcast(F32), ALU.subtract) \
                        .then_inc(hid_split, 1)
                dve.wait_ge(resid_ready, 3 * i + 3)
                add_norm(h, "down1", x1, i, LN_ATTN1, xh)
                ln_out("ln_attn1_T", i)
                for t in range(NT):
                    k, f_ = bank_of(BODY, f"v1_{t}", i)
                    v.tensor_copy(v1[:, t, :], k[:, 0:KV1 * HD1]).then_inc(f_, 1)
                for m in range(1, 8, 2):
                    k, f_ = bank_of(BODY, f"q1_{m}", i)
                    v.tensor_copy(q1T[:, m, :], k[:, 0:S]).then_inc(f_, 1)
                attention(1, i)
                add_norm(h, "proj1", h, i, LN_MOE, x_moe)
                ln_out("ln_moe_T", i)
                k, f_ = bank_of(BODY, "logits", i)
                v.tensor_copy(logits_all[:].rearrange("p (b t) e -> p b (t e)", b=B)[:, i], k[:, 0:NT * E]) \
                    .then_inc(f_, 1)
            v.nop().then_inc(logits_ready, B)

            then()
            dve.wait_ge(h_stored, 32 * B + 16)
            by_token = lambda z: z[:].rearrange("p e n -> p n e")
            bc = lambda z: z.unsqueeze(1).to_broadcast([P, E, TILES])
            v.tensor_reduce(kv[:, 0, :], logits_all[:], AX.X, ALU.max)
            then()
            tt(pr[:], logits_all[:].rearrange("p n e -> p e n"), bc(kv[:, 0, :]), ALU.subtract) \
                .then_inc(lse_shift, 1)
            dve.wait_ge(lse_exp, 1)
            v.tensor_reduce(kv[:, 0, :], by_token(pr), AX.X, ALU.add)
            then()
            v.reciprocal(kv[:, 1, :], kv[:, 0, :])
            then()
            tt(pr[:], pr[:], bc(kv[:, 1, :]), ALU.mult)
            then()
            tb = const_cols("tiebreak").rearrange("p (e n) -> p e n", e=E)
            for k, (oh, src) in enumerate(((oh1, pr), (oh2, r_b))):
                v.tensor_reduce(kv[:, 2 + k, :], by_token(src), AX.X, ALU.max)
                then()
                tt(r_a[:], src[:], bc(kv[:, 2 + k, :]), ALU.is_equal)
                then()
                tt(r_a[:], r_a[:], tb, ALU.mult)
                then()
                v.tensor_reduce(kv[:, 4, :], by_token(r_a), AX.X, ALU.max)
                then()
                tt(oh[:], tb, bc(kv[:, 4, :]), ALU.is_equal)
                then()
                if k == 0:
                    stt(r_b[:].rearrange("p e n -> p (e n)"), oh1[:].rearrange("p e n -> p (e n)"), -2.0,
                        pr[:].rearrange("p e n -> p (e n)"), ALU.mult, ALU.add)
                    then()
            tt(kv[:, 4, :], kv[:, 2, :], kv[:, 3, :], ALU.add)
            then()
            ts(kv[:, 4, :], kv[:, 4, :], 1e-9, None, ALU.add)
            then()
            v.reciprocal(kv[:, 5, :], kv[:, 4, :])
            then()
            for k in range(2):
                tt(wk[:, k, :], kv[:, 2 + k, :], kv[:, 5, :], ALU.mult)
            then()
            tt(r_a[:], oh1[:], bc(wk[:, 0, :]), ALU.mult)
            tt(r_b[:], oh2[:], bc(wk[:, 1, :]), ALU.mult)
            then()
            tt(gts[:], r_a[:], r_b[:], ALU.add)
            v.memset(thr[:], 0)
            for k in range(STEPS):
                v.memset(bits[:, k:k + 1], (k + 1) << (GATE_BITS - 2))
            then()
            by_expert = lambda z: z.unsqueeze(2).to_broadcast([P, STEPS, E])
            with dve.Fori(0, SEARCH // 3) as r:
                for u in range(3):
                    tt(cand[:], thr[:].unsqueeze(1).to_broadcast([P, STEPS, E]), by_expert(bits[:]), ALU.bitwise_or)
                    then()
                    tt(reach[:], gts[:].unsqueeze(1).to_broadcast([P, STEPS, E, TILES]),
                       cand[:].bitcast(F32).unsqueeze(3).to_broadcast([P, STEPS, E, TILES]), ALU.is_ge)
                    then()
                    v.tensor_reduce(cnt[:].rearrange("p (k e) -> p k e", e=E), reach[:], AX.X, ALU.add) \
                        .then_inc(counts_ready, 1)
                    dve.wait_ge(counts_taken, r * 3 + (u + 1))
                    stt(won[:], ps[7][:, 0:STEPS * E].rearrange("p (k e) -> p k e", e=E), float(CAP), by_expert(bits[:]),
                        ALU.is_ge, ALU.mult)
                    then()
                    v.tensor_reduce(best[:], won[:].rearrange("p k e -> p e k"), AX.X, ALU.max)
                    ts(bits[:], bits[:], 2, None, ALU.logical_shift_right)
                    then()
                    tt(thr[:], thr[:], best[:], ALU.bitwise_or)
                    then()
            t_f = thr[:].bitcast(F32).unsqueeze(2).to_broadcast([P, E, TILES])
            flat = lambda z: z[:].rearrange("p e n -> p (e n)")
            tt(selm[:], gts[:], t_f, ALU.is_gt)
            tt(eqm[:], gts[:], t_f, ALU.is_equal)
            ts(r_a[:], gts[:], 0.0, None, ALU.is_gt)
            then()
            tt(eqm[:], eqm[:], r_a[:], ALU.mult)
            then()
            v.tensor_copy(sel_eq[:, 0, :], flat(eqm))
            v.tensor_copy(sel_eq[:, 1, :], flat(selm)).then_inc(sel_ready, 1)

            def ranks(name):
                w = E * TILES
                k, f_ = bank_of(ROUTE, name)
                v.tensor_copy(flat(r_tot), k[:, 0:w])
                then()
                v.tensor_tensor_scan(flat(r_a), const_cols("scan_keep"), flat(r_tot), 0.0, ALU.mult, ALU.add)
                then()
                tt(flat(r_b), flat(r_a), flat(r_tot), ALU.subtract)
                then()
                tt(flat(r_c), k[:, w:2 * w], flat(r_b), ALU.add).then_inc(f_, 1)
                then()

            ranks("prefix")
            v.tensor_reduce(cnt[:, 0:E], ps[6][:, 0:E * TILES].rearrange("p (e n) -> p e n", e=E), AX.X, ALU.add)
            then()
            ts(want[:], cnt[:, 0:E], -1.0, float(CAP), ALU.mult, ALU.add)
            then()
            tt(r_c[:], r_c[:], want[:].unsqueeze(2).to_broadcast([P, E, TILES]), ALU.is_lt)
            then()
            tt(r_c[:], r_c[:], eqm[:], ALU.mult)
            then()
            tt(selm[:], selm[:], r_c[:], ALU.add)
            then()
            v.tensor_copy(sel_eq[:, 0, :], flat(selm)).then_inc(sel_ready, 1)
            ranks("slots")
            tt(flat(r_c), flat(r_c), const_cols("expert_row"), ALU.add)
            then()
            for k, oh in enumerate((oh1, oh2)):
                tt(r_a[:], oh[:], r_c[:], ALU.mult)
                tt(r_b[:], oh[:], selm[:], ALU.mult)
                then()
                v.tensor_reduce(pos_f[:, 2 * k, :], by_token(r_a), AX.X, ALU.add)
                v.tensor_reduce(pos_f[:, 2 * k + 1, :], by_token(r_b), AX.X, ALU.add)
                then()
                tt(gath_i[:, k, :], pos_f[:, 2 * k, :], pos_f[:, 2 * k + 1, :], ALU.mult)
                tt(wk[:, k, :], wk[:, k, :], pos_f[:, 2 * k + 1, :], ALU.mult)
                ts(kv[:, 6, :], pos_f[:, 2 * k + 1, :], -1e6, 1e6, ALU.mult, ALU.add)
                then()
                tt(scat_i[:, k, :], pos_f[:, 2 * k, :], kv[:, 6, :], ALU.add)
                then()
            v.nop().then_inc(index_ready, 1)

            def gate_lowers(e):
                dve.wait_ge(gate_upper, e + 1)
                for w, raw in ((gate_w, gate_raw), (up_w, up_raw)):
                    last = tt(w[:, 1].rearrange("p c n -> p (c n)"), raw[:],
                              w[:, 0].rearrange("p c n -> p (c n)").bitcast(F32), ALU.subtract)
                last.then_inc(gate_split, 1)

            def down_lowers(e):
                dve.wait_ge(down_upper, e + 1)
                tt(down_w[:, 1].rearrange("p m n -> p (m n)"), down_raw[:],
                   down_w[:, 0].rearrange("p m n -> p (m n)").bitcast(F32), ALU.subtract).then_inc(down_split, 1)

            def x_lowers(section, e, i):
                for hf in range(2):
                    for c in range(DC):
                        dve.wait_ge(x_upper, 2 * DC * e + (DC * hf + c + 1))
                        bank = banks.bank(section, f"xT{c}_{hf}")
                        half = slice(HALF * hf, HALF * (hf + 1))
                        tt(xeT[:, 1, c, half], ps[bank][:, 0:HALF], xeT[:, 0, c, half].bitcast(F32), ALU.subtract) \
                            .then_inc(freed[bank], 1)
                then()
                v.nop().then_inc(x_split, 2 * DC)

            def hidden(section, e, i):
                for q in range(2 * FM + 1):
                    if q < 2 * FM:
                        banks.wait_taken(dve, section, f"gate{q}", i)
                        k, f_ = bank_of(section, f"up{q}", i)
                        tt(prod[:, q % 2, :], k[:, 0:HALF], sil[:, q % 2, :], ALU.mult).then_inc(f_, 1)
                    if q >= 1:
                        hf, m = divmod(q - 1, FM)
                        dve.wait_ge(h_upper, 2 * FM * e + q)
                        half = slice(HALF * hf, HALF * (hf + 1))
                        tt(hT[:, 1, m, half], prod[:, (q - 1) % 2, :], hT[:, 0, m, half].bitcast(F32),
                           ALU.subtract).then_inc(h_split, 1)
                        then()

            def take_down(section, e, i):
                dve.wait_ge(ye_free, 32 * e + 16)
                for j in range(0, 2):
                    k, f_ = bank_of(section, f"down{j}", i)
                    v.tensor_copy(ye[0:CP, 2 * j:2 * j + 2, :].rearrange("p j d -> p (j d)"), k[0:CP, :]) \
                        .then_inc(f_, 1)

            gate_lowers(0)
            x_lowers(ROUTE, 0, 0)
            with dve.Fori(0, E - 1) as e:
                down_lowers(e)
                hidden(EXPERT, e, e)
                gate_lowers(e + 1)
                x_lowers(EXPERT, e + 1, e)
                take_down(EXPERT, e, e)
            down_lowers(E - 1)
            hidden(LAST, E - 1, 0)
            take_down(LAST, E - 1, 0)

            dve.wait_ge(h_reloaded, 16)
            for k in range(4):
                dve.wait_ge(gathered[k], 16 * 2 * TILES // 4)
                for n in range(TILES // 4 * k, TILES // 4 * (k + 1)):
                    stt(xall[:, n, :], y1[:, n, :], wk[:, 0, n:n + 1], xall[:, n, :], ALU.mult, ALU.add)
                then()
                for n in range(TILES // 4 * k, TILES // 4 * (k + 1)):
                    last = stt(xall[:, n, :], y2[:, n, :], wk[:, 1, n:n + 1], xall[:, n, :], ALU.mult, ALU.add)
                last.then_inc(out_ready, 1)

        @block.gpsimd
        def _(pool):
            g = nc.gpsimd
            then = g.drain
            for bank in range(8):
                g.nop().then_inc(freed[bank], 1)
            g.memset(halo[:], 0.0)
            g.memset(gray[:], 0.0)
            g.memset(vpad[:], 0.0)
            g.memset(zeros[:], 0.0).then_inc(cleared, 1)
            g.nop().then_inc(ye_free, 16)

            banks.wait_taken(pool, SETUP, "txt_index")
            for b in range(B):
                g.indirect_dma_start(emb[:, b, :], None, a["L0_txt_embed_weight"],
                                     bass.IndirectOffsetOnAxis(ap=hash_i[:, b:b + 1], axis=0)) \
                    .then_inc(emb_loaded, 16)
            pool.wait_ge(setup_dve, 1)
            pool.wait_ge(h_stored, 16)

            def inverse_deviation(i, k):
                for t in range(NT):
                    pool.wait_ge(var_ready, ln_count(i, k, t))
                    g.tensor_tensor(rstd[:, t:t + 1], mean_var[:, t, 1:2], eps[:, 0:1], ALU.add)
                    then()
                    g.tensor_tensor(rstd[:, t:t + 1], rstd[:, t:t + 1], power[:, 0:1], ALU.pow) \
                        .then_inc(rstd_ready, 1)

            def row(z):
                return z.unsqueeze(1).to_broadcast([P, NT, D])

            inverse_deviation(0, -2)
            inverse_deviation(0, -1)
            pool.wait_ge(loaded, 16 * LOADS)
            with pool.Fori(0, B) as i:
                pool.wait_ge(norm_ready, i * (5 * NT) + NT)
                g.tensor_tensor(y[:], x1[:], row(bo_r), ALU.add).then_inc(resid_ready, 1)
                for t in range(NT):
                    banks.wait_taken(pool, BODY, f"qk0_{t}", i)
                    sin = const_cols("sin").rearrange("p (t x d) -> p t x d", t=NT, x=2)[:, t]
                    heads = lambda z: z.rearrange("p (x h d) -> p x h d", x=2, h=H0)
                    for x in range(2):
                        for lo_ in (0, 8):
                            last = g.tensor_tensor(
                                heads(rot2[:, t])[:, x, :, lo_:lo_ + 8], heads(qk[:, t])[:, x, :, 8 - lo_:16 - lo_],
                                sin[:, x, lo_:lo_ + 8].unsqueeze(1).to_broadcast([P, H0, 8]), ALU.mult)
                    last.then_inc(rot2_ready, 1)
                inverse_deviation(i, LN_MLP)
                g.tensor_tensor(x1[:], h_in[:], y[:], ALU.add)
                then()
                g.tensor_tensor(x1[:], x1[:], row(b2_r), ALU.add).then_inc(resid_ready, 1)
                inverse_deviation(i, LN_FFN)
                g.tensor_tensor(x1[:], h[:], row(bf2_r), ALU.add).then_inc(resid_ready, 1)
                for k in (LN_ATTN1, LN_FIRST, LN_ATTN0, LN_MOE):
                    inverse_deviation(i, k)

            pool.wait_ge(index_ready, 1)
            pool.wait_ge(expert_in_cleared, 16)
            pool.wait_ge(xall_loaded, 16)
            for k in range(2):
                for n in range(TILES):
                    g.indirect_dma_start(xg_dram, bass.IndirectOffsetOnAxis(ap=scat_i[:, k, n:n + 1], axis=0),
                                         xall[:, n, :], None, bounds_check=E * CAP - 1, oob_is_err=False) \
                        .then_inc(scattered, 16)
            pool.wait_ge(ye_free, 32 * E + 16)
            for n in range(TILES):
                for k, dst in enumerate((y1, y2)):
                    g.indirect_dma_start(dst[:, n, :], None, yg_dram,
                                         bass.IndirectOffsetOnAxis(ap=gath_i[:, k, n:n + 1], axis=0)) \
                        .then_inc(gathered[n // (TILES // 4)], 16)


_INS = ["x", "x_txt", "L0_tok_scharr", "L0_txt_embed_weight", "L0_txt_proj_weight", "L0_txt_scale",
        "L0_attn_ln1_g", "L0_attn_ln1_b", "L0_attn_Wqkv", "L0_attn_bqkv", "L0_attn_Wo", "L0_attn_bo",
        "L0_attn_ln2_g", "L0_attn_ln2_b", "L0_attn_W1", "L0_attn_b1", "L0_attn_W2", "L0_attn_b2",
        "L0_ffn_W1", "L0_ffn_b1", "L0_ffn_W2", "L0_ffn_b2", "L1_attn_Wq", "L1_attn_Wk", "L1_attn_Wv",
        "L1_attn_Wo", "L1_attn_q_phase_angle", "L1_attn_alibi_log_slopes", "L1_ffn_router_gate",
        "L1_ffn_gate_w", "L1_ffn_up_w", "L1_ffn_down_w"]


def kernel(**inputs):
    import concourse.bacc as bacc
    from concourse.bass_utils import run_bass_kernel_spmd

    nc = bacc.Bacc("TRN2", target_bir_lowering=False, num_devices=1)
    arrays, aps = {}, {}
    for name in _INS:
        x = np.ascontiguousarray(inputs[name])
        if x.ndim == 0:
            x = x.reshape(1)
        arrays[f"in_{name}"] = x
        aps[name] = nc.dram_tensor(f"in_{name}", x.shape, mybir.dt.from_np(x.dtype), kind="ExternalInput").ap()
    arrays["in_const"] = shape_constants()
    const = nc.dram_tensor("in_const", (P, NC_COLS), F32, kind="ExternalInput").ap()
    out = nc.dram_tensor("out_0", (B, S, D), F32, kind="ExternalOutput").ap()
    early_fusion_kernel(nc, aps, const, out)
    r = run_bass_kernel_spmd(nc, [arrays], core_ids=[0])
    return r.results[0]["out_0"]
```
